# Optimizing a Trainium2 kernel written in Bass

```python
import numpy as np
import jax
import jax.numpy as jnp

def _softmax(x, axis=-1):
    return jax.nn.softmax(x, axis=axis)

def _gelu(x):
    return jax.nn.gelu(x, approximate=True)

def _silu(x):
    return jax.nn.silu(x)

def _sigmoid(x):
    return jax.nn.sigmoid(x)

def _layernorm(x, axis=-1, eps=1e-05):
    m = jnp.mean(x, axis=axis, keepdims=True)
    v = jnp.var(x, axis=axis, keepdims=True)
    return (x - m) / jnp.sqrt(v + eps)

def _scatter_add(tgt, idx, src, axis=0):
    return tgt.at[idx].add(src)

def _segment_sum(src, seg, n):
    return jax.ops.segment_sum(src, seg, n)
kernel_name = 'mk_vit_tower_d1_tok_img512_r4_a7b2cb'

def setup_inputs(seed: int=0):
    np.random.seed(seed)
    _w = jnp.asarray

    def _rec_inputs():
        import jax
        import jax.numpy as jnp
        _rk = jax.random.key(seed)
        x = -0.000190493 + 0.999948 * jax.random.normal(jax.random.fold_in(_rk, 1), (64, 2, 104, 104), jnp.float32)
        return x
    x = _rec_inputs()

    def _L0_tok_setup():
        import jax, jax.numpy as jnp
        import numpy as np
        HP = 4
        PATCH = 8
        EPS = 1e-07

        def _shifts(x):
            h, w = (x.shape[2], x.shape[3])
            pad2 = ((0, 0), (0, 0))
            left_up = jnp.pad(x[:, :, HP:, :w - HP], pad2 + ((0, HP), (HP, 0)))
            right_up = jnp.pad(x[:, :, HP:, HP:], pad2 + ((0, HP), (0, HP)))
            left_down = jnp.pad(x[:, :, :h - HP, :w - HP], pad2 + ((HP, 0), (HP, 0)))
            right_down = jnp.pad(x[:, :, :h - HP, HP:], pad2 + ((HP, 0), (0, HP)))
            return (left_up, right_up, left_down, right_down)
        key = jax.random.key(seed)
        k1, k2, k3, k4 = jax.random.split(key, 4)
        B, C, S = (128, 2, 104)
        embed_dim = 128
        x = jax.random.normal(k1, (B, C, S, S), dtype=jnp.float32)
        gamma = 1.0 + 0.05 * jax.random.normal(k2, (10, S, S), dtype=jnp.float32)
        beta = 0.05 * jax.random.normal(k3, (10, S, S), dtype=jnp.float32)
        W = 0.02 * jax.random.normal(k4, (embed_dim, 10, PATCH, PATCH), dtype=jnp.float32)
        b = jnp.zeros((embed_dim,), dtype=jnp.float32)
        return {'x': x, 'gamma': gamma, 'beta': beta, 'W': W, 'b': b}
    _L0_tok_all = _L0_tok_setup()
    _L0_tok_in = {k: v for k, v in _L0_tok_all.items() if k in ('gamma', 'beta', 'W', 'b')}
    del _L0_tok_all

    def _L0_attn_setup():
        import jax, jax.numpy as jnp
        import numpy as np
        B, S, D = (2, 512, 128)
        H = 8
        G = 4
        LAMBDA_INIT = 0.2
        EPS = 1e-05
        key = jax.random.key(seed)
        ks = jax.random.split(key, 16)
        n = jax.random.normal
        return {'x': n(ks[0], (B, S, D), jnp.float32), 'K1_w': n(ks[1], (D, D), jnp.float32) * 0.02, 'K1_b': n(ks[2], (D,), jnp.float32) * 0.02, 'Q1_w': n(ks[3], (D, D), jnp.float32) * 0.02, 'K2_w': n(ks[4], (D, D), jnp.float32) * 0.02, 'K2_b': n(ks[5], (D,), jnp.float32) * 0.02, 'Q2_w': n(ks[6], (D, D), jnp.float32) * 0.02, 'V_w': n(ks[7], (D, D), jnp.float32) * 0.02, 'lambda_q1': n(ks[8], (H, 1), jnp.float32), 'lambda_k1': n(ks[9], (H, 1), jnp.float32), 'lambda_q2': n(ks[10], (H, 1), jnp.float32), 'lambda_k2': n(ks[11], (H, 1), jnp.float32), 'gn_w': jnp.ones((D,), jnp.float32), 'gn_b': jnp.zeros((D,), jnp.float32), 'out_w': n(ks[12], (D, D), jnp.float32) * 0.02, 'out_b': n(ks[13], (D,), jnp.float32) * 0.02}
    _L0_attn_all = _L0_attn_setup()
    _L0_attn_in = {k: v for k, v in _L0_attn_all.items() if k in ('K1_w', 'K1_b', 'Q1_w', 'K2_w', 'K2_b', 'Q2_w', 'V_w', 'lambda_q1', 'lambda_k1', 'lambda_q2', 'lambda_k2', 'gn_w', 'gn_b', 'out_w', 'out_b')}
    del _L0_attn_all

    def _L0_ffn_setup():
        import jax, jax.numpy as jnp
        import numpy as np
        K = 2
        key = jax.random.key(seed)
        k1, k2, k3, k4 = jax.random.split(key, 4)
        B, L, D, H, E = (8, 256, 128, 256, 16)
        x = jax.random.normal(k1, (B, L, D), dtype=jnp.float32)
        W_gate = jax.random.normal(k2, (D, E), dtype=jnp.float32) * 0.02
        W1 = jax.random.normal(k3, (E, D, H), dtype=jnp.float32) * 0.02
        W2 = jax.random.normal(k4, (E, H, D), dtype=jnp.float32) * 0.02
        return {'x': x, 'W_gate': W_gate, 'W1': W1, 'W2': W2}
    _L0_ffn_all = _L0_ffn_setup()
    _L0_ffn_in = {k: v for k, v in _L0_ffn_all.items() if k in ('W_gate', 'W1', 'W2')}
    del _L0_ffn_all
    return {'x': x, 'L0_tok_gamma': _L0_tok_in['gamma'], 'L0_tok_beta': _L0_tok_in['beta'], 'L0_tok_W': _L0_tok_in['W'], 'L0_tok_b': _L0_tok_in['b'], 'L0_attn_K1_w': _L0_attn_in['K1_w'], 'L0_attn_K1_b': _L0_attn_in['K1_b'], 'L0_attn_Q1_w': _L0_attn_in['Q1_w'], 'L0_attn_K2_w': _L0_attn_in['K2_w'], 'L0_attn_K2_b': _L0_attn_in['K2_b'], 'L0_attn_Q2_w': _L0_attn_in['Q2_w'], 'L0_attn_V_w': _L0_attn_in['V_w'], 'L0_attn_lambda_q1': _L0_attn_in['lambda_q1'], 'L0_attn_lambda_k1': _L0_attn_in['lambda_k1'], 'L0_attn_lambda_q2': _L0_attn_in['lambda_q2'], 'L0_attn_lambda_k2': _L0_attn_in['lambda_k2'], 'L0_attn_gn_w': _L0_attn_in['gn_w'], 'L0_attn_gn_b': _L0_attn_in['gn_b'], 'L0_attn_out_w': _L0_attn_in['out_w'], 'L0_attn_out_b': _L0_attn_in['out_b'], 'L0_ffn_W_gate': _L0_ffn_in['W_gate'], 'L0_ffn_W1': _L0_ffn_in['W1'], 'L0_ffn_W2': _L0_ffn_in['W2']}

def reference(x, L0_tok_gamma, L0_tok_beta, L0_tok_W, L0_tok_b, L0_attn_K1_w, L0_attn_K1_b, L0_attn_Q1_w, L0_attn_K2_w, L0_attn_K2_b, L0_attn_Q2_w, L0_attn_V_w, L0_attn_lambda_q1, L0_attn_lambda_k1, L0_attn_lambda_q2, L0_attn_lambda_k2, L0_attn_gn_w, L0_attn_gn_b, L0_attn_out_w, L0_attn_out_b, L0_ffn_W_gate, L0_ffn_W1, L0_ffn_W2):
    import jax
    import jax.numpy as jnp

    def _L0_tok_ref(x, gamma, beta, W, b):
        import jax, jax.numpy as jnp
        import numpy as np
        HP = 4
        PATCH = 8
        EPS = 1e-07

        def _shifts(x):
            h, w = (x.shape[2], x.shape[3])
            pad2 = ((0, 0), (0, 0))
            left_up = jnp.pad(x[:, :, HP:, :w - HP], pad2 + ((0, HP), (HP, 0)))
            right_up = jnp.pad(x[:, :, HP:, HP:], pad2 + ((0, HP), (0, HP)))
            left_down = jnp.pad(x[:, :, :h - HP, :w - HP], pad2 + ((HP, 0), (HP, 0)))
            right_down = jnp.pad(x[:, :, :h - HP, HP:], pad2 + ((HP, 0), (0, HP)))
            return (left_up, right_up, left_down, right_down)
        lu, ru, ld, rd = _shifts(x)
        concat = jnp.concatenate((x, lu, ru, ld, rd), axis=1)
        mean = jnp.mean(concat, axis=(1, 2, 3), keepdims=True)
        var = jnp.var(concat, axis=(1, 2, 3), keepdims=True)
        normed = (concat - mean) * jax.lax.rsqrt(var + EPS)
        normed = normed * gamma[None] + beta[None]
        y = jax.lax.conv_general_dilated(normed, W, window_strides=(PATCH, PATCH), padding='VALID', dimension_numbers=('NCHW', 'OIHW', 'NCHW'))
        y = y + b[None, :, None, None]
        B, E = (y.shape[0], y.shape[1])
        y = y.reshape(B, E, -1).transpose(0, 2, 1)
        return y

    def _L0_attn_ref(x, K1_w, K1_b, Q1_w, K2_w, K2_b, Q2_w, V_w, lambda_q1, lambda_k1, lambda_q2, lambda_k2, gn_w, gn_b, out_w, out_b):
        import jax, jax.numpy as jnp
        import numpy as np
        B, S, D = (2, 512, 128)
        H = 8
        G = 4
        LAMBDA_INIT = 0.2
        EPS = 1e-05
        b, s, d = x.shape
        hd = d // H

        def heads(t):
            return t.reshape(b, s, H, hd).transpose(0, 2, 1, 3)
        q1 = heads(x @ Q1_w.T)
        k1 = heads(x @ K1_w.T + K1_b)
        q2 = heads(x @ Q2_w.T)
        k2 = heads(x @ K2_w.T + K2_b)
        v = heads(x @ V_w.T)
        scale = hd ** 0.5
        a1 = jax.nn.softmax(jnp.einsum('bhqd,bhkd->bhqk', q1, k1) / scale, axis=-1)
        a2 = jax.nn.softmax(jnp.einsum('bhqd,bhkd->bhqk', q2, k2) / scale, axis=-1)
        lam = jnp.exp(lambda_q1 * lambda_k1) - jnp.exp(lambda_q2 * lambda_k2) + LAMBDA_INIT
        attn = a1 - lam.reshape(1, H, 1, 1) * a2
        o = jnp.einsum('bhqk,bhkd->bhqd', attn, v)
        o = o.transpose(0, 2, 1, 3).reshape(b, s, d)
        xc = o.transpose(0, 2, 1).reshape(b, G, d // G, s)
        mu = xc.mean(axis=(2, 3), keepdims=True)
        var = xc.var(axis=(2, 3), keepdims=True)
        xn = ((xc - mu) * jax.lax.rsqrt(var + EPS)).reshape(b, d, s)
        xn = xn * gn_w[None, :, None] + gn_b[None, :, None]
        y = xn.transpose(0, 2, 1) @ out_w.T + out_b
        return y

    def _L0_ffn_ref(x, W_gate, W1, W2):
        import jax, jax.numpy as jnp
        import numpy as np
        K = 2
        B, L, D = x.shape
        E = W_gate.shape[1]
        xf = x.reshape(-1, D)
        T = xf.shape[0]
        probs = jax.nn.softmax(xf @ W_gate, axis=-1)
        top_g, top_i = jax.lax.top_k(probs, K)
        gates = jnp.zeros((T, E), dtype=x.dtype).at[jnp.arange(T)[:, None], top_i].set(top_g)

        def step(y, params):
            W1e, W2e, ge = params
            h = jax.nn.gelu(xf @ W1e, approximate=False)
            return (y + ge[:, None] * (h @ W2e), None)
        y0 = jnp.zeros((T, D), dtype=x.dtype)
        y, _ = jax.lax.scan(step, y0, (W1, W2, gates.T))
        return y.reshape(B, L, D)
    h = _L0_tok_ref(x, L0_tok_gamma, L0_tok_beta, L0_tok_W, L0_tok_b)
    h = h + _L0_attn_ref(_layernorm(h, axis=-1), L0_attn_K1_w, L0_attn_K1_b, L0_attn_Q1_w, L0_attn_K2_w, L0_attn_K2_b, L0_attn_Q2_w, L0_attn_V_w, L0_attn_lambda_q1, L0_attn_lambda_k1, L0_attn_lambda_q2, L0_attn_lambda_k2, L0_attn_gn_w, L0_attn_gn_b, L0_attn_out_w, L0_attn_out_b)
    h = h + _L0_ffn_ref(_layernorm(h, axis=-1), L0_ffn_W_gate, L0_ffn_W1, L0_ffn_W2)
    return h

_drawn_inputs = setup_inputs


def setup_inputs(seed=0):
    import zlib

    import numpy as np

    out = dict(_drawn_inputs(seed))
    spreads = {'L0_tok_b': (0.0, 0.1), 'L0_attn_gn_w': (1.0, 0.2), 'L0_attn_gn_b': (0.0, 0.1)}
    factors = {'L0_attn_K1_w': 3.548,
     'L0_attn_K1_b': 8.0,
     'L0_attn_Q1_w': 3.614,
     'L0_attn_K2_w': 4.668,
     'L0_attn_K2_b': 8.0,
     'L0_attn_Q2_w': 4.569,
     'L0_ffn_W_gate': 7.171,
     'L0_ffn_W1': 6.777,
     'L0_ffn_W2': 6.561}
    for name, (base, spread) in spreads.items():
        noise = np.random.default_rng([zlib.crc32(name.encode()), seed]).standard_normal(out[name].shape)
        drawn = base * np.exp(spread * noise) if base else spread * noise
        out[name] = jnp.asarray(drawn.astype(out[name].dtype))
    for name, factor in factors.items():
        out[name] = (out[name] * factor).astype(out[name].dtype)
    return out
```

```python
import concourse.bass as bass
from concourse import mybir
from concourse.bass import ds
from contextlib import ExitStack

F32 = mybir.dt.float32
BF16 = mybir.dt.bfloat16
U32 = mybir.dt.uint32
I32 = mybir.dt.int32
ALU = mybir.AluOpType
ACT = mybir.ActivationFunctionType
AX = mybir.AxisListType

B, C, S = 64, 2, 104
PATCH, HALF = 8, 4
NP = S // PATCH
NT = NP * NP
ND = NP + 1
V = 5
D = 128
GB = 8
NG = B // GB
GT = GB * NT
TT = 104
TPG = GT // TT
NTILES = NG * TPG
TOKENS = B * NT
IMG = PATCH * S
DPAD = IMG + S + IMG + HALF


def wait_value(eng, sem, value, met):
    if met is not None and not isinstance(value, int):
        value = eng.snap(eng.to_reg(value))
        eng.wait_ge(met, 1)
    eng.wait_ge(sem, value)


def wait_count(eng, sem, per, b, n, met=None):
    value = per * b + n
    if isinstance(value, int) and value <= 0:
        return
    wait_value(eng, sem, value, met)


class Chain:

    def __init__(self, eng, sem, per, b):
        self.eng, self.sem, self.per, self.b, self.n = eng, sem, per, b, 0

    def link(self, ins, met=None):
        self.n += 1
        ins.then_inc(self.sem, 1)
        wait_value(self.eng, self.sem, self.per * self.b + self.n, met)

    def end(self):
        assert self.n == self.per, (self.n, self.per)


def rounds(eng, n, first, last, body):
    for b in range(first):
        body(b, b // 2, b % 2)
    with eng.Fori(first // 2, (n - last) // 2) as i:
        body(2 * i, i, 0)
        body(2 * i + 1, i, 1)
    for b in range(n - last, n):
        body(b, b // 2, b % 2)


def sb_of(nc, ctx, prefix):
    return lambda name, shape, dt=F32: ctx.enter_context(nc.sbuf_tensor(f"{prefix}_{name}", shape, dt))


def ps_of(nc, ctx, prefix):
    return lambda name, shape, dt=F32: ctx.enter_context(nc.psum_tensor(f"{prefix}_{name}", shape, dt))


def sem_of(nc, ctx, prefix):
    return lambda name: ctx.enter_context(nc.semaphore(f"{prefix}_{name}"))


def token_phase(nc, x, gamma, beta, tok_w, tok_b, edge_masks, ident, hid, xt):
    ctx = ExitStack()
    with ctx:
        sb, ps, sem = sb_of(nc, ctx, "t"), ps_of(nc, ctx, "t"), sem_of(nc, ctx, "t")
        raw_p = [sb(f"raw_p{u}", [GB * NP, C, IMG]) for u in range(2)]
        raw_d = [sb(f"raw_d{u}", [GB * ND, DPAD + S]) for u in range(2)]
        cols_p = sb("cols_p", [GB * NP, NP, C, PATCH, PATCH])
        cols_d = sb("cols_d", [GB * ND, ND, C, PATCH, PATCH])
        pat = sb("pat", [128, GB, NP, NP])
        dia = sb("dia", [128, GB, ND, ND])
        norm = sb("norm", [128, V, GB, NT])
        gam = sb("gam", [128, V, NT])
        bet = sb("bet", [128, V, NT])
        w = sb("w", [128, V, D])
        bias = sb("bias", [TT, D])
        masks = sb("masks", [128, 2])
        ones = sb("ones", [128, 128])
        half = sb("half", [128, TPG])
        st = sb("st", [128, GB, V, 6])
        mv = sb("mv", [128, GB, 2])
        mm = sb("mm", [128, GB])
        ms = sb("ms", [128, GB, 2])
        var = sb("var", [128, GB])
        rstd = sb("rstd", [128, GB])
        shift = sb("shift", [128, GB])
        tst = sb("tst", [TT, TPG, 6])
        tmv = sb("tmv", [TT, TPG, 2])
        tvar = sb("tvar", [TT, TPG])
        trstd = sb("trstd", [TT, TPG])
        xl = sb("xl", [TT, TPG, D])
        tp = [ps(f"tp{i}", [128, 4, 128]) for i in range(4)]
        stp = ps("stp", [128, 512])
        yp = [ps(f"yp{i}", [128, 512]) for i in range(2)]
        xp = ps("xp", [128, 4, TT])

        s_const = sem("const")
        s_in = [sem("in0"), sem("in1")]
        s_init = sem("init")
        s_cols = sem("cols")
        s_tp = sem("tp")
        s_tpe = sem("tpe")
        s_stat = sem("stat")
        s_statp = sem("statp")
        s_var = sem("var")
        s_rstd = sem("rstd")
        s_shift = sem("shift")
        s_norm = sem("norm")
        s_gam = sem("gam")
        s_bet = sem("bet")
        s_yp = sem("yp")
        s_y = sem("y")
        s_tvar = sem("tvar")
        s_trstd = sem("trstd")
        s_xl = sem("xl")
        s_xp = sem("xp")
        s_xpe = sem("xpe")
        s_dve = sem("dve")
        DVE_LINKS = 6 + 2 * TPG
        FILLS = 8
        XFILLS = 4

        block = ctx.enter_context(nc.Block())

        @block.sync
        def _(sp):
            sp.dma_start(gam[:, :, :], gamma).then_inc(s_const, 16)
            sp.dma_start(bet[:, :, :], beta).then_inc(s_const, 16)
            sp.dma_start(w[:, :, :], tok_w).then_inc(s_const, 16)
            sp.dma_start(bias[:, :], tok_b).then_inc(s_const, 16)
            sp.dma_start(masks[:, :], edge_masks).then_inc(s_const, 16)
            sp.dma_start(ident[0][:, :], ident[1]).then_inc(s_const, 16)

            def load(g, i, u):
                if isinstance(g, int) and g < 2:
                    sp.wait_ge(s_init, 1)
                wait_count(sp, s_cols, 2, g - 2, 2)
                img = x[ds(g * GB, GB)] if not isinstance(g, int) else x[g * GB:(g + 1) * GB]
                for c in range(C):
                    sp.dma_start(raw_p[u][:, c, :], img[:, c].rearrange("b (p i) w -> b p (i w)", i=PATCH))\
                        .then_inc(s_in[u], 16)
                    o = HALF + c * IMG
                    sp.dma_start(raw_d[u][GB:GB * NP, o:o + IMG],
                                 img[:, c, HALF:S - HALF].rearrange("b (p i) w -> p b (i w)", i=PATCH))\
                        .then_inc(s_in[u], 16)
                    o = HALF + c * IMG
                    h = HALF * S
                    sp.dma_start(raw_d[u][0:GB, o + h:o + 2 * h],
                                 img[:, c, 0:HALF].rearrange("b i w -> b (i w)")).then_inc(s_in[u], 16)
                    sp.dma_start(raw_d[u][GB * NP:GB * ND, o:o + h],
                                 img[:, c, S - HALF:S].rearrange("b i w -> b (i w)")).then_inc(s_in[u], 16)

            rounds(sp, NG, 2, 0, load)

        LOADS = 16 * C * 4

        @block.gpsimd
        def _(pool):
            pool.memset(ones[:, :], 1.0 / 128.0)
            pool.memset(half[:, :], -0.5)
            pool.memset(raw_d[0][:, :], 0.0)
            pool.memset(raw_d[1][:, :], 0.0).then_inc(s_init, 1)
            pool.wait_ge(s_const, 96)

            def body(g, i, u):
                wait_value(pool, s_in[u], LOADS * (i + 1), s_const)
                wait_count(pool, s_tp, FILLS, g - 1, 4, met=s_const)
                for c in range(C):
                    ins = pool.tensor_copy(cols_p[:, :, c, :, :],
                                           raw_p[u][:, c, :].rearrange("p (i q j) -> p q i j", i=PATCH, j=PATCH))
                ins.then_inc(s_cols, 1)
                wait_count(pool, s_tp, FILLS, g - 1, FILLS, met=s_const)
                for c in range(C):
                    o = c * IMG
                    pool.tensor_copy(cols_d[:, 0:NP, c, :, :],
                                     raw_d[u][:, o:o + IMG].rearrange("p (i q j) -> p q i j", i=PATCH, j=PATCH))
                    o += S
                    ins = pool.tensor_copy(cols_d[:, NP, c, :, :],
                                           raw_d[u][:, o:o + IMG].rearrange("p (i w) -> p i w", w=S)[:, :, 0:PATCH])
                ins.then_inc(s_cols, 1)
                wait_count(pool, s_var, 1, g, 1)
                pool.tensor_tensor(rstd[:, :], var[:, :], half[:, 0:GB], ALU.pow).then_inc(s_rstd, 1)
                for b in range(GB):
                    wait_count(pool, s_gam, GB, g, b + 1)
                    pool.tensor_tensor(norm[:, :, b, :], norm[:, :, b, :], bet[:, :, :], ALU.add).then_inc(s_bet, 1)
                wait_count(pool, s_tvar, 1, g, 1)
                pool.tensor_tensor(trstd[:, :], tvar[:, :], half[0:TT, :], ALU.pow).then_inc(s_trstd, 1)

            rounds(pool, NG, 2, 0, body)

        def fills():
            for k in range(4):
                yield "p", 4 * k, min(4, NP - 4 * k)
            for k in range(4):
                yield "d", 4 * k, min(4, ND - 4 * k)

        @block.tensor
        def _(pe):
            pe.wait_ge(s_const, 96)
            pe.wait_ge(s_init, 1)

            def body(g, i, u):
                for f, (kind, q0, n) in enumerate(fills()):
                    if f in (0, 4):
                        wait_count(pe, s_cols, 2, g, 1 + f // 4)
                    wait_count(pe, s_tpe, FILLS, g, f - 3)
                    cols, rows = (cols_p, GB * NP) if kind == "p" else (cols_d, GB * ND)
                    for q in range(n):
                        ins = pe.transpose(tp[f % 4][:, q, 0:rows],
                                           cols[:, q0 + q, :, :, :].rearrange("p c i j -> p (c i j)"),
                                           ident[0][0:rows, 0:rows])
                    ins.then_inc(s_tp, 1)
                wait_count(pe, s_stat, 1, g, 1)
                pe.matmul(stp[:, 0:2 * GB], ones[:, :], mv[:, :, :].rearrange("p b k -> p (b k)"),
                          start=True, stop=True).then_inc(s_statp, 1)
                for t in range(TPG):
                    wait_count(pe, s_bet, GB, g, -(-TT * (t + 1) // NT))
                    wait_count(pe, s_y, TPG, g, t - 1)
                    for v in range(V):
                        ins = pe.matmul(yp[t % 2][0:TT, 0:D],
                                        norm[:, v, :, :].rearrange("p b n -> p (b n)")[:, t * TT:(t + 1) * TT],
                                        w[:, v, :], start=v == 0, stop=v == V - 1)
                    ins.then_inc(s_yp, 1)
                for k in range(XFILLS):
                    wait_count(pe, s_xl, XFILLS, g, k + 1)
                    wait_count(pe, s_xpe, XFILLS, g, k)
                    for t in range(4 * k, min(4 * k + 4, TPG)):
                        ins = pe.transpose(xp[:, t - 4 * k, :], xl[:, t, :], ident[0][0:TT, 0:TT])
                    ins.then_inc(s_xp, 1)

            rounds(pe, NG, 2, 0, body)

        @block.scalar
        def _(act):
            act.wait_ge(s_const, 96)

            def body(g, i, u):
                wait_count(act, s_gam, GB, g - 1, GB)
                for f, (kind, q0, n) in enumerate(fills()):
                    wait_count(act, s_tp, FILLS, g, f + 1)
                    src = tp[f % 4]
                    if kind == "p":
                        ins = act.activation(pat[:, :, :, q0:q0 + n].rearrange("p b a q -> p q (b a)"),
                                             src[:, 0:n, 0:GB * NP], ACT.Copy)
                    else:
                        out = dia[:, :, :, :].rearrange("p b a q -> p q a b")
                        src = src[:, :, 0:GB * ND].rearrange("p q (a b) -> p q a b", b=GB)
                        lo, hi = q0, q0 + n
                        if lo == 0:
                            act.activation(out[:, 0], src[:, 0], ACT.Copy, scale=masks[:, 0:1])
                            lo = 1
                        if hi == ND:
                            act.activation(out[:, NP], src[:, NP - q0], ACT.Copy, scale=masks[:, 1:2])
                            hi = NP
                        ins = act.activation(out[:, lo:hi], src[:, lo - q0:hi - q0], ACT.Copy)
                    ins.then_inc(s_tpe, 1)
                wait_count(act, s_shift, 1, g, 1)
                for b in range(GB):
                    for buf in (pat, dia):
                        ins = act.activation(buf[:, b, :, :], buf[:, b, :, :], ACT.Identity,
                                             bias=shift[:, b:b + 1], scale=rstd[:, b:b + 1])
                    ins.then_inc(s_norm, 1)
                for k in range(XFILLS):
                    wait_count(act, s_xp, XFILLS, g, k + 1)
                    n = min(4, TPG - 4 * k)
                    act.activation(xt[:, ds(g * GT + 4 * k * TT, n * TT)].rearrange("p (t n) -> p t n", n=TT),
                                   xp[:, 0:n, :], ACT.Copy).then_inc(s_xpe, 1)

            rounds(act, NG, 2, 0, body)

        @block.vector
        def _(dve):
            dve.wait_ge(s_const, 96)

            def body(g, i, u):
                chain = Chain(dve, s_dve, DVE_LINKS, g)
                wait_count(dve, s_tpe, FILLS, g, FILLS, met=s_const)
                for b in range(GB):
                    dve.bn_stats(st[:, b, 0, :], pat[:, b, :, :].rearrange("p a q -> p (a q)"))
                    for v, (r, c) in enumerate(((1, 0), (1, 1), (0, 0), (0, 1))):
                        ins = dve.bn_stats(st[:, b, v + 1, :], dia[:, b, r:r + NP, c:c + NP])
                chain.link(ins, met=s_const)
                for b in range(GB):
                    ins = dve.bn_aggr(mv[:, b, :], st[:, b, :, :].rearrange("p v k -> p (v k)"))
                chain.link(ins)
                chain.link(dve.tensor_tensor(mm[:, :], mv[:, :, 0], mv[:, :, 0], ALU.mult))
                dve.tensor_tensor(mv[:, :, 1], mv[:, :, 1], mm[:, :], ALU.add).then_inc(s_stat, 1)
                wait_count(dve, s_statp, 1, g, 1)
                chain.link(dve.tensor_copy(ms[:, :, :].rearrange("p b k -> p (b k)"), stp[:, 0:2 * GB]))
                chain.link(dve.tensor_tensor(mm[:, :], ms[:, :, 0], ms[:, :, 0], ALU.mult))
                chain.link(dve.tensor_tensor(mm[:, :], ms[:, :, 1], mm[:, :], ALU.subtract))
                dve.tensor_scalar(var[:, :], mm[:, :], 0.0, 1e-7, ALU.max, ALU.add).then_inc(s_var, 1)
                wait_count(dve, s_rstd, 1, g, 1)
                dve.scalar_tensor_tensor(out=shift[:, :], in0=ms[:, :, 0], scalar=-1.0, in1=rstd[:, :],
                                         op0=ALU.mult, op1=ALU.mult).then_inc(s_shift, 1)
                wait_count(dve, s_yp, TPG, g - 1, TPG)
                for b in range(GB):
                    wait_count(dve, s_norm, GB, g, b + 1)
                    out = norm[:, :, b, :].rearrange("p v (a q) -> p v a q", q=NP)
                    gm = gam[:, :, :].rearrange("p v (a q) -> p v a q", q=NP)
                    dve.tensor_tensor(out[:, 0], pat[:, b, :, :], gm[:, 0], ALU.mult)
                    for v, (r, c) in enumerate(((1, 0), (1, 1), (0, 0), (0, 1))):
                        ins = dve.tensor_tensor(out[:, v + 1], dia[:, b, r:r + NP, c:c + NP], gm[:, v + 1], ALU.mult)
                    ins.then_inc(s_gam, 1)
                for t in range(TPG):
                    wait_count(dve, s_yp, TPG, g, t + 1)
                    row = hid[:, ds(g * TPG + t, 1), :].rearrange("p o d -> p (o d)")
                    ins = dve.tensor_tensor(row, yp[t % 2][0:TT, 0:D], bias[:, :], ALU.add)
                    ins.then_inc(s_y, 1)
                    wait_count(dve, s_y, TPG, g, t + 1, met=s_const)
                    chain.link(dve.bn_stats(tst[:, t, :], row), met=s_const)
                    chain.link(dve.bn_aggr(tmv[:, t, :], tst[:, t, :]))
                dve.tensor_scalar(tvar[:, :], tmv[:, :, 1], 1e-5, None, ALU.add).then_inc(s_tvar, 1)
                wait_count(dve, s_trstd, 1, g, 1)
                for t in range(TPG):
                    wait_count(dve, s_xp, XFILLS, g - 1, t // 4 + 1)
                    row = hid[:, ds(g * TPG + t, 1), :].rearrange("p o d -> p (o d)")
                    ins = dve.tensor_scalar(xl[:, t, :], row, tmv[:, t, 0:1], trstd[:, t:t + 1],
                                            ALU.subtract, ALU.mult)
                    if t % 4 == 3 or t == TPG - 1:
                        ins.then_inc(s_xl, 1)
                chain.end()

            rounds(dve, NG, 2, 0, body)


H = 8
HD = D // H
HP = H // 2
A = 2
KA, KB = 128, NT - 128
KBP = 64
SLOTS = H + HP
UNIT = 3
UNITS = A * SLOTS // UNIT
UPM = UNITS // A


def attention_phase(nc, proj_w, k_bias, head_mask, head_mask16, sel_w, lam_in, ident, xt):
    ctx = ExitStack()
    with ctx:
        sb, ps, sem = sb_of(nc, ctx, "a"), ps_of(nc, ctx, "a"), sem_of(nc, ctx, "a")
        w = sb("w", [128, 5, D])
        kbias = sb("kbias", [128, A])
        hmask = sb("hmask", [128, H])
        hmask16 = sb("hmask16", [128, H], BF16)
        sel = sb("sel", [128, A, SLOTS, 128], BF16)
        lam4 = sb("lam4", [128, 4])
        lw = sb("lw", [128, 4])
        coef = sb("coef", [128, A, 2])
        par = sb("par", [128, 2])
        xc = [sb(f"xc{u}", [128, KA + KBP]) for u in range(2)]
        qf = [sb(f"qf{u}", [128, A, NT]) for u in range(2)]
        qb = [sb(f"qb{u}", [128, A, KA + KBP], BF16) for u in range(2)]
        kf = [sb(f"kf{u}", [128, A, NT]) for u in range(2)]
        kb = [sb(f"kb{u}", [128, A, NT], BF16) for u in range(2)]
        kma = [sb(f"kma{u}", [128, A, H, KA]) for u in range(2)]
        kmb = [sb(f"kmb{u}", [128, A, H, KBP]) for u in range(2)]
        km16 = [sb(f"km16{u}", [128, A, H, NT], BF16) for u in range(2)]
        mxs = sb("mxs", [128, A, SLOTS])
        mxt = sb("mxt", [128, 128])
        nm = [sb(f"nm{u}", [128, NT], BF16) for u in range(2)]
        prob = sb("prob", [128, UNITS, UNIT, NT])
        va = [sb(f"va{u}", [128, HP, 2, 2 * HD]) for u in range(2)]
        vb = [sb(f"vb{u}", [128, HP, 2, 2 * HD]) for u in range(2)]
        den = sb("den", [128, A, 2, NT])
        term = [sb(f"term{u}", [128, A, 2, NT]) for u in range(2)]
        half = sb("half", [128, 2, NT])
        bx = ps("bx", [128, 512])
        by = ps("by", [128, 512])
        bm = [ps(f"bm{i}", [128, 512]) for i in range(2)]
        bs = [ps(f"bs{i}", [128, 512]) for i in range(2)]
        bo = [ps(f"bo{i}", [128, 512]) for i in range(2)]

        s_const = sem("const")
        s_zero = sem("zero")
        s_ones = sem("ones")
        s_coef = sem("coef")
        s_xc = sem("xc")
        s_q = sem("q")
        s_k = sem("k")
        s_qe = sem("qe")
        s_ke = sem("ke")
        s_v = sem("v")
        s_ve = sem("ve")
        s_km = sem("km")
        s_km16 = sem("km16")
        s_m = sem("m")
        s_mx = sem("mx")
        s_mxt = sem("mxt")
        s_mt = sem("mt")
        s_nm = sem("nm")
        s_s = sem("s")
        s_p = sem("p")
        s_pv = sem("pv")
        s_term = sem("term")
        s_o = sem("o")
        s_dve = sem("dve")
        s_pool = sem("pool")
        DVE_LINKS = A * 2
        block = ctx.enter_context(nc.Block())

        @block.sync
        def _(sp):
            for dst, src in ((w[:, :, :], proj_w), (kbias[:, :], k_bias), (hmask[:, :], head_mask),
                             (hmask16[:, :], head_mask16), (sel[:, :, :, :], sel_w), (lam4[:, :], lam_in[0]),
                             (par[:, :], lam_in[1])):
                sp.dma_start(dst, src).then_inc(s_const, 16)
        CONST = 16 * 7

        @block.gpsimd
        def _(pool):
            for u in range(2):
                for t in (xc[u][:, NT:], qb[u][:, :, NT:], kmb[u][:, :, :, KB:], nm[u][:, :], va[u][:, :, :, :],
                          vb[u][:, :, :, :]):
                    pool.memset(t, 0.0)
            pool.memset(mxt[:, :], 0.0).then_inc(s_zero, 1)
            pool.wait_ge(s_zero, 1)
            for u in range(2):
                pool.memset(va[u][:, :, 0, HD:], 1.0)
                ins = pool.memset(va[u][:, :, 1, 0:HD], 1.0)
            ins.then_inc(s_zero, 1)
            pool.wait_ge(s_const, CONST)

            def fetch(b, i, u):
                wait_count(pool, s_v, 1, b - 2, 1, met=s_const)
                pool.tensor_copy(xc[u][:, 0:NT], xt[:, ds(b * NT, NT)]).then_inc(s_xc, 1)

            def spread(b, i, u):
                wait_count(pool, s_ke, 1, b, 1)
                wait_count(pool, s_s, UNITS, b - 2, UNITS)
                for a in range(A):
                    pool.tensor_tensor(kma[u][:, a, :, :], kf[u][:, a, 0:KA].unsqueeze(1).broadcast_to([128, H, KA]),
                                       hmask[:, :].unsqueeze(2).broadcast_to([128, H, KA]), ALU.mult)
                    ins = pool.tensor_tensor(kmb[u][:, a, :, 0:KB],
                                             kf[u][:, a, KA:NT].unsqueeze(1).broadcast_to([128, H, KB]),
                                             hmask[:, :].unsqueeze(2).broadcast_to([128, H, KB]), ALU.mult)
                ins.then_inc(s_km, 1)

            def gather(b, i, u):
                wait_count(pool, s_term, A, b, A)
                wait_count(pool, s_o, 1, b - 1, 1)
                pool.tensor_tensor(half[:, :, :], term[u][:, 0, :, :], term[u][:, 1, :, :], ALU.add).then_inc(s_pool, 1)
                wait_count(pool, s_pool, 1, b, 1)
                pool.tensor_tensor(xt[:, ds(b * NT, NT)], half[:, 0, :], half[:, 1, :], ALU.add).then_inc(s_o, 1)

            def body(b, i, u):
                if not (isinstance(b, int) and b == 0):
                    gather(b - 1, None, 1 - u)
                if not (isinstance(b, int) and b + 2 >= B):
                    fetch(b + 2, None, u)
                if not (isinstance(b, int) and b + 1 >= B):
                    spread(b + 1, None, 1 - u)

            fetch(0, 0, 0)
            fetch(1, 0, 1)
            spread(0, 0, 0)
            rounds(pool, B, 2, 2, body)
            gather(B - 1, None, 1)

        @block.tensor
        def _(pe):
            pe.wait_ge(s_const, CONST)
            pe.wait_ge(s_zero, 2)
            pe.wait_ge(s_ones, 1)

            def project(b, u):
                wait_count(pe, s_xc, 1, b, 1)
                wait_count(pe, s_ve, 1, b - 1, 1)
                for a in range(A):
                    ins = pe.matmul(bx[:, a * NT:(a + 1) * NT], w[:, a, :], xc[u][:, 0:NT], start=True, stop=True)
                ins.then_inc(s_q, 1)
                wait_count(pe, s_nm, 1, b - 1, 1)
                for a in range(A):
                    ins = pe.matmul(by[:, a * NT:(a + 1) * NT], w[:, 2 + a, :], xc[u][:, 0:NT], start=True, stop=True)
                ins.then_inc(s_k, 1)

            def values(b, u):
                wait_count(pe, s_qe, 1, b, 1)
                pe.matmul(bx[:, 0:D], xc[u][:, 0:KA], w[:, 4, :], start=True, stop=True)
                pe.matmul(bx[0:KBP, D:2 * D], xc[u][:, KA:], w[:, 4, :], start=True, stop=True)
                pe.matmul(bx[KBP:, D:2 * D], xc[u][:, KA:], w[:, 4, :], start=True, stop=True).then_inc(s_v, 1)

            def score_for_max(b, u, n):
                wait_count(pe, s_km16, 1, b, 1)
                wait_count(pe, s_mx, UNITS, b, n - 1)
                a, j = divmod(n, UPM)
                out, q, k = bm[n % 2], qb[u], km16[u]
                first = UNIT * j
                heads = min(H, first + UNIT) - first
                if heads > 0:
                    ins = pe.matmul(out[:, 0:heads * NT], q[:, a, 0:KA],
                                    k[:, a, first:first + heads, :].rearrange("p h n -> p (h n)"), start=True, stop=True)
                heads = max(heads, 0)
                for s in range(heads, UNIT):
                    pair = first + s - H
                    for o in range(2):
                        ins = pe.matmul(out[o * KBP:(o + 1) * KBP, s * NT:(s + 1) * NT], q[:, a, KA:],
                                        k[:, a, 2 * pair + o, :], start=True, stop=True)
                ins.then_inc(s_m, 1)

            def max_across(b, u):
                wait_count(pe, s_mxt, 1, b, 1)
                wait_count(pe, s_ke, 1, b, 1)
                pe.transpose(by[:, 0:128], mxt[:, :], ident[0][:, :]).then_inc(s_mt, 1)

            def score(b, u, n):
                if n == 0:
                    wait_count(pe, s_km, 1, b, 1)
                    wait_count(pe, s_nm, 1, b, 1)
                    wait_count(pe, s_qe, 1, b, 1)
                wait_count(pe, s_p, UNITS, b, n - 1)
                a, j = divmod(n, UPM)
                for s in range(UNIT):
                    t = UNIT * j + s
                    out = bs[n % 2][:, s * NT:(s + 1) * NT]
                    keys = kma[u][:, a, t, :] if t < H else \
                        kmb[u][:, a, 2 * (t - H):2 * (t - H) + 2, :].rearrange("p h n -> p (h n)")
                    pe.matmul(out, keys, qf[u][:, a, :], start=True, stop=False)
                    ins = pe.matmul(out, sel[:, a, t, :], nm[u][:, :], start=False, stop=True)
                ins.then_inc(s_s, 1)

            def weigh(b, u, a):
                wait_count(pe, s_p, UNITS, b, UPM * (a + 1))
                wait_count(pe, s_ve, 1, b, 1)
                wait_count(pe, s_term, A, b - 1, a + 1)
                for o in range(2):
                    cols = slice(o * NT, (o + 1) * NT)
                    for t in range(2):
                        for g in range(HP):
                            slot = 2 * g + o if t == 0 else H + g
                            v = va[u] if t == 0 else vb[u]
                            ins = pe.matmul(bo[a][32 * g:32 * g + 32, cols], v[:, g, o, :],
                                            prob[:, UPM * a + slot // UNIT, slot % UNIT, :], start=t == 0, stop=t == 1)
                ins.then_inc(s_pv, 1)

            def body(b, i, u):
                more = not (isinstance(b, int) and b + 1 >= B)
                nb, nu = b + 1, 1 - u
                if more:
                    project(nb, nu)
                score(b, u, 0)
                score(b, u, 1)
                if more:
                    values(nb, nu)
                score(b, u, 2)
                for n in range(3, 6):
                    if more:
                        score_for_max(nb, nu, n - 3)
                    score(b, u, n)
                weigh(b, u, 0)
                if more:
                    score_for_max(nb, nu, 3)
                score(b, u, 6)
                if more:
                    score_for_max(nb, nu, 4)
                    score_for_max(nb, nu, 5)
                score(b, u, 7)
                if more:
                    score_for_max(nb, nu, 6)
                    score_for_max(nb, nu, 7)
                    max_across(nb, nu)
                weigh(b, u, 1)

            project(0, 0)
            values(0, 0)
            for n in range(UNITS):
                score_for_max(0, 0, n)
            max_across(0, 0)
            rounds(pe, B, 2, 2, body)

        @block.scalar
        def _(act):
            act.wait_ge(s_const, CONST)
            act.wait_ge(s_zero, 2)

            def evict(b, u):
                wait_count(act, s_q, 1, b, 1)
                wait_count(act, s_s, UNITS, b - 2, UNITS)
                src = bx[:, 0:A * NT].rearrange("p (a n) -> p a n", a=A)
                act.activation(qf[u][:, :, :], src, ACT.Copy)
                act.activation(qb[u][:, :, 0:NT], src, ACT.Copy).then_inc(s_qe, 1)
                wait_count(act, s_k, 1, b, 1)
                wait_count(act, s_km, 1, b - 2, 1)
                wait_count(act, s_km16, 1, b - 2, 1)
                for a in range(A):
                    src = by[:, a * NT:(a + 1) * NT]
                    act.activation(kf[u][:, a, :], src, ACT.Identity, bias=kbias[:, a:a + 1])
                    ins = act.activation(kb[u][:, a, :], src, ACT.Identity, bias=kbias[:, a:a + 1])
                ins.then_inc(s_ke, 1)

            def values(b, u):
                wait_count(act, s_v, 1, b, 1)
                wait_count(act, s_pv, A, b - 2, A)
                v = bx[:, 0:2 * D].rearrange("p (t g o d) -> p t g o d", t=2, g=HP, o=2)
                act.activation(va[u][:, :, 0, 0:HD], v[:, 0, :, 0, :], ACT.Copy)
                act.activation(va[u][:, :, 1, HD:], v[:, 0, :, 1, :], ACT.Copy)
                act.activation(vb[u][0:KBP, :, 0, 0:HD], v[0:KBP, 1, :, 0, :], ACT.Copy)
                act.activation(vb[u][KBP:, :, 1, HD:], v[KBP:, 1, :, 1, :], ACT.Copy).then_inc(s_ve, 1)

            def exps(b, u, n):
                wait_count(act, s_s, UNITS, b, n + 1)
                wait_count(act, s_pv, A, b - 1, n // UPM + 1)
                act.activation(prob[:, n, :, :].rearrange("p s n -> p (s n)"), bs[n % 2][:, 0:UNIT * NT],
                               ACT.Exp, scale=HD ** -0.5).then_inc(s_p, 1)

            def body(b, i, u):
                more = not (isinstance(b, int) and b + 1 >= B)
                if more:
                    evict(b + 1, 1 - u)
                exps(b, u, 0)
                exps(b, u, 1)
                if more:
                    values(b + 1, 1 - u)
                for n in range(2, UNITS):
                    exps(b, u, n)

            act.wait_ge(s_coef, 1)
            act.activation(lw[:, 2:4], lw[:, 0:2], ACT.Exp).then_inc(s_coef, 1)
            evict(0, 0)
            values(0, 0)
            rounds(act, B, 2, 2, body)

        @block.vector
        def _(dve):
            dve.wait_ge(s_const, CONST)
            dve.wait_ge(s_zero, 2)
            for u in range(2):
                dve.memset(vb[u][0:KB, :, 0, HD:], 1.0)
                ins = dve.memset(vb[u][KBP:KBP + KB, :, 1, 0:HD], 1.0)
            ins.then_inc(s_ones, 1)
            dve.tensor_tensor(lw[:, 0:2], lam4[:, 0:2], lam4[:, 2:4], ALU.mult).then_inc(s_coef, 1)
            dve.wait_ge(s_coef, 2)
            dve.tensor_tensor(coef[:, 1, 0:1], lw[:, 3:4], lw[:, 2:3], ALU.subtract).then_inc(s_coef, 1)
            dve.wait_ge(s_coef, 3)
            dve.tensor_scalar(coef[:, 1, 1:2], coef[:, 1, 0:1], -0.2, None, ALU.add).then_inc(s_coef, 1)
            dve.wait_ge(s_coef, 4)
            dve.tensor_copy(coef[:, 0, :], par[:, :])
            dve.tensor_scalar(lw[:, 0:2], par[:, :], coef[:, 1, 1:2], None, ALU.mult).then_inc(s_coef, 1)
            dve.wait_ge(s_coef, 5)
            dve.tensor_copy(coef[:, 1, :], lw[:, 0:2]).then_inc(s_coef, 1)
            dve.wait_ge(s_coef, 6)

            def spread(b, u):
                wait_count(dve, s_ke, 1, b, 1)
                wait_count(dve, s_m, UNITS, b - 2, UNITS)
                for a in range(A):
                    ins = dve.tensor_tensor(km16[u][:, a, :, :], kb[u][:, a, :].unsqueeze(1).broadcast_to([128, H, NT]),
                                            hmask16[:, :].unsqueeze(2).broadcast_to([128, H, NT]), ALU.mult)
                ins.then_inc(s_km16, 1)

            def reduce(b, u, n):
                wait_count(dve, s_m, UNITS, b, n + 1)
                wait_count(dve, s_mxt, 1, b - 1, 1)
                a, j = divmod(n, UPM)
                dve.tensor_reduce(mxs[:, a, UNIT * j:UNIT * j + UNIT],
                                  bm[n % 2][:, 0:UNIT * NT].rearrange("p (s n) -> p s n", n=NT),
                                  AX.X, ALU.max).then_inc(s_mx, 1)

            def arrange(b, u):
                wait_count(dve, s_mx, UNITS, b, UNITS)
                wait_count(dve, s_mt, 1, b - 1, 1)
                dve.tensor_copy(mxt[:, 0:A * H].rearrange("p (a h) -> p a h", a=A), mxs[:, :, 0:H])
                for o in (32, 64):
                    ins = dve.tensor_copy(mxt[:, o:o + A * HP].rearrange("p (a h) -> p a h", a=A), mxs[:, :, H:])
                ins.then_inc(s_mxt, 1)

            def negate(b, u):
                wait_count(dve, s_mt, 1, b, 1)
                wait_count(dve, s_s, UNITS, b - 2, UNITS)
                dve.tensor_copy(nm[u][0:32, 0:KA], by[0:32, 0:KA])
                dve.tensor_copy(nm[u][32:64, KA:], by[32:64, 0:KB])
                dve.tensor_copy(nm[u][64:96, KA:], by[64:96, KBP:KBP + KB]).then_inc(s_nm, 1)

            def divide(b, u, a, chain):
                wait_count(dve, s_pv, A, b, a + 1, met=s_const)
                wait_count(dve, s_o, 1, b - 2, 1, met=s_const)
                for o in range(2):
                    ins = dve.stream_shuffle(den[:, a, o, :], bo[a][:, o * NT:(o + 1) * NT],
                                             [HD + k % HD if o == 0 else k % HD for k in range(32)])
                chain.link(ins)
                chain.link(dve.reciprocal(den[:, a, :, :], den[:, a, :, :]))
                for o in range(2):
                    ins = dve.scalar_tensor_tensor(out=term[u][:, a, o, :], in0=den[:, a, o, :],
                                                   scalar=coef[:, a, o:o + 1], in1=bo[a][:, o * NT:(o + 1) * NT],
                                                   op0=ALU.mult, op1=ALU.mult)
                ins.then_inc(s_term, 1)

            def body(b, i, u):
                more = not (isinstance(b, int) and b + 1 >= B)
                nb, nu = b + 1, 1 - u
                chain = Chain(dve, s_dve, DVE_LINKS, b)
                if more:
                    spread(nb, nu)
                    for n in range(3):
                        reduce(nb, nu, n)
                divide(b, u, 0, chain)
                if more:
                    for n in range(3, UNITS):
                        reduce(nb, nu, n)
                    arrange(nb, nu)
                    negate(nb, nu)
                divide(b, u, 1, chain)
                chain.end()

            spread(0, 0)
            for n in range(UNITS):
                reduce(0, 0, n)
            arrange(0, 0)
            negate(0, 0)
            rounds(dve, B, 2, 2, body)


E = 16
K = 2
F = 256
ROW = D + 1
PT = 128
CAP = TOKENS + PT
MTILES = (K * TOKENS + E * (PT - 1)) // PT
XROWS = E * CAP + PT
NOWHERE = 1 << 20


def routing_phase(nc, gn, group_mean, out_w, out_b, gate_w, iotas, prefix, w1, w2, ident, hid, xt, gates, table,
                  weights, xd):
    ctx = ExitStack()
    with ctx:
        sb, ps, sem = sb_of(nc, ctx, "r"), ps_of(nc, ctx, "r"), sem_of(nc, ctx, "r")
        gnw = sb("gnw", [128, 2])
        gmean = sb("gmean", [128, 128])
        ow = sb("ow", [128, D])
        ob = sb("ob", [TT, D])
        gw = sb("gw", [128, E])
        iota_e = sb("iota_e", [TT, E])
        region = sb("region", [TT, E])
        dest = sb("dest", [TT, TPG, K])
        tile_no = sb("tile_no", [1, MTILES])
        pre = sb("pre", [TT, 2, TT], BF16)
        half = sb("half", [128, TPG])
        pad = sb("pad", [PT, ROW])
        st = sb("st", [128, GB, 6])
        mv = sb("mv", [128, GB, 2])
        mm = sb("mm", [128, GB])
        ms = sb("ms", [128, GB, 2])
        var = sb("var", [128, GB])
        rstd = sb("rstd", [128, GB])
        scale = sb("scale", [128, GB])
        shift = sb("shift", [128, GB])
        xn = [sb(f"xn{u}", [128, GB, NT]) for u in range(2)]
        tst = sb("tst", [TT, TPG, 6])
        tmv = sb("tmv", [TT, TPG, 2])
        tvar = sb("tvar", [TT, TPG])
        trstd = sb("trstd", [TT, TPG])
        rows = [sb(f"rows{u}", [TT, TPG, K, ROW]) for u in range(2)]
        x2t = sb("x2t", [128, TPG, TT])
        logit = sb("logit", [TT, TPG, E])
        top = sb("top", [TT, TPG])
        prob = sb("prob", [TT, TPG, E])
        rsum = sb("rsum", [TT, TPG])
        best = sb("best", [TT, TPG, 8])
        which = sb("which", [TT, TPG, 8], U32)
        whichf = sb("whichf", [TT, TPG, K])
        hot = sb("hot", [TT, TPG, K, E])
        hot16 = sb("hot16", [TT, TPG, E], BF16)
        base = sb("base", [TT, TPG + 1, E])
        pos = sb("pos", [TT, TPG, E])
        picked = sb("picked", [TT, TPG, K, E])
        slotf = sb("slotf", [TT, TPG, K])
        slot = [sb(f"slot{u}", [TT, TPG, K], U32) for u in range(2)]
        cnt = sb("cnt", [1, E], I32)
        ntile = sb("ntile", [1, E])
        cum = [sb(f"cum{i}", [1, E]) for i in range(2)]
        skip = sb("skip", [1, E])
        past = sb("past", [1, MTILES, E])
        tab = sb("tab", [1, MTILES])
        padrow = sb("padrow", [1, E], I32)
        gp = ps("gp", [128, 512])
        cy = [ps(f"cy{i}", [128, 512]) for i in range(2)]
        xp = [ps(f"xp{i}", [128, 4, TT]) for i in range(2)]
        lg = ps("lg", [128, TPG, E])
        pf = ps("pf", [128, 2, TPG * E])

        s_const = sem("const")
        s_init = sem("init")
        s_stat = sem("stat")
        s_statp = sem("statp")
        s_var = sem("var")
        s_rstd = sem("rstd")
        s_shift = sem("shift")
        s_xn = sem("xn")
        s_hb = sem("hb")
        s_cy = sem("cy")
        s_h = sem("h")
        s_tvar = sem("tvar")
        s_trstd = sem("trstd")
        s_x2 = sem("x2")
        s_x2b = sem("x2b")
        s_xp = sem("xp")
        s_xpe = sem("xpe")
        s_lg = sem("lg")
        s_sub = sem("sub")
        s_exp = sem("exp")
        s_hot = sem("hot")
        s_pf = sem("pf")
        s_slot = sem("slot")
        s_sc = [sem("sc0"), sem("sc1")]
        s_pad = sem("pad")
        s_padw = sem("padw")
        s_dve = sem("dve")
        s_end = sem("end")
        s_w = sem("w")
        LINKS = 23 + 3 * TPG
        XF = 4
        block = ctx.enter_context(nc.Block())

        @block.sync
        def _(sp):
            for dst, src in ((gnw[:, :], gn), (gmean[:, :], group_mean), (ow[:, :], out_w), (ob[:, :], out_b),
                             (gw[:, :], gate_w), (iota_e[:, :], iotas[0]), (region[:, :], iotas[1]),
                             (dest[:, :, :], iotas[2]), (tile_no[:, :], iotas[3]), (pre[:, :, :], prefix)):
                sp.dma_start(dst, src).then_inc(s_const, 16)
            sp.dma_start(weights[0][:, :, :], w1).then_inc(s_w, 16)
            sp.dma_start(weights[1][:, :, :, :], w2).then_inc(s_w, 16)
            sp.wait_ge(s_pad, 1)
            for e in range(E):
                row = sp.value_load(padrow[0:1, e:e + 1], min_val=e * CAP, max_val=e * CAP + TOKENS)
                sp.dma_start(xd[ds(row, PT), :], pad[:, :]).then_inc(s_padw, 16)
            sp.dma_start(xd[E * CAP:E * CAP + PT, :], pad[:, :]).then_inc(s_padw, 16)
            sp.wait_ge(s_padw, 16 * (E + 1))
            sp.wait_ge(s_w, 32)
        CONST = 160

        @block.gpsimd
        def _(pool):
            pool.memset(half[:, :], -0.5)
            pool.memset(pad[:, 0:D], 0.0)
            pool.memset(pad[:, D:ROW].bitcast(U32), NOWHERE)
            pool.memset(base[:, :, :], 0.0).then_inc(s_init, 1)
            pool.wait_ge(s_init, 1)
            pool.wait_ge(s_const, CONST)

            def body(g, i, u):
                tiles = hid[:, ds(g * TPG, TPG), :]
                pool.tensor_tensor(tiles, tiles, ob[:, :].unsqueeze(1).broadcast_to([TT, TPG, D]), ALU.add)\
                    .then_inc(s_hb, 1)
                wait_count(pool, s_var, 1, g, 1)
                pool.tensor_tensor(rstd[:, :], var[:, :], half[:, 0:GB], ALU.pow).then_inc(s_rstd, 1)
                wait_count(pool, s_tvar, 1, g, 1)
                pool.tensor_tensor(trstd[:, :], tvar[:, :], half[0:TT, :], ALU.pow).then_inc(s_trstd, 1)
                wait_count(pool, s_slot, 1, g, 1)
                wait_count(pool, s_x2b, XF, g, XF, met=s_const)
                for t in range(TPG):
                    for k in range(K):
                        pool.indirect_dma_start(xd[:, :], bass.IndirectOffsetOnAxis(ap=slot[u][:, t, k:k + 1], axis=0),
                                                rows[u][:, t, k, :], None).then_inc(s_sc[u], 16)

            rounds(pool, NG, 2, 0, body)
            for u in range(2):
                pool.wait_ge(s_sc[u], 16 * K * TPG * NG // 2)

        @block.tensor
        def _(pe):
            pe.wait_ge(s_const, CONST)

            def body(g, i, u):
                wait_count(pe, s_stat, 1, g, 1)
                pe.matmul(gp[:, 0:2 * GB], gmean[:, :], mv[:, :, :].rearrange("p b k -> p (b k)"),
                          start=True, stop=True).then_inc(s_statp, 1)
                for t in range(TPG):
                    wait_count(pe, s_xn, GB, g, -(-TT * (t + 1) // NT))
                    wait_count(pe, s_h, TPG, g, t - 1)
                    pe.matmul(cy[t % 2][0:TT, 0:D], xn[u][:, :, :].rearrange("p b n -> p (b n)")[:, t * TT:(t + 1) * TT],
                              ow[:, :], start=True, stop=True).then_inc(s_cy, 1)
                for k in range(XF):
                    wait_count(pe, s_x2, XF, g, k + 1)
                    wait_count(pe, s_xpe, XF, g, k - 1)
                    for t in range(4 * k, min(4 * k + 4, TPG)):
                        ins = pe.transpose(xp[k % 2][:, t - 4 * k, :], rows[u][:, t, 0, 0:D], ident[0][0:TT, 0:TT])
                    ins.then_inc(s_xp, 1)
                wait_count(pe, s_sub, 1, g - 1, 1)
                for t in range(TPG):
                    wait_count(pe, s_xpe, XF, g, t // 4 + 1)
                    ins = pe.matmul(lg[0:TT, t, :], x2t[:, t, :], gw[:, :], start=True, stop=True)
                ins.then_inc(s_lg, 1)
                wait_count(pe, s_hot, 1, g, 1)
                wait_count(pe, s_slot, 1, g - 1, 1)
                for m in range(2):
                    ins = pe.matmul(pf[0:TT, m, :], pre[:, m, :], hot16[:, :, :].rearrange("p t e -> p (t e)"),
                                    start=True, stop=True)
                ins.then_inc(s_pf, 1)

            rounds(pe, NG, 2, 0, body)

        @block.scalar
        def _(act):
            act.wait_ge(s_const, CONST)

            def body(g, i, u):
                wait_count(act, s_shift, 1, g, 1)
                wait_count(act, s_cy, TPG, g - 2, TPG)
                for b in range(GB):
                    act.activation(xn[u][:, b, :], xt[:, ds((g * GB + b) * NT, NT)], ACT.Identity,
                                   bias=shift[:, b:b + 1], scale=scale[:, b:b + 1]).then_inc(s_xn, 1)
                wait_count(act, s_lg, 1, g - 1, 1)
                for k in range(XF):
                    n = min(4, TPG - 4 * k)
                    wait_count(act, s_x2, XF, g, k + 1)
                    act.activation(rows[u][:, 4 * k:4 * k + n, 1, 0:D], rows[u][:, 4 * k:4 * k + n, 0, 0:D], ACT.Copy)\
                        .then_inc(s_x2b, 1)
                    wait_count(act, s_xp, XF, g, k + 1)
                    act.activation(x2t[:, 4 * k:4 * k + n, :], xp[k % 2][:, 0:n, :], ACT.Copy).then_inc(s_xpe, 1)
                wait_count(act, s_sub, 1, g, 1)
                act.activation(prob[:, :, :], logit[:, :, :], ACT.Exp).then_inc(s_exp, 1)

            rounds(act, NG, 2, 0, body)

        @block.vector
        def _(dve):
            dve.wait_ge(s_const, CONST)
            dve.wait_ge(s_init, 1)

            def body(g, i, u):
                chain = Chain(dve, s_dve, LINKS, g)
                link = chain.link
                wait_count(dve, s_statp, 1, g - 1, 1, met=s_const)
                for b in range(GB):
                    ins = dve.bn_stats(st[:, b, :], xt[:, ds((g * GB + b) * NT, NT)])
                link(ins, met=s_const)
                for b in range(GB):
                    ins = dve.bn_aggr(mv[:, b, :], st[:, b, :])
                link(ins)
                link(dve.tensor_tensor(mm[:, :], mv[:, :, 0], mv[:, :, 0], ALU.mult))
                dve.tensor_tensor(mv[:, :, 1], mv[:, :, 1], mm[:, :], ALU.add).then_inc(s_stat, 1)
                wait_count(dve, s_statp, 1, g, 1)
                link(dve.tensor_copy(ms[:, :, :].rearrange("p b k -> p (b k)"), gp[:, 0:2 * GB]))
                link(dve.tensor_tensor(mm[:, :], ms[:, :, 0], ms[:, :, 0], ALU.mult))
                link(dve.tensor_tensor(mm[:, :], ms[:, :, 1], mm[:, :], ALU.subtract))
                dve.tensor_scalar(var[:, :], mm[:, :], 0.0, 1e-5, ALU.max, ALU.add).then_inc(s_var, 1)
                wait_count(dve, s_rstd, 1, g, 1)
                wait_count(dve, s_xn, GB, g - 1, GB)
                link(dve.tensor_scalar(scale[:, :], rstd[:, :], gnw[:, 0:1], None, ALU.mult))
                link(dve.tensor_tensor(mm[:, :], ms[:, :, 0], scale[:, :], ALU.mult))
                dve.tensor_scalar(shift[:, :], mm[:, :], -1.0, gnw[:, 1:2], ALU.mult, ALU.add).then_inc(s_shift, 1)
                wait_count(dve, s_hb, 1, g, 1)
                for t in range(TPG):
                    wait_count(dve, s_cy, TPG, g, t + 1)
                    row = hid[:, ds(g * TPG + t, 1), :].rearrange("p o d -> p (o d)")
                    dve.tensor_tensor(row, cy[t % 2][0:TT, 0:D], row, ALU.add).then_inc(s_h, 1)
                    wait_count(dve, s_h, TPG, g, t + 1, met=s_const)
                    link(dve.bn_stats(tst[:, t, :], row), met=s_const)
                    link(dve.bn_aggr(tmv[:, t, :], tst[:, t, :]))
                dve.tensor_scalar(tvar[:, :], tmv[:, :, 1], 1e-5, None, ALU.add).then_inc(s_tvar, 1)
                wait_count(dve, s_trstd, 1, g, 1)
                if isinstance(g, int):
                    if i > 0:
                        dve.wait_ge(s_sc[u], 16 * K * TPG * i)
                else:
                    dve.wait_ge(s_sc[u], i * (16 * K * TPG))
                for t in range(TPG):
                    row = hid[:, ds(g * TPG + t, 1), :].rearrange("p o d -> p (o d)")
                    ins = dve.tensor_scalar(rows[u][:, t, 0, 0:D], row, tmv[:, t, 0:1], trstd[:, t:t + 1],
                                            ALU.subtract, ALU.mult)
                    if t % 4 == 3 or t == TPG - 1:
                        ins.then_inc(s_x2, 1)
                link(dve.tensor_copy(rows[u][:, :, :, D].bitcast(U32), dest[:, :, :]))
                link(dve.tensor_scalar(dest[:, :, :], dest[:, :, :], float(K * GT), None, ALU.add))
                wait_count(dve, s_lg, 1, g, 1)
                wait_count(dve, s_exp, 1, g - 1, 1)
                link(dve.tensor_reduce(top[:, :], lg[0:TT, :, :], AX.X, ALU.max))
                dve.tensor_tensor(logit[:, :, :], lg[0:TT, :, :], top[:, :].unsqueeze(2).broadcast_to([TT, TPG, E]),
                                  ALU.subtract).then_inc(s_sub, 1)
                wait_count(dve, s_exp, 1, g, 1)
                link(dve.tensor_reduce(rsum[:, :], prob[:, :, :], AX.X, ALU.add))
                link(dve.reciprocal(rsum[:, :], rsum[:, :]))
                link(dve.tensor_tensor(prob[:, :, :], prob[:, :, :], rsum[:, :].unsqueeze(2).broadcast_to([TT, TPG, E]),
                                       ALU.mult), met=s_const)
                for t in range(TPG):
                    ins = dve.max(best[:, t, :], prob[:, t, :])
                link(ins, met=s_const)
                for t in range(TPG):
                    ins = dve.max_index(which[:, t, :], best[:, t, :], prob[:, t, :])
                link(ins)
                dve.tensor_copy(gates[:, ds(g * TPG, TPG), :], best[:, :, 0:K])
                link(dve.tensor_copy(whichf[:, :, :], which[:, :, 0:K]))
                link(dve.tensor_tensor(hot[:, :, :, :],
                                       iota_e[:, :].unsqueeze(1).unsqueeze(1).broadcast_to([TT, TPG, K, E]),
                                       whichf[:, :, :].unsqueeze(3).broadcast_to([TT, TPG, K, E]), ALU.is_equal))
                dve.tensor_tensor(hot16[:, :, :], hot[:, :, 0, :], hot[:, :, 1, :], ALU.add).then_inc(s_hot, 1)
                link(dve.tensor_copy(base[:, 0, :], base[:, TPG, :]))
                wait_count(dve, s_pf, 1, g, 1)
                tot = pf[0:TT, 1, :].rearrange("p (t e) -> p t e", e=E)
                for t in range(TPG):
                    link(dve.tensor_tensor(base[:, t + 1, :], tot[:, t, :], base[:, t, :], ALU.add))
                link(dve.tensor_tensor(pos[:, :, :], pf[0:TT, 0, :].rearrange("p (t e) -> p t e", e=E),
                                       base[:, 0:TPG, :], ALU.add))
                link(dve.tensor_tensor(pos[:, :, :], pos[:, :, :], region[:, :].unsqueeze(1).broadcast_to([TT, TPG, E]),
                                       ALU.add))
                link(dve.tensor_tensor(picked[:, :, :, :], hot[:, :, :, :],
                                       pos[:, :, :].unsqueeze(2).broadcast_to([TT, TPG, K, E]), ALU.mult))
                link(dve.tensor_reduce(slotf[:, :, :], picked[:, :, :, :], AX.X, ALU.add))
                dve.tensor_copy(slot[u][:, :, :], slotf[:, :, :]).then_inc(s_slot, 1)
                chain.end()

            rounds(dve, NG, 2, 0, body)

            n = [0]

            def link(ins):
                n[0] += 1
                ins.then_inc(s_end, 1)
                dve.wait_ge(s_end, n[0])

            count = base[0:1, TPG, :]
            link(dve.tensor_copy(cnt[:, :], count))
            dve.tensor_tensor(padrow[:, :], count, region[0:1, :], ALU.add).then_inc(s_pad, 1)
            link(dve.tensor_scalar(skip[:, :], count, float(PT - 1), None, ALU.add))
            link(dve.tensor_copy(cnt[:, :], skip[:, :]))
            link(dve.tensor_single_scalar(cnt[:, :], cnt[:, :], PT.bit_length() - 1, ALU.logical_shift_right))
            link(dve.tensor_copy(ntile[:, :], cnt[:, :]))
            link(dve.tensor_copy(cum[0][:, :], ntile[:, :]))
            for k, s in enumerate((1, 2, 4, 8)):
                a, b = cum[k % 2], cum[1 - k % 2]
                link(dve.tensor_copy(b[:, :], a[:, :]))
                link(dve.tensor_tensor(b[:, s:], a[:, s:], a[:, :E - s], ALU.add))
            link(dve.tensor_scalar(skip[:, :], ntile[:, :], -float(PT), float(CAP), ALU.mult, ALU.add))
            link(dve.tensor_tensor(past[:, :, :], tile_no[:, :].unsqueeze(2).broadcast_to([1, MTILES, E]),
                                   cum[0][:, :].unsqueeze(1).broadcast_to([1, MTILES, E]), ALU.is_ge))
            link(dve.tensor_reduce(tab[:, :], past[:, :, :], AX.X, ALU.add))
            link(dve.tensor_scalar(table[0:1, 1, :], tab[:, :], float(E - 1), None, ALU.min))
            link(dve.tensor_tensor(past[:, :, :], past[:, :, :], skip[:, :].unsqueeze(1).broadcast_to([1, MTILES, E]),
                                   ALU.mult))
            link(dve.tensor_reduce(tab[:, :], past[:, :, :], AX.X, ALU.add))
            link(dve.scalar_tensor_tensor(out=tab[:, :], in0=tile_no[:, :], scalar=float(PT), in1=tab[:, :],
                                          op0=ALU.mult, op1=ALU.add))
            link(dve.tensor_scalar(table[0:1, 0, :], tab[:, :], float(E * CAP), None, ALU.min))


def expert_phase(nc, weights, ident, table, xd, yd):
    w1s, w2s = weights
    ctx = ExitStack()
    with ctx:
        sb, ps, sem = sb_of(nc, ctx, "e"), ps_of(nc, ctx, "e"), sem_of(nc, ctx, "e")
        R = 8
        YR = 4
        w1c = [sb(f"w1c{u}", [128, F]) for u in range(2)]
        xin = [sb(f"xin{u}", [PT, ROW]) for u in range(R)]
        xts = [sb(f"xts{u}", [128, PT]) for u in range(2)]
        act1 = [sb(f"act{u}", [128, 2, PT]) for u in range(2)]
        ys = [sb(f"ys{u}", [PT, D]) for u in range(YR)]
        tp = [ps(f"tp{u}", [128, 512]) for u in range(2)]
        hp = [ps(f"hp{u}", [128, 512]) for u in range(2)]
        yp = [ps(f"yp{u}", [128, 512]) for u in range(2)]
        s_go = sem("go")
        go = sb("go", [128, 1])
        s_in = [sem(f"in{u}") for u in range(R)]
        s_wc = sem("wc")
        s_tp = sem("tp")
        s_xt = sem("xt")
        s_hp = sem("hp")
        s_act = sem("act")
        s_yp = sem("yp")
        s_ys = sem("ys")
        s_out = [sem(f"out{u}") for u in range(R)]
        block = ctx.enter_context(nc.Block())

        def tiles(eng, body):
            for t in range(R):
                body(t, 0, t)
            with eng.Fori(1, MTILES // R - 1) as i:
                for u in range(R):
                    body(i * R + u, i, u)
            for t in range(MTILES - R, MTILES):
                body(t, t // R, t % R)

        def ahead(t, i, u, n):
            if isinstance(t, int) and t + n >= MTILES:
                return None
            return t + n, i + (u + n) // R, (u + n) % R

        @block.sync
        def _(sp):
            def load(t, i, u):
                row = sp.value_load(table[0:1, 0, ds(t, 1)], min_val=0, max_val=E * CAP)
                if not (isinstance(t, int) and t < R):
                    sp.wait_ge(s_out[u], i * 16)
                sp.dma_start(xin[u][:, :], xd[ds(row, PT), :]).then_inc(s_in[u], 16)

            tiles(sp, load)

        @block.tensor
        def _(pe):
            def flip(t, i, u):
                pe.wait_ge(s_in[u], i * 16 + 16)
                wait_count(pe, s_xt, 1, t, -1)
                pe.transpose(tp[u % 2][:, 0:PT], xin[u][:, 0:D], ident[0][:, :]).then_inc(s_tp, 1)

            def up(t, i, u):
                v = u % 2
                wait_count(pe, s_wc, 1, t, 1)
                wait_count(pe, s_xt, 1, t, 1)
                wait_count(pe, s_act, 1, t, -1)
                for f in range(2):
                    ins = pe.matmul(hp[v][:, f * PT:(f + 1) * PT], w1c[v][:, f * 128:(f + 1) * 128], xts[v][:, :],
                                    start=True, stop=True)
                ins.then_inc(s_hp, 1)

            def down(t, i, u):
                v = u % 2
                e = pe.value_load(table[0:1, 1, ds(t, 1)], min_val=0, max_val=E - 1)
                wait_count(pe, s_act, 1, t, 1)
                wait_count(pe, s_ys, 1, t, -1)
                for f in range(2):
                    ins = pe.matmul(yp[v][:, 0:D], act1[v][:, f, :],
                                    w2s[:, ds(e, 1), f, :].rearrange("p o d -> p (o d)"), start=f == 0, stop=f == 1)
                ins.then_inc(s_yp, 1)

            def body(t, i, u):
                if nxt := ahead(t, i, u, 2):
                    flip(*nxt)
                if nxt := ahead(t, i, u, 1):
                    up(*nxt)
                down(t, i, u)

            flip(0, 0, 0)
            flip(1, 0, 1)
            up(0, 0, 0)
            tiles(pe, body)

        @block.scalar
        def _(act):
            def evict(t, i, u):
                wait_count(act, s_tp, 1, t, 1)
                wait_count(act, s_hp, 1, t, -1)
                act.activation(xts[u % 2][:, :], tp[u % 2][:, 0:PT], ACT.Copy).then_inc(s_xt, 1)

            def gelu(t, i, u):
                wait_count(act, s_hp, 1, t, 1)
                wait_count(act, s_yp, 1, t, -1)
                act.activation(act1[u % 2][:, :, :].rearrange("p f n -> p (f n)"), hp[u % 2][:, 0:2 * PT], ACT.Gelu)\
                    .then_inc(s_act, 1)

            def body(t, i, u):
                if nxt := ahead(t, i, u, 2):
                    evict(*nxt)
                if nxt := ahead(t, i, u, 1):
                    gelu(*nxt)

            evict(0, 0, 0)
            evict(1, 0, 1)
            gelu(0, 0, 0)
            tiles(act, body)

        @block.vector
        def _(dve):
            def stage(t, i, u):
                e = dve.value_load(table[0:1, 1, ds(t, 1)], min_val=0, max_val=E - 1)
                wait_count(dve, s_hp, 1, t, -1)
                dve.tensor_copy(w1c[u % 2][:, :], w1s[:, ds(e, 1), :].rearrange("p o f -> p (o f)")).then_inc(s_wc, 1)

            def body(t, i, u):
                if nxt := ahead(t, i, u, 2):
                    stage(*nxt)
                wait_count(dve, s_yp, 1, t, 1)
                if not (isinstance(t, int) and t < YR):
                    dve.wait_ge(s_out[(u + YR) % R], (i + (u >= YR)) * 16)
                dve.tensor_copy(ys[u % YR][:, :], yp[u % 2][:, 0:D]).then_inc(s_ys, 1)

            stage(0, 0, 0)
            stage(1, 0, 1)
            tiles(dve, body)

        @block.gpsimd
        def _(pool):
            pool.memset(go[:, :], 0.0).then_inc(s_go, 1)

            def send(t, i, u):
                pool.wait_ge(s_in[u], i * 16 + 16)
                wait_count(pool, s_ys, 1, t, 1, met=s_go)
                pool.indirect_dma_start(yd[:, :], bass.IndirectOffsetOnAxis(ap=xin[u][:, D:ROW].bitcast(U32), axis=0),
                                        ys[u % YR][:, :], None, bounds_check=K * TOKENS - 1, oob_is_err=False)\
                    .then_inc(s_out[u], 16)

            tiles(pool, send)
            for u in range(R):
                pool.wait_ge(s_out[u], 16 * MTILES // R)


def combine_phase(nc, hid, gates, yd, out):
    ctx = ExitStack()
    with ctx:
        sb, sem = sb_of(nc, ctx, "c"), sem_of(nc, ctx, "c")
        N = 4
        yin = [sb(f"yin{u}", [TT, N, K * D]) for u in range(2)]
        res = [sb(f"res{u}", [TT, N, D]) for u in range(2)]
        s_in = [sem("in0"), sem("in1")]
        s_one = sem("one")
        s_two = sem("two")
        s_out = [sem("out0"), sem("out1")]
        yv = yd.rearrange("(t p k) d -> p t (k d)", p=TT, k=K)
        ov = out.rearrange("b n d -> (b n) d").rearrange("(t p) d -> p t d", p=TT)
        block = ctx.enter_context(nc.Block())
        ROUNDS = NTILES // N

        @block.sync
        def _(sp):
            def load(r, i, u):
                wait_count(sp, s_two, N, r - 2, N)
                sp.dma_start(yin[u][:, :, :], yv[:, ds(r * N, N), :]).then_inc(s_in[u], 16)

            rounds(sp, ROUNDS, 2, 0, load)

        @block.vector
        def _(dve):
            def body(r, i, u):
                dve.wait_ge(s_in[u], i * 16 + 16)
                if isinstance(r, int):
                    if i > 0:
                        dve.wait_ge(s_out[u], 16 * i)
                else:
                    dve.wait_ge(s_out[u], i * 16)
                for k, s in ((0, s_one), (1, s_two)):
                    for t in range(N):
                        row = hid[:, ds(r * N + t, 1), :] if k == 0 else res[u][:, t:t + 1, :]
                        if k:
                            wait_count(dve, s_one, N, r, t + 1)
                        dve.scalar_tensor_tensor(
                            out=res[u][:, t, :], in0=yin[u][:, t, k * D:(k + 1) * D],
                            scalar=gates[:, ds(r * N + t, 1), k], in1=row.rearrange("p o d -> p (o d)"),
                            op0=ALU.mult, op1=ALU.add).then_inc(s, 1)

            rounds(dve, ROUNDS, 2, 0, body)

        @block.scalar
        def _(act):
            def store(r, i, u):
                wait_count(act, s_two, N, r, N)
                act.dma_start(ov[:, ds(r * N, N), :], res[u][:, :, :]).then_inc(s_out[u], 16)

            rounds(act, ROUNDS, 2, 0, store)
            for u in range(2):
                act.wait_ge(s_out[u], 16 * ROUNDS // 2)


def vit_tower_kernel(nc, x, gamma, beta, tok_w, tok_b, edge_masks, ident_in, proj_w, k_bias, head_mask, head_mask16,
                     sel, lam, parity, gn, group_mean, out_w, out_b, gate_w, iota_e, region, dest, tile_no, prefix,
                     w1, w2, out):
    xd = nc.dram_tensor("routed_rows", [XROWS, ROW], F32, kind="Internal").ap()
    yd = nc.dram_tensor("expert_rows", [K * TOKENS, D], F32, kind="Internal").ap()
    ctx = ExitStack()
    with ctx:
        sb = sb_of(nc, ctx, "k")
        hid = sb("hid", [TT, NTILES, D])
        ident = (sb("ident", [128, 128]), ident_in)
        gates = sb("gates", [TT, NTILES, K])
        table = sb("table", [1, 2, MTILES], I32)
        xt = sb("xt", [128, TOKENS])
        token_phase(nc, x, gamma, beta, tok_w, tok_b, edge_masks, ident, hid, xt)
        attention_phase(nc, proj_w, k_bias, head_mask, head_mask16, sel, (lam, parity), ident, xt)
        weights = (sb("w1s", [128, E, F]), sb("w2s", [128, E, 2, D]))
        routing_phase(nc, gn, group_mean, out_w, out_b, gate_w, (iota_e, region, dest, tile_no), prefix,
                      w1, w2, ident, hid, xt, gates, table, weights, xd)
        expert_phase(nc, weights, ident, table, xd, yd)
        combine_phase(nc, hid, gates, yd, out)


def kernel(**inputs):
    import ml_dtypes as _ml
    import numpy as _np
    import concourse.bacc as _bacc
    from concourse import mybir as _mybir
    from concourse.bass_utils import run_bass_kernel_spmd as _run

    a = {n: _np.asarray(v) for n, v in inputs.items()}

    def pixels(m):
        return m.reshape(V, C, NP, PATCH, NP, PATCH).transpose(1, 3, 5, 0, 2, 4).reshape(128, V, NT)

    part = _np.arange(128)
    heads = (part[:, None] // HD == _np.arange(H)[None]).astype(_np.float32)
    sel = _np.zeros((128, A, SLOTS, 128), _np.float32)
    for m in range(A):
        for h in range(H):
            sel[m * H + h, m, h, :] = -1
            sel[32 + 32 * (h % 2) + m * HP + h // 2, m, h, :] = -1
        for g in range(HP):
            for o in range(2):
                sel[[m * H + 2 * g + o, 32 + 32 * o + m * HP + g], m, H + g, KBP * o:KBP * o + KB] = -1
    tok = _np.arange(TT)
    laid = {
        "x": a["x"],
        "gamma": pixels(a["L0_tok_gamma"]),
        "beta": pixels(a["L0_tok_beta"]),
        "tok_w": a["L0_tok_W"].reshape(D, V, 128).transpose(2, 1, 0),
        "tok_b": _np.broadcast_to(a["L0_tok_b"], (TT, D)),
        "edge_masks": _np.stack([part % PATCH >= HALF, part % PATCH < HALF], 1).astype(_np.float32),
        "ident_in": _np.eye(128, dtype=_np.float32),
        "proj_w": _np.stack([a[f"L0_attn_{n}_w"].T for n in ("Q1", "Q2", "K1", "K2", "V")], 1),
        "k_bias": _np.stack([a["L0_attn_K1_b"], a["L0_attn_K2_b"]], 1),
        "head_mask": heads,
        "head_mask16": heads.astype(_ml.bfloat16),
        "sel": sel.astype(_ml.bfloat16),
        "lam": _np.stack([_np.repeat(a[f"L0_attn_lambda_{n}"][:, 0], HD) for n in ("q1", "q2", "k1", "k2")], 1),
        "parity": _np.stack([part % (2 * HD) < HD, part % (2 * HD) >= HD], 1).astype(_np.float32),
        "gn": _np.stack([a["L0_attn_gn_w"], a["L0_attn_gn_b"]], 1),
        "group_mean": ((part[:, None] // 32 == part[None] // 32) / 32).astype(_np.float32),
        "out_w": a["L0_attn_out_w"].T,
        "out_b": _np.broadcast_to(a["L0_attn_out_b"], (TT, D)),
        "gate_w": a["L0_ffn_W_gate"],
        "iota_e": _np.broadcast_to(_np.arange(E, dtype=_np.float32), (TT, E)),
        "region": _np.broadcast_to(_np.arange(E, dtype=_np.float32) * CAP, (TT, E)),
        "dest": (K * (_np.arange(TPG)[None, :, None] * TT + tok[:, None, None]) + _np.arange(K)).astype(_np.float32),
        "tile_no": _np.arange(MTILES, dtype=_np.float32)[None],
        "prefix": _np.stack([tok[:, None] < tok[None], _np.ones((TT, TT), bool)], 1).astype(_ml.bfloat16),
        "w1": a["L0_ffn_W1"].transpose(1, 0, 2),
        "w2": a["L0_ffn_W2"].reshape(E, 2, 128, D).transpose(2, 0, 1, 3),
    }
    nc = _bacc.Bacc("TRN2", target_bir_lowering=False, num_devices=1)
    arrays, args = {}, {}
    for name, v in laid.items():
        v = _np.ascontiguousarray(v)
        arrays[f"in_{name}_dram"] = v
        args[name] = nc.dram_tensor(f"in_{name}_dram", v.shape, _mybir.dt.from_np(v.dtype), kind="ExternalInput").ap()
    args["out"] = nc.dram_tensor("out_0_dram", (B, NT, D), _mybir.dt.float32, kind="ExternalOutput").ap()
    vit_tower_kernel(nc, **args)
    r = _run(nc, [arrays], core_ids=[0])
    return r.results[0]["out_0_dram"]
```

```python
import concourse.bass as bass
from concourse import mybir
from concourse.bass import ds
from contextlib import ExitStack

F32 = mybir.dt.float32
BF16 = mybir.dt.bfloat16
U32 = mybir.dt.uint32
I32 = mybir.dt.int32
ALU = mybir.AluOpType
ACT = mybir.ActivationFunctionType
AX = mybir.AxisListType

B, C, S = 64, 2, 104
PATCH, HALF = 8, 4
NP = S // PATCH
NT = NP * NP
ND = NP + 1
V = 5
D = 128
GB = 8
NG = B // GB
GT = GB * NT
TT = 104
TPG = GT // TT
NTILES = NG * TPG
TOKENS = B * NT
IMG = PATCH * S
DPAD = IMG + S + IMG + HALF


def wait_value(eng, sem, value, met):
    if met is not None and not isinstance(value, int):
        value = eng.snap(eng.to_reg(value))
        eng.wait_ge(met, 1)
    eng.wait_ge(sem, value)


def wait_count(eng, sem, per, b, n, met=None):
    value = per * b + n
    if isinstance(value, int) and value <= 0:
        return
    wait_value(eng, sem, value, met)


class Chain:

    def __init__(self, eng, sem, per, b):
        self.eng, self.sem, self.per, self.b, self.n = eng, sem, per, b, 0

    def link(self, ins, met=None):
        self.n += 1
        ins.then_inc(self.sem, 1)
        wait_value(self.eng, self.sem, self.per * self.b + self.n, met)

    def end(self):
        assert self.n == self.per, (self.n, self.per)


def rounds(eng, n, first, last, body):
    for b in range(first):
        body(b, b // 2, b % 2)
    with eng.Fori(first // 2, (n - last) // 2) as i:
        body(2 * i, i, 0)
        body(2 * i + 1, i, 1)
    for b in range(n - last, n):
        body(b, b // 2, b % 2)


def sb_of(nc, ctx, prefix):
    return lambda name, shape, dt=F32: ctx.enter_context(nc.sbuf_tensor(f"{prefix}_{name}", shape, dt))


def ps_of(nc, ctx, prefix):
    return lambda name, shape, dt=F32: ctx.enter_context(nc.psum_tensor(f"{prefix}_{name}", shape, dt))


def sem_of(nc, ctx, prefix):
    return lambda name: ctx.enter_context(nc.semaphore(f"{prefix}_{name}"))


def token_phase(nc, x, gamma, beta, tok_w, tok_b, edge_masks, ident, hid, xt):
    ctx = ExitStack()
    with ctx:
        sb, ps, sem = sb_of(nc, ctx, "t"), ps_of(nc, ctx, "t"), sem_of(nc, ctx, "t")
        raw_p = [sb(f"raw_p{u}", [GB * NP, C, IMG]) for u in range(2)]
        raw_d = [sb(f"raw_d{u}", [GB * ND, DPAD + S]) for u in range(2)]
        cols_p = sb("cols_p", [GB * NP, NP, C, PATCH, PATCH])
        cols_d = sb("cols_d", [GB * ND, ND, C, PATCH, PATCH])
        pat = sb("pat", [128, GB, NP, NP])
        dia = sb("dia", [128, GB, ND, ND])
        norm = sb("norm", [128, V, GB, NT])
        gam = sb("gam", [128, V, NT])
        bet = sb("bet", [128, V, NT])
        w = sb("w", [128, V, D])
        bias = sb("bias", [TT, D])
        masks = sb("masks", [128, 2])
        ones = sb("ones", [128, 128])
        half = sb("half", [128, TPG])
        st = sb("st", [128, GB, V, 6])
        mv = sb("mv", [128, GB, 2])
        mm = sb("mm", [128, GB])
        ms = sb("ms", [128, GB, 2])
        var = sb("var", [128, GB])
        rstd = sb("rstd", [128, GB])
        shift = sb("shift", [128, GB])
        tst = sb("tst", [TT, TPG, 6])
        tmv = sb("tmv", [TT, TPG, 2])
        tvar = sb("tvar", [TT, TPG])
        trstd = sb("trstd", [TT, TPG])
        xl = sb("xl", [TT, TPG, D])
        tp = [ps(f"tp{i}", [128, 4, 128]) for i in range(4)]
        stp = ps("stp", [128, 512])
        yp = [ps(f"yp{i}", [128, 512]) for i in range(2)]
        xp = ps("xp", [128, 4, TT])

        s_const = sem("const")
        s_in = [sem("in0"), sem("in1")]
        s_init = sem("init")
        s_cols = sem("cols")
        s_tp = sem("tp")
        s_tpe = sem("tpe")
        s_stat = sem("stat")
        s_statp = sem("statp")
        s_var = sem("var")
        s_rstd = sem("rstd")
        s_shift = sem("shift")
        s_norm = sem("norm")
        s_gam = sem("gam")
        s_bet = sem("bet")
        s_yp = sem("yp")
        s_y = sem("y")
        s_tvar = sem("tvar")
        s_trstd = sem("trstd")
        s_xl = sem("xl")
        s_xp = sem("xp")
        s_xpe = sem("xpe")
        s_dve = sem("dve")
        DVE_LINKS = 6 + 2 * TPG
        FILLS = 8
        XFILLS = 4

        block = ctx.enter_context(nc.Block())

        @block.sync
        def _(sp):
            sp.dma_start(gam[:, :, :], gamma).then_inc(s_const, 16)
            sp.dma_start(bet[:, :, :], beta).then_inc(s_const, 16)
            sp.dma_start(w[:, :, :], tok_w).then_inc(s_const, 16)
            sp.dma_start(bias[:, :], tok_b).then_inc(s_const, 16)
            sp.dma_start(masks[:, :], edge_masks).then_inc(s_const, 16)
            sp.dma_start(ident[0][:, :], ident[1]).then_inc(s_const, 16)

            def load(g, i, u):
                if isinstance(g, int) and g < 2:
                    sp.wait_ge(s_init, 1)
                wait_count(sp, s_cols, 2, g - 2, 2)
                img = x[ds(g * GB, GB)] if not isinstance(g, int) else x[g * GB:(g + 1) * GB]
                for c in range(C):
                    sp.dma_start(raw_p[u][:, c, :], img[:, c].rearrange("b (p i) w -> b p (i w)", i=PATCH))\
                        .then_inc(s_in[u], 16)
                    o = HALF + c * IMG
                    sp.dma_start(raw_d[u][GB:GB * NP, o:o + IMG],
                                 img[:, c, HALF:S - HALF].rearrange("b (p i) w -> p b (i w)", i=PATCH))\
                        .then_inc(s_in[u], 16)
                    o = HALF + c * IMG
                    h = HALF * S
                    sp.dma_start(raw_d[u][0:GB, o + h:o + 2 * h],
                                 img[:, c, 0:HALF].rearrange("b i w -> b (i w)")).then_inc(s_in[u], 16)
                    sp.dma_start(raw_d[u][GB * NP:GB * ND, o:o + h],
                                 img[:, c, S - HALF:S].rearrange("b i w -> b (i w)")).then_inc(s_in[u], 16)

            rounds(sp, NG, 2, 0, load)

        LOADS = 16 * C * 4

        @block.gpsimd
        def _(pool):
            pool.memset(ones[:, :], 1.0 / 128.0)
            pool.memset(half[:, :], -0.5)
            pool.memset(raw_d[0][:, :], 0.0)
            pool.memset(raw_d[1][:, :], 0.0).then_inc(s_init, 1)
            pool.wait_ge(s_const, 96)

            def body(g, i, u):
                wait_value(pool, s_in[u], LOADS * (i + 1), s_const)
                wait_count(pool, s_tp, FILLS, g - 1, 4, met=s_const)
                for c in range(C):
                    ins = pool.tensor_copy(cols_p[:, :, c, :, :],
                                           raw_p[u][:, c, :].rearrange("p (i q j) -> p q i j", i=PATCH, j=PATCH))
                ins.then_inc(s_cols, 1)
                wait_count(pool, s_tp, FILLS, g - 1, FILLS, met=s_const)
                for c in range(C):
                    o = c * IMG
                    pool.tensor_copy(cols_d[:, 0:NP, c, :, :],
                                     raw_d[u][:, o:o + IMG].rearrange("p (i q j) -> p q i j", i=PATCH, j=PATCH))
                    o += S
                    ins = pool.tensor_copy(cols_d[:, NP, c, :, :],
                                           raw_d[u][:, o:o + IMG].rearrange("p (i w) -> p i w", w=S)[:, :, 0:PATCH])
                ins.then_inc(s_cols, 1)
                wait_count(pool, s_var, 1, g, 1)
                pool.tensor_tensor(rstd[:, :], var[:, :], half[:, 0:GB], ALU.pow).then_inc(s_rstd, 1)
                for b in range(GB):
                    wait_count(pool, s_gam, GB, g, b + 1)
                    pool.tensor_tensor(norm[:, :, b, :], norm[:, :, b, :], bet[:, :, :], ALU.add).then_inc(s_bet, 1)
                wait_count(pool, s_tvar, 1, g, 1)
                pool.tensor_tensor(trstd[:, :], tvar[:, :], half[0:TT, :], ALU.pow).then_inc(s_trstd, 1)

            rounds(pool, NG, 2, 0, body)

        def fills():
            for k in range(4):
                yield "p", 4 * k, min(4, NP - 4 * k)
            for k in range(4):
                yield "d", 4 * k, min(4, ND - 4 * k)

        @block.tensor
        def _(pe):
            pe.wait_ge(s_const, 96)
            pe.wait_ge(s_init, 1)

            def body(g, i, u):
                for f, (kind, q0, n) in enumerate(fills()):
                    if f in (0, 4):
                        wait_count(pe, s_cols, 2, g, 1 + f // 4)
                    wait_count(pe, s_tpe, FILLS, g, f - 3)
                    cols, rows = (cols_p, GB * NP) if kind == "p" else (cols_d, GB * ND)
                    for q in range(n):
                        ins = pe.transpose(tp[f % 4][:, q, 0:rows],
                                           cols[:, q0 + q, :, :, :].rearrange("p c i j -> p (c i j)"),
                                           ident[0][0:rows, 0:rows])
                    ins.then_inc(s_tp, 1)
                wait_count(pe, s_stat, 1, g, 1)
                pe.matmul(stp[:, 0:2 * GB], ones[:, :], mv[:, :, :].rearrange("p b k -> p (b k)"),
                          start=True, stop=True).then_inc(s_statp, 1)
                for t in range(TPG):
                    wait_count(pe, s_bet, GB, g, -(-TT * (t + 1) // NT))
                    wait_count(pe, s_y, TPG, g, t - 1)
                    for v in range(V):
                        ins = pe.matmul(yp[t % 2][0:TT, 0:D],
                                        norm[:, v, :, :].rearrange("p b n -> p (b n)")[:, t * TT:(t + 1) * TT],
                                        w[:, v, :], start=v == 0, stop=v == V - 1)
                    ins.then_inc(s_yp, 1)
                for k in range(XFILLS):
                    wait_count(pe, s_xl, XFILLS, g, k + 1)
                    wait_count(pe, s_xpe, XFILLS, g, k)
                    for t in range(4 * k, min(4 * k + 4, TPG)):
                        ins = pe.transpose(xp[:, t - 4 * k, :], xl[:, t, :], ident[0][0:TT, 0:TT])
                    ins.then_inc(s_xp, 1)

            rounds(pe, NG, 2, 0, body)

        @block.scalar
        def _(act):
            act.wait_ge(s_const, 96)

            def body(g, i, u):
                wait_count(act, s_gam, GB, g - 1, GB)
                for f, (kind, q0, n) in enumerate(fills()):
                    wait_count(act, s_tp, FILLS, g, f + 1)
                    src = tp[f % 4]
                    if kind == "p":
                        ins = act.activation(pat[:, :, :, q0:q0 + n].rearrange("p b a q -> p q (b a)"),
                                             src[:, 0:n, 0:GB * NP], ACT.Copy)
                    else:
                        out = dia[:, :, :, :].rearrange("p b a q -> p q a b")
                        src = src[:, :, 0:GB * ND].rearrange("p q (a b) -> p q a b", b=GB)
                        lo, hi = q0, q0 + n
                        if lo == 0:
                            act.activation(out[:, 0], src[:, 0], ACT.Copy, scale=masks[:, 0:1])
                            lo = 1
                        if hi == ND:
                            act.activation(out[:, NP], src[:, NP - q0], ACT.Copy, scale=masks[:, 1:2])
                            hi = NP
                        ins = act.activation(out[:, lo:hi], src[:, lo - q0:hi - q0], ACT.Copy)
                    ins.then_inc(s_tpe, 1)
                wait_count(act, s_shift, 1, g, 1)
                for b in range(GB):
                    for buf in (pat, dia):
                        ins = act.activation(buf[:, b, :, :], buf[:, b, :, :], ACT.Identity,
                                             bias=shift[:, b:b + 1], scale=rstd[:, b:b + 1])
                    ins.then_inc(s_norm, 1)
                for k in range(XFILLS):
                    wait_count(act, s_xp, XFILLS, g, k + 1)
                    n = min(4, TPG - 4 * k)
                    act.activation(xt[:, ds(g * GT + 4 * k * TT, n * TT)].rearrange("p (t n) -> p t n", n=TT),
                                   xp[:, 0:n, :], ACT.Copy).then_inc(s_xpe, 1)

            rounds(act, NG, 2, 0, body)

        @block.vector
        def _(dve):
            dve.wait_ge(s_const, 96)

            def body(g, i, u):
                chain = Chain(dve, s_dve, DVE_LINKS, g)
                wait_count(dve, s_tpe, FILLS, g, FILLS, met=s_const)
                for b in range(GB):
                    dve.bn_stats(st[:, b, 0, :], pat[:, b, :, :].rearrange("p a q -> p (a q)"))
                    for v, (r, c) in enumerate(((1, 0), (1, 1), (0, 0), (0, 1))):
                        ins = dve.bn_stats(st[:, b, v + 1, :], dia[:, b, r:r + NP, c:c + NP])
                chain.link(ins, met=s_const)
                for b in range(GB):
                    ins = dve.bn_aggr(mv[:, b, :], st[:, b, :, :].rearrange("p v k -> p (v k)"))
                chain.link(ins)
                chain.link(dve.tensor_tensor(mm[:, :], mv[:, :, 0], mv[:, :, 0], ALU.mult))
                dve.tensor_tensor(mv[:, :, 1], mv[:, :, 1], mm[:, :], ALU.add).then_inc(s_stat, 1)
                wait_count(dve, s_statp, 1, g, 1)
                chain.link(dve.tensor_copy(ms[:, :, :].rearrange("p b k -> p (b k)"), stp[:, 0:2 * GB]))
                chain.link(dve.tensor_tensor(mm[:, :], ms[:, :, 0], ms[:, :, 0], ALU.mult))
                chain.link(dve.tensor_tensor(mm[:, :], ms[:, :, 1], mm[:, :], ALU.subtract))
                dve.tensor_scalar(var[:, :], mm[:, :], 0.0, 1e-7, ALU.max, ALU.add).then_inc(s_var, 1)
                wait_count(dve, s_rstd, 1, g, 1)
                dve.scalar_tensor_tensor(out=shift[:, :], in0=ms[:, :, 0], scalar=-1.0, in1=rstd[:, :],
                                         op0=ALU.mult, op1=ALU.mult).then_inc(s_shift, 1)
                wait_count(dve, s_yp, TPG, g - 1, TPG)
                for b in range(GB):
                    wait_count(dve, s_norm, GB, g, b + 1)
                    out = norm[:, :, b, :].rearrange("p v (a q) -> p v a q", q=NP)
                    gm = gam[:, :, :].rearrange("p v (a q) -> p v a q", q=NP)
                    dve.tensor_tensor(out[:, 0], pat[:, b, :, :], gm[:, 0], ALU.mult)
                    for v, (r, c) in enumerate(((1, 0), (1, 1), (0, 0), (0, 1))):
                        ins = dve.tensor_tensor(out[:, v + 1], dia[:, b, r:r + NP, c:c + NP], gm[:, v + 1], ALU.mult)
                    ins.then_inc(s_gam, 1)
                for t in range(TPG):
                    wait_count(dve, s_yp, TPG, g, t + 1)
                    row = hid[:, ds(g * TPG + t, 1), :].rearrange("p o d -> p (o d)")
                    ins = dve.tensor_tensor(row, yp[t % 2][0:TT, 0:D], bias[:, :], ALU.add)
                    ins.then_inc(s_y, 1)
                    wait_count(dve, s_y, TPG, g, t + 1, met=s_const)
                    chain.link(dve.bn_stats(tst[:, t, :], row), met=s_const)
                    chain.link(dve.bn_aggr(tmv[:, t, :], tst[:, t, :]))
                dve.tensor_scalar(tvar[:, :], tmv[:, :, 1], 1e-5, None, ALU.add).then_inc(s_tvar, 1)
                wait_count(dve, s_trstd, 1, g, 1)
                for t in range(TPG):
                    wait_count(dve, s_xp, XFILLS, g - 1, t // 4 + 1)
                    row = hid[:, ds(g * TPG + t, 1), :].rearrange("p o d -> p (o d)")
                    ins = dve.tensor_scalar(xl[:, t, :], row, tmv[:, t, 0:1], trstd[:, t:t + 1],
                                            ALU.subtract, ALU.mult)
                    if t % 4 == 3 or t == TPG - 1:
                        ins.then_inc(s_xl, 1)
                chain.end()

            rounds(dve, NG, 2, 0, body)


H = 8
HD = D // H
HP = H // 2
A = 2
KA, KB = 128, NT - 128
KBP = 64
ODD = KA + KBP
TAILS = ((0, 2, 4), (1, 3, 5), (6, 7))
SLOTS = H + len(TAILS)
UNIT = 3
STEPS = -(-SLOTS // UNIT)
FLIPS = -(-SLOTS // 2)
PVS = HP + 1


def slots_of(j):
    return range(UNIT * j, min(UNIT * j + UNIT, SLOTS))


def attention_phase(nc, proj_w, k_bias, head_mask, lam_in, ident, xt):
    ctx = ExitStack()
    with ctx:
        sb, ps, sem = sb_of(nc, ctx, "a"), ps_of(nc, ctx, "a"), sem_of(nc, ctx, "a")
        w = sb("w", [128, 5, D])
        kbias = sb("kbias", [128, A])
        hmask = sb("hmask", [128, H])
        lam4 = sb("lam4", [128, 4, SLOTS])
        lw = sb("lw", [128, 2, SLOTS])
        nlam = sb("nlam", [128, SLOTS])
        xc = [sb(f"xc{u}", [128, KA + KBP]) for u in range(2)]
        qf = [sb(f"qf{u}", [128, A, NT]) for u in range(2)]
        kf = [sb(f"kf{u}", [128, A, KB + NT]) for u in range(2)]
        qm = [sb(f"qm{u}", [128, A, SLOTS, 128]) for u in range(2)]
        nmax = sb("nmax", [128, A, SLOTS])
        rsum = sb("rsum", [128, A, SLOTS])
        rcp = sb("rcp", [128, A, SLOTS])
        prob = sb("prob", [128, STEPS, A, UNIT, NT])
        att = sb("att", [128, FLIPS, ODD + NT])
        flip = sb("flip", [128, FLIPS, 3, 128])
        va = [sb(f"va{u}", [128, HP, 2, 2 * HD]) for u in range(2)]
        vb = [sb(f"vb{u}", [128, HP, 2 * HD]) for u in range(2)]
        vc = [sb(f"vc{u}", [128, 96]) for u in range(2)]
        bx = ps("bx", [128, 512])
        bs = [ps(f"bs{i}", [128, 512]) for i in range(4)]
        bt = [ps(f"bt{i}", [128, 512]) for i in range(2)]
        bo = ps("bo", [128, 512])

        s_const = sem("const")
        s_zero = sem("zero")
        s_lam = sem("lam")
        s_xc = sem("xc")
        s_q, s_qe = sem("q"), sem("qe")
        s_k, s_ke = sem("k"), sem("ke")
        s_kt = sem("kt")
        s_v, s_ve = sem("v"), sem("ve")
        s_qm = sem("qm")
        s_s = sem("s")
        s_mx = sem("mx")
        s_p = sem("p")
        s_comb = sem("comb")
        s_t, s_te = sem("t"), sem("te")
        s_pv = sem("pv")
        s_o = sem("o")
        s_dve = sem("dve")
        UNITS = A * STEPS
        LINKS = 3 * STEPS
        block = ctx.enter_context(nc.Block())

        @block.sync
        def _(sp):
            for dst, src in ((w[:, :, :], proj_w), (kbias[:, :], k_bias), (hmask[:, :], head_mask),
                             (lam4[:, :, :], lam_in)):
                sp.dma_start(dst, src).then_inc(s_const, 16)
        CONST = 16 * 4

        @block.gpsimd
        def _(pool):
            for u in range(2):
                for t in (xc[u][:, NT:], qm[u][:, :, H:, :], va[u][:, :, :, :], vb[u][:, :, :], vc[u][:, :]):
                    pool.memset(t, 0.0)
            ins = pool.memset(att[:, :, :], 0.0)
            ins.then_inc(s_zero, 1)
            pool.wait_ge(s_zero, 1)
            pool.wait_ge(s_const, CONST)

            def fetch(b, u):
                wait_count(pool, s_v, 1, b - 2, 1, met=s_const)
                pool.tensor_copy(xc[u][:, 0:NT], xt[:, ds(b * NT, NT)]).then_inc(s_xc, 1)

            def spread(b, u):
                wait_count(pool, s_qe, 1, b, 1)
                wait_count(pool, s_s, UNITS, b - 2, UNITS)
                for a in range(A):
                    pool.tensor_tensor(qm[u][:, a, 0:H, :], qf[u][:, a, 0:KA].unsqueeze(1).broadcast_to([128, H, KA]),
                                       hmask[:, :].unsqueeze(2).broadcast_to([128, H, KA]), ALU.mult)
                    for i, heads in enumerate(TAILS):
                        n, hs = len(heads), slice(heads[0], heads[-1] + 1, heads[1] - heads[0])
                        ins = pool.tensor_tensor(
                            qm[u][:, a, H + i, 0:n * KB].rearrange("p (h n) -> p h n", n=KB),
                            qf[u][:, a, KA:NT].unsqueeze(1).broadcast_to([128, n, KB]),
                            hmask[:, hs].unsqueeze(2).broadcast_to([128, n, KB]), ALU.mult)
                ins.then_inc(s_qm, 1)

            def wrap(b, u):
                wait_count(pool, s_ke, 1, b, 1, met=s_const)
                pool.tensor_copy(kf[u][:, :, 0:KB], kf[u][:, :, NT:]).then_inc(s_kt, 1)

            def body(b, i, u):
                if not (isinstance(b, int) and b + 2 >= B):
                    fetch(b + 2, u)
                    spread(b + 2, u)
                    wrap(b + 2, u)

            for b in range(2):
                fetch(b, b)
            for b in range(2):
                spread(b, b)
                wrap(b, b)
            rounds(pool, B, 2, 2, body)

        @block.tensor
        def _(pe):
            pe.wait_ge(s_const, CONST)
            pe.wait_ge(s_zero, 1)

            def queries(b, u):
                wait_count(pe, s_xc, 1, b, 1)
                wait_count(pe, s_ve, 1, b - 1, 1)
                for a in range(A):
                    ins = pe.matmul(bx[:, a * NT:(a + 1) * NT], w[:, a, :], xc[u][:, 0:NT], start=True, stop=True)
                ins.then_inc(s_q, 1)

            def keys(b, u):
                wait_count(pe, s_qe, 1, b, 1)
                for a in range(A):
                    ins = pe.matmul(bx[:, a * NT:(a + 1) * NT], w[:, 2 + a, :], xc[u][:, 0:NT], start=True, stop=True)
                ins.then_inc(s_k, 1)

            def values(b, u):
                wait_count(pe, s_ke, 1, b, 1)
                pe.matmul(bx[:, 0:D], xc[u][:, 0:KA], w[:, 4, :], start=True, stop=True)
                pe.matmul(bx[0:KBP, D:2 * D], xc[u][:, KA:], w[:, 4, :], start=True, stop=True)
                pe.matmul(bx[KBP:, D:2 * D], xc[u][:, KA:], w[:, 4, :], start=True, stop=True).then_inc(s_v, 1)

            def score(b, u, j):
                if j == 0:
                    wait_count(pe, s_qm, 1, b, 1)
                    wait_count(pe, s_kt, 1, b, 1)
                for a in range(A):
                    n = A * j + a
                    wait_count(pe, s_p, UNITS, b, n - 3)
                    for s, t in enumerate(slots_of(j)):
                        k0 = 0 if t % 2 else KB
                        ins = pe.matmul(bs[n % 4][:, s * NT:(s + 1) * NT], qm[u][:, a, t, :], kf[u][:, a, k0:k0 + NT],
                                        start=True, stop=True)
                    ins.then_inc(s_s, 1)

            def turn(b, j):
                done = min(SLOTS, UNIT * (j + 1))
                for k in range(FLIPS):
                    if not UNIT * j < min(2 * k + 2, SLOTS) <= done:
                        continue
                    wait_count(pe, s_comb, STEPS, b, j + 1)
                    wait_count(pe, s_te, FLIPS, b, k - 1)
                    for c, col in enumerate((0, KA, ODD + KB)[:3 if 2 * k + 1 < SLOTS else 2]):
                        ins = pe.transpose(bt[k % 2][:, c * 128:(c + 1) * 128], att[:, k, col:col + 128], ident[0][:, :])
                    ins.then_inc(s_t, 1)

            def weigh(b, u, g):
                wait_count(pe, s_te, FLIPS, b, g + 1 if g < HP else FLIPS)
                if g == 0:
                    wait_count(pe, s_ve, 1, b, 1)
                    wait_count(pe, s_o, 1, b - 1, 1)
                if g < HP:
                    out = bo[32 * g:32 * g + 32, 0:KA]
                    for o in range(2):
                        pe.matmul(out, va[u][:, g, o, :], flip[:, g, 2 * o, :], start=o == 0, stop=False)
                    ins = pe.matmul(out, vb[u][:, g, :], flip[:, g, 1, :], start=False, stop=True)
                else:
                    for g in range(HP):
                        out = bo[32 * g:32 * g + 32, KA:NT]
                        for o in range(2):
                            i = next(i for i, heads in enumerate(TAILS) if 2 * g + o in heads)
                            at = KB * TAILS[i].index(2 * g + o)
                            pe.matmul(out, va[u][:, g, o, :], flip[:, HP + i // 2, 2 * (i % 2), at:at + KB],
                                      start=o == 0, stop=False)
                        if g < HP - 1:
                            ins = pe.matmul(out, vb[u][:, g, :], flip[:, HP, 1, KB * g:KB * g + KB], start=False, stop=True)
                        else:
                            for o in range(2):
                                ins = pe.matmul(out, vc[u][:, 32 * o:32 * o + 32], flip[:, HP + 1, 1, KB * o:KB * o + KB],
                                                start=False, stop=o == 1)
                ins.then_inc(s_pv, 1)

            def body(b, i, u):
                left = B if not isinstance(b, int) else B - b
                past = not (isinstance(b, int) and b == 0)
                score(b, u, 2)
                if past:
                    turn(b - 1, 3)
                    weigh(b - 1, 1 - u, 3)
                if left > 1:
                    values(b + 1, 1 - u)
                score(b, u, 3)
                turn(b, 0)
                if past:
                    weigh(b - 1, 1 - u, HP)
                if left > 1:
                    score(b + 1, 1 - u, 0)
                if left > 2:
                    queries(b + 2, u)
                turn(b, 1)
                weigh(b, u, 0)
                if left > 1:
                    score(b + 1, 1 - u, 1)
                if left > 2:
                    keys(b + 2, u)
                turn(b, 2)
                weigh(b, u, 1)
                weigh(b, u, 2)

            queries(0, 0)
            keys(0, 0)
            values(0, 0)
            queries(1, 1)
            keys(1, 1)
            score(0, 0, 0)
            score(0, 0, 1)
            rounds(pe, B, 2, 2, body)
            turn(B - 1, 3)
            weigh(B - 1, 1, 3)
            weigh(B - 1, 1, HP)

        @block.scalar
        def _(act):
            act.wait_ge(s_const, CONST)
            act.wait_ge(s_zero, 1)

            def queries(b, u):
                wait_count(act, s_q, 1, b, 1)
                wait_count(act, s_qm, 1, b - 2, 1)
                act.activation(qf[u][:, :, :], bx[:, 0:A * NT].rearrange("p (a n) -> p a n", a=A), ACT.Copy,
                               scale=HD ** -0.5).then_inc(s_qe, 1)

            def keys(b, u):
                wait_count(act, s_k, 1, b, 1)
                wait_count(act, s_s, UNITS, b - 2, UNITS)
                for a in range(A):
                    ins = act.activation(kf[u][:, a, KB:], bx[:, a * NT:(a + 1) * NT], ACT.Identity,
                                         bias=kbias[:, a:a + 1])
                ins.then_inc(s_ke, 1)

            def values(b, u):
                wait_count(act, s_v, 1, b, 1)
                wait_count(act, s_pv, PVS, b - 2, PVS)
                v = bx[:, 0:2 * D].rearrange("p (t g o d) -> p t g o d", t=2, g=HP, o=2)
                act.activation(va[u][:, :, 0, 0:HD], v[:, 0, :, 0, :], ACT.Copy)
                act.activation(va[u][:, :, 1, HD:], v[:, 0, :, 1, :], ACT.Copy)
                act.activation(vb[u][0:KBP, :, 0:HD], v[0:KBP, 1, :, 0, :], ACT.Copy)
                act.activation(vc[u][0:KBP, :].rearrange("p (o c) -> p o c", o=2)[:, :, 0:HD], v[0:KBP, 1, HP - 1, :, :],
                               ACT.Copy)
                act.activation(vb[u][KBP:, :, HD:], v[KBP:, 1, :, 1, :], ACT.Copy).then_inc(s_ve, 1)

            def exps(b, j):
                wait_count(act, s_comb, STEPS, b - 1, j + 1)
                for a in range(A):
                    n = A * j + a
                    wait_count(act, s_mx, UNITS, b, n + 1)
                    for s, t in enumerate(slots_of(j)):
                        ins = act.activation(prob[:, j, a, s, :], bs[n % 4][:, s * NT:(s + 1) * NT], ACT.Exp,
                                             bias=nmax[:, a, t:t + 1], accum_out=rsum[:, a, t:t + 1])
                    ins.then_inc(s_p, 1)

            def evict(b, ks):
                for k in ks:
                    wait_count(act, s_t, FLIPS, b, k + 1)
                    wait_count(act, s_pv, PVS, b - 1, min(k, HP) + 1)
                    n = 3 * 128 if 2 * k + 1 < SLOTS else 2 * 128
                    act.activation(flip[:, k, :, :].rearrange("p c q -> p (c q)")[:, 0:n], bt[k % 2][:, 0:n], ACT.Copy).then_inc(s_te, 1)

            def body(b, i, u):
                left = B if not isinstance(b, int) else B - b
                exps(b, 1)
                if not (isinstance(b, int) and b == 0):
                    evict(b - 1, (4, 5))
                exps(b, 2)
                evict(b, (0,))
                if left > 1:
                    values(b + 1, 1 - u)
                exps(b, 3)
                if left > 2:
                    queries(b + 2, u)
                evict(b, (1, 2))
                if left > 1:
                    exps(b + 1, 0)
                if left > 2:
                    keys(b + 2, u)
                evict(b, (3,))

            act.wait_ge(s_lam, 1)
            act.activation(lw[:, :, :], lw[:, :, :], ACT.Exp).then_inc(s_lam, 1)
            queries(0, 0)
            keys(0, 0)
            values(0, 0)
            queries(1, 1)
            keys(1, 1)
            exps(0, 0)
            rounds(act, B, 2, 2, body)
            evict(B - 1, (4, 5))

        @block.vector
        def _(dve):
            dve.wait_ge(s_zero, 1)
            dve.wait_ge(s_const, CONST)
            dve.tensor_tensor(lw[:, :, :], lam4[:, 0:2, :], lam4[:, 2:4, :], ALU.mult).then_inc(s_lam, 1)
            dve.wait_ge(s_lam, 2)
            dve.tensor_tensor(nlam[:, :], lw[:, 1, :], lw[:, 0, :], ALU.subtract).then_inc(s_lam, 1)
            dve.wait_ge(s_lam, 3)
            dve.tensor_scalar(nlam[:, :], nlam[:, :], -0.2, None, ALU.add).then_inc(s_lam, 1)
            dve.wait_ge(s_lam, 4)

            def reduce(b, j):
                m = len(slots_of(j))
                for a in range(A):
                    n = A * j + a
                    wait_count(dve, s_s, UNITS, b, n + 1)
                    dve.tensor_reduce(nmax[:, a, UNIT * j:UNIT * j + m],
                                      bs[n % 4][:, 0:m * NT].rearrange("p (s n) -> p s n", n=NT),
                                      AX.X, ALU.max, negate=True).then_inc(s_mx, 1)

            def combine(b, j, chain):
                m = len(slots_of(j))
                cols = slice(UNIT * j, UNIT * j + m)
                wait_count(dve, s_p, UNITS, b, A * (j + 1))
                wait_count(dve, s_t, FLIPS, b - 1, (UNIT * j + m - 1) // 2 + 1)
                chain.link(dve.reciprocal(rcp[:, :, cols], rsum[:, :, cols]))
                chain.link(dve.tensor_tensor(rcp[:, 1, cols], rcp[:, 1, cols], nlam[:, cols], ALU.mult))
                for s, t in enumerate(slots_of(j)):
                    ins = dve.tensor_scalar(prob[:, j, 1, s, :], prob[:, j, 1, s, :], rcp[:, 1, t:t + 1], None, ALU.mult)
                chain.link(ins)
                for s, t in enumerate(slots_of(j)):
                    at = ODD * (t % 2)
                    ins = dve.scalar_tensor_tensor(out=att[:, t // 2, at:at + NT], in0=prob[:, j, 0, s, :], scalar=rcp[:, 0, t:t + 1],
                                                   in1=prob[:, j, 1, s, :], op0=ALU.mult, op1=ALU.add)
                ins.then_inc(s_comb, 1)

            def put(b):
                wait_count(dve, s_pv, PVS, b, PVS)
                dve.tensor_copy(xt[:, ds(b * NT, NT)], bo[:, 0:NT]).then_inc(s_o, 1)

            def body(b, i, u):
                more = not (isinstance(b, int) and b + 1 >= B)
                chain = Chain(dve, s_dve, LINKS, b)
                for j in range(STEPS):
                    combine(b, j, chain)
                    if j + 2 < STEPS:
                        reduce(b, j + 2)
                    elif more:
                        reduce(b + 1, j + 2 - STEPS)
                    if j == 1 and not (isinstance(b, int) and b == 0):
                        put(b - 1)
                chain.end()

            reduce(0, 0)
            reduce(0, 1)
            rounds(dve, B, 2, 2, body)
            put(B - 1)


E = 16
K = 2
F = 256
ROW = D + 1
PT = 128
CAP = TOKENS + PT
MTILES = (K * TOKENS + E * (PT - 1)) // PT
XROWS = E * CAP + PT
NOWHERE = 1 << 20


def routing_phase(nc, gn, group_mean, out_w, out_b, gate_w, iotas, prefix, w1, w2, ident, hid, xt, gates, table,
                  weights, xd):
    ctx = ExitStack()
    with ctx:
        sb, ps, sem = sb_of(nc, ctx, "r"), ps_of(nc, ctx, "r"), sem_of(nc, ctx, "r")
        gnw = sb("gnw", [128, 2])
        gmean = sb("gmean", [128, 128])
        ow = sb("ow", [128, D])
        ob = sb("ob", [TT, D])
        gw = sb("gw", [128, E])
        iota_e = sb("iota_e", [TT, E])
        region = sb("region", [TT, E])
        dest = sb("dest", [TT, TPG, K])
        tile_no = sb("tile_no", [1, MTILES])
        pre = sb("pre", [TT, 2, TT], BF16)
        half = sb("half", [128, TPG])
        pad = sb("pad", [PT, ROW])
        st = sb("st", [128, GB, 6])
        mv = sb("mv", [128, GB, 2])
        mm = sb("mm", [128, GB])
        ms = sb("ms", [128, GB, 2])
        var = sb("var", [128, GB])
        rstd = sb("rstd", [128, GB])
        scale = sb("scale", [128, GB])
        shift = sb("shift", [128, GB])
        xn = [sb(f"xn{u}", [128, GB, NT]) for u in range(2)]
        tst = sb("tst", [TT, TPG, 6])
        tmv = sb("tmv", [TT, TPG, 2])
        tvar = sb("tvar", [TT, TPG])
        trstd = sb("trstd", [TT, TPG])
        rows = [sb(f"rows{u}", [TT, TPG, K, ROW]) for u in range(2)]
        x2t = sb("x2t", [128, TPG, TT])
        logit = sb("logit", [TT, TPG, E])
        top = sb("top", [TT, TPG])
        prob = sb("prob", [TT, TPG, E])
        rsum = sb("rsum", [TT, TPG])
        best = sb("best", [TT, TPG, 8])
        which = sb("which", [TT, TPG, 8], U32)
        whichf = sb("whichf", [TT, TPG, K])
        hot = sb("hot", [TT, TPG, K, E])
        hot16 = sb("hot16", [TT, TPG, E], BF16)
        base = sb("base", [TT, TPG + 1, E])
        pos = sb("pos", [TT, TPG, E])
        picked = sb("picked", [TT, TPG, K, E])
        slotf = sb("slotf", [TT, TPG, K])
        slot = [sb(f"slot{u}", [TT, TPG, K], U32) for u in range(2)]
        cnt = sb("cnt", [1, E], I32)
        ntile = sb("ntile", [1, E])
        cum = [sb(f"cum{i}", [1, E]) for i in range(2)]
        skip = sb("skip", [1, E])
        past = sb("past", [1, MTILES, E])
        tab = sb("tab", [1, MTILES])
        padrow = sb("padrow", [1, E], I32)
        gp = ps("gp", [128, 512])
        cy = [ps(f"cy{i}", [128, 512]) for i in range(2)]
        xp = [ps(f"xp{i}", [128, 4, TT]) for i in range(2)]
        lg = ps("lg", [128, TPG, E])
        pf = ps("pf", [128, 2, TPG * E])

        s_const = sem("const")
        s_init = sem("init")
        s_stat = sem("stat")
        s_statp = sem("statp")
        s_var = sem("var")
        s_rstd = sem("rstd")
        s_shift = sem("shift")
        s_xn = sem("xn")
        s_hb = sem("hb")
        s_cy = sem("cy")
        s_h = sem("h")
        s_ts = sem("ts")
        s_tvar = sem("tvar")
        s_trstd = sem("trstd")
        s_x2 = sem("x2")
        s_x2b = sem("x2b")
        s_xp = sem("xp")
        s_xpe = sem("xpe")
        s_lg = sem("lg")
        s_sub = sem("sub")
        s_exp = sem("exp")
        s_hot = sem("hot")
        s_pf = sem("pf")
        s_slot = sem("slot")
        s_sc = [sem("sc0"), sem("sc1")]
        s_pad = sem("pad")
        s_padw = sem("padw")
        s_proj = sem("proj")
        s_gate = sem("gate")
        s_end = sem("end")
        s_w = sem("w")
        PROJ_LINKS, GATE_LINKS = 11, 13 + TPG
        XF = 4
        block = ctx.enter_context(nc.Block())

        @block.sync
        def _(sp):
            for dst, src in ((gnw[:, :], gn), (gmean[:, :], group_mean), (ow[:, :], out_w), (ob[:, :], out_b),
                             (gw[:, :], gate_w), (iota_e[:, :], iotas[0]), (region[:, :], iotas[1]),
                             (dest[:, :, :], iotas[2]), (tile_no[:, :], iotas[3]), (pre[:, :, :], prefix)):
                sp.dma_start(dst, src).then_inc(s_const, 16)
            sp.dma_start(weights[0][:, :, :], w1).then_inc(s_w, 16)
            sp.dma_start(weights[1][:, :, :, :], w2).then_inc(s_w, 16)
            sp.wait_ge(s_pad, 1)
            for e in range(E):
                row = sp.value_load(padrow[0:1, e:e + 1], min_val=e * CAP, max_val=e * CAP + TOKENS)
                sp.dma_start(xd[ds(row, PT), :], pad[:, :]).then_inc(s_padw, 16)
            sp.dma_start(xd[E * CAP:E * CAP + PT, :], pad[:, :]).then_inc(s_padw, 16)
            sp.wait_ge(s_padw, 16 * (E + 1))
            sp.wait_ge(s_w, 32)
        CONST = 160

        @block.gpsimd
        def _(pool):
            pool.memset(half[:, :], -0.5)
            pool.memset(pad[:, 0:D], 0.0)
            pool.memset(pad[:, D:ROW].bitcast(U32), NOWHERE)
            pool.memset(base[:, :, :], 0.0).then_inc(s_init, 1)
            pool.wait_ge(s_init, 1)
            pool.wait_ge(s_const, CONST)

            def image_power(g):
                wait_count(pool, s_var, 1, g, 1)
                pool.tensor_tensor(rstd[:, :], var[:, :], half[:, 0:GB], ALU.pow).then_inc(s_rstd, 1)

            def token_power(g):
                wait_count(pool, s_tvar, 1, g, 1)
                pool.tensor_tensor(trstd[:, :], tvar[:, :], half[0:TT, :], ALU.pow).then_inc(s_trstd, 1)

            def send(g, u, tiles):
                wait_count(pool, s_slot, 1, g, 1, met=s_const)
                wait_count(pool, s_x2b, XF, g, XF, met=s_const)
                for t in tiles:
                    for k in range(K):
                        pool.indirect_dma_start(xd[:, :], bass.IndirectOffsetOnAxis(ap=slot[u][:, t, k:k + 1], axis=0),
                                                rows[u][:, t, k, :], None).then_inc(s_sc[u], 16)

            def body(g, i, u):
                more = not (isinstance(g, int) and g + 1 >= NG)
                past = not (isinstance(g, int) and g == 0)
                if past:
                    send(g - 1, 1 - u, range(0, 4))
                token_power(g)
                if past:
                    send(g - 1, 1 - u, range(4, 8))
                if more:
                    image_power(g + 1)
                if past:
                    send(g - 1, 1 - u, range(8, TPG))

            image_power(0)
            rounds(pool, NG, 2, 2, body)
            send(NG - 1, 1, range(TPG))
            for u in range(2):
                pool.wait_ge(s_sc[u], 16 * K * TPG * NG // 2)

        @block.tensor
        def _(pe):
            pe.wait_ge(s_const, CONST)

            def stats(g):
                wait_count(pe, s_stat, 1, g, 1)
                pe.matmul(gp[:, 0:2 * GB], gmean[:, :], mv[:, :, :].rearrange("p b k -> p (b k)"),
                          start=True, stop=True).then_inc(s_statp, 1)

            def project(g, u, ks):
                for k in ks:
                    wait_count(pe, s_h, XF, g, k - 1)
                    for t in range(4 * k, min(4 * k + 4, TPG)):
                        wait_count(pe, s_xn, GB, g, -(-TT * (t + 1) // NT))
                        ins = pe.matmul(cy[k % 2][0:TT, (t - 4 * k) * D:(t - 4 * k + 1) * D],
                                        xn[u][:, :, :].rearrange("p b n -> p (b n)")[:, t * TT:(t + 1) * TT],
                                        ow[:, :], start=True, stop=True)
                    ins.then_inc(s_cy, 1)

            def turn(g, u):
                for k in range(XF):
                    wait_count(pe, s_x2, XF, g, k + 1)
                    wait_count(pe, s_xpe, XF, g, k - 1)
                    for t in range(4 * k, min(4 * k + 4, TPG)):
                        ins = pe.transpose(xp[k % 2][:, t - 4 * k, :], rows[u][:, t, 0, 0:D], ident[0][0:TT, 0:TT])
                    ins.then_inc(s_xp, 1)

            def logits(g):
                wait_count(pe, s_sub, 1, g - 1, 1)
                for t in range(TPG):
                    wait_count(pe, s_xpe, XF, g, t // 4 + 1)
                    ins = pe.matmul(lg[0:TT, t, :], x2t[:, t, :], gw[:, :], start=True, stop=True)
                ins.then_inc(s_lg, 1)

            def count(g):
                wait_count(pe, s_hot, 1, g, 1)
                wait_count(pe, s_slot, 1, g - 1, 1)
                for m in range(2):
                    ins = pe.matmul(pf[0:TT, m, :], pre[:, m, :], hot16[:, :, :].rearrange("p t e -> p (t e)"),
                                    start=True, stop=True)
                ins.then_inc(s_pf, 1)

            def body(g, i, u):
                more = not (isinstance(g, int) and g + 1 >= NG)
                turn(g, u)
                logits(g)
                if more:
                    stats(g + 1)
                count(g)
                if more:
                    project(g + 1, 1 - u, range(XF))

            stats(0)
            project(0, 0, range(XF))
            rounds(pe, NG, 2, 2, body)

        @block.scalar
        def _(act):
            act.wait_ge(s_const, CONST)

            def normalise(g, u):
                wait_count(act, s_shift, 1, g, 1)
                wait_count(act, s_cy, XF, g - 2, XF)
                for b in range(GB):
                    act.activation(xn[u][:, b, :], xt[:, ds((g * GB + b) * NT, NT)], ACT.Identity,
                                   bias=shift[:, b:b + 1], scale=scale[:, b:b + 1]).then_inc(s_xn, 1)

            def body(g, i, u):
                wait_count(act, s_lg, 1, g - 1, 1)
                for k in range(XF):
                    n = min(4, TPG - 4 * k)
                    wait_count(act, s_xp, XF, g, k + 1)
                    act.activation(x2t[:, 4 * k:4 * k + n, :], xp[k % 2][:, 0:n, :], ACT.Copy).then_inc(s_xpe, 1)
                wait_count(act, s_sub, 1, g, 1)
                act.activation(prob[:, :, :], logit[:, :, :], ACT.Exp).then_inc(s_exp, 1)
                if not (isinstance(g, int) and g + 1 >= NG):
                    normalise(g + 1, 1 - u)
                for k in range(XF):
                    n = min(4, TPG - 4 * k)
                    act.activation(rows[u][:, 4 * k:4 * k + n, 1, 0:D], rows[u][:, 4 * k:4 * k + n, 0, 0:D], ACT.Copy)\
                        .then_inc(s_x2b, 1)

            normalise(0, 0)
            rounds(act, NG, 2, 2, body)

        @block.vector
        def _(dve):
            dve.wait_ge(s_const, CONST)
            dve.wait_ge(s_init, 1)

            def image_stats(g, link):
                wait_count(dve, s_statp, 1, g - 1, 1, met=s_const)
                for b in range(GB):
                    ins = dve.bn_stats(st[:, b, :], xt[:, ds((g * GB + b) * NT, NT)])
                link(ins, met=s_const)
                for b in range(GB):
                    ins = dve.bn_aggr(mv[:, b, :], st[:, b, :])
                link(ins)
                link(dve.tensor_tensor(mm[:, :], mv[:, :, 0], mv[:, :, 0], ALU.mult))
                dve.tensor_tensor(mv[:, :, 1], mv[:, :, 1], mm[:, :], ALU.add).then_inc(s_stat, 1)

            def image_var(g, link):
                wait_count(dve, s_statp, 1, g, 1)
                link(dve.tensor_copy(ms[:, :, :].rearrange("p b k -> p (b k)"), gp[:, 0:2 * GB]))
                link(dve.tensor_tensor(mm[:, :], ms[:, :, 0], ms[:, :, 0], ALU.mult))
                link(dve.tensor_tensor(mm[:, :], ms[:, :, 1], mm[:, :], ALU.subtract))
                dve.tensor_scalar(var[:, :], mm[:, :], 0.0, 1e-5, ALU.max, ALU.add).then_inc(s_var, 1)

            def image_affine(g, link):
                wait_count(dve, s_rstd, 1, g, 1)
                wait_count(dve, s_xn, GB, g - 1, GB)
                link(dve.tensor_scalar(scale[:, :], rstd[:, :], gnw[:, 0:1], None, ALU.mult))
                link(dve.tensor_tensor(mm[:, :], ms[:, :, 0], scale[:, :], ALU.mult))
                dve.tensor_scalar(shift[:, :], mm[:, :], -1.0, gnw[:, 1:2], ALU.mult, ALU.add).then_inc(s_shift, 1)

            def residual(g, link):
                tiles = hid[:, ds(g * TPG, TPG), :]
                dve.tensor_tensor(tiles, tiles, ob[:, :].unsqueeze(1).broadcast_to([TT, TPG, D]), ALU.add)\
                    .then_inc(s_hb, 1)
                wait_count(dve, s_hb, 1, g, 1)
                for k in range(XF + 2):
                    if k < XF:
                        n = min(4, TPG - 4 * k)
                        wait_count(dve, s_cy, XF, g, k + 1)
                        tiles = hid[:, ds(g * TPG + 4 * k, n), :]
                        dve.tensor_tensor(tiles, cy[k % 2][0:TT, 0:n * D].rearrange("p (t d) -> p t d", d=D), tiles,
                                          ALU.add).then_inc(s_h, 1)
                    if 0 < k <= XF:
                        wait_count(dve, s_h, XF, g, k, met=s_const)
                        for t in range(4 * (k - 1), min(4 * k, TPG)):
                            row = hid[:, ds(g * TPG + t, 1), :].rearrange("p o d -> p (o d)")
                            ins = dve.bn_stats(tst[:, t, :], row)
                        ins.then_inc(s_ts, 1)
                    if 1 < k:
                        wait_count(dve, s_ts, XF, g, k - 1, met=s_const)
                        for t in range(4 * (k - 2), min(4 * (k - 1), TPG)):
                            ins = dve.bn_aggr(tmv[:, t, :], tst[:, t, :])
                link(ins)
                dve.tensor_scalar(tvar[:, :], tmv[:, :, 1], 1e-5, None, ALU.add).then_inc(s_tvar, 1)

            def normalise(g, i, u, link):
                wait_count(dve, s_trstd, 1, g, 1)
                if isinstance(g, int):
                    if g >= 2:
                        dve.wait_ge(s_sc[u], 16 * K * TPG * (g // 2))
                else:
                    dve.wait_ge(s_sc[u], i * (16 * K * TPG))
                for t in range(TPG):
                    row = hid[:, ds(g * TPG + t, 1), :].rearrange("p o d -> p (o d)")
                    ins = dve.tensor_scalar(rows[u][:, t, 0, 0:D], row, tmv[:, t, 0:1], trstd[:, t:t + 1],
                                            ALU.subtract, ALU.mult)
                    if t % 4 == 3 or t == TPG - 1:
                        ins.then_inc(s_x2, 1)
                link(dve.tensor_copy(rows[u][:, :, :, D].bitcast(U32), dest[:, :, :]))
                link(dve.tensor_scalar(dest[:, :, :], dest[:, :, :], float(K * GT), None, ALU.add), met=s_const)

            def less_top(g, link):
                wait_count(dve, s_lg, 1, g, 1)
                wait_count(dve, s_exp, 1, g - 1, 1)
                link(dve.tensor_reduce(top[:, :], lg[0:TT, :, :], AX.X, ALU.max))
                dve.tensor_tensor(logit[:, :, :], lg[0:TT, :, :], top[:, :].unsqueeze(2).broadcast_to([TT, TPG, E]),
                                  ALU.subtract).then_inc(s_sub, 1)

            def best_two(g, link):
                wait_count(dve, s_exp, 1, g, 1)
                link(dve.tensor_reduce(rsum[:, :], prob[:, :, :], AX.X, ALU.add))
                link(dve.reciprocal(rsum[:, :], rsum[:, :]))
                link(dve.tensor_tensor(prob[:, :, :], prob[:, :, :], rsum[:, :].unsqueeze(2).broadcast_to([TT, TPG, E]),
                                       ALU.mult), met=s_const)
                for t in range(TPG):
                    ins = dve.max(best[:, t, :], prob[:, t, :])
                link(ins, met=s_const)
                for t in range(TPG):
                    ins = dve.max_index(which[:, t, :], best[:, t, :], prob[:, t, :])
                link(ins)
                dve.tensor_copy(gates[:, ds(g * TPG, TPG), :], best[:, :, 0:K])
                link(dve.tensor_copy(whichf[:, :, :], which[:, :, 0:K]))
                link(dve.tensor_tensor(hot[:, :, :, :],
                                       iota_e[:, :].unsqueeze(1).unsqueeze(1).broadcast_to([TT, TPG, K, E]),
                                       whichf[:, :, :].unsqueeze(3).broadcast_to([TT, TPG, K, E]), ALU.is_equal))
                dve.tensor_tensor(hot16[:, :, :], hot[:, :, 0, :], hot[:, :, 1, :], ALU.add).then_inc(s_hot, 1)

            def places(g, u, link):
                link(dve.tensor_copy(base[:, 0, :], base[:, TPG, :]))
                wait_count(dve, s_pf, 1, g, 1)
                tot = pf[0:TT, 1, :].rearrange("p (t e) -> p t e", e=E)
                for t in range(TPG):
                    link(dve.tensor_tensor(base[:, t + 1, :], tot[:, t, :], base[:, t, :], ALU.add))
                link(dve.tensor_tensor(pos[:, :, :], pf[0:TT, 0, :].rearrange("p (t e) -> p t e", e=E),
                                       base[:, 0:TPG, :], ALU.add))
                link(dve.tensor_tensor(pos[:, :, :], pos[:, :, :], region[:, :].unsqueeze(1).broadcast_to([TT, TPG, E]),
                                       ALU.add))
                link(dve.tensor_tensor(picked[:, :, :, :], hot[:, :, :, :],
                                       pos[:, :, :].unsqueeze(2).broadcast_to([TT, TPG, K, E]), ALU.mult))
                link(dve.tensor_reduce(slotf[:, :, :], picked[:, :, :, :], AX.X, ALU.add))
                dve.tensor_copy(slot[u][:, :, :], slotf[:, :, :]).then_inc(s_slot, 1)

            def body(g, i, u):
                more = not (isinstance(g, int) and g + 1 >= NG)
                proj, gate = Chain(dve, s_proj, PROJ_LINKS, g + 1), Chain(dve, s_gate, GATE_LINKS, g)
                if more:
                    image_stats(g + 1, proj.link)
                less_top(g, gate.link)
                if more:
                    image_var(g + 1, proj.link)
                best_two(g, gate.link)
                if more:
                    image_affine(g + 1, proj.link)
                places(g, u, gate.link)
                gate.end()
                if more:
                    residual(g + 1, proj.link)
                    normalise(g + 1, i + u, 1 - u, proj.link)
                    proj.end()

            proj = Chain(dve, s_proj, PROJ_LINKS, 0)
            image_stats(0, proj.link)
            image_var(0, proj.link)
            image_affine(0, proj.link)
            residual(0, proj.link)
            normalise(0, 0, 0, proj.link)
            proj.end()
            rounds(dve, NG, 2, 2, body)

            n = [0]

            def link(ins):
                n[0] += 1
                ins.then_inc(s_end, 1)
                dve.wait_ge(s_end, n[0])

            count = base[0:1, TPG, :]
            link(dve.tensor_copy(cnt[:, :], count))
            dve.tensor_tensor(padrow[:, :], count, region[0:1, :], ALU.add).then_inc(s_pad, 1)
            link(dve.tensor_scalar(skip[:, :], count, float(PT - 1), None, ALU.add))
            link(dve.tensor_copy(cnt[:, :], skip[:, :]))
            link(dve.tensor_single_scalar(cnt[:, :], cnt[:, :], PT.bit_length() - 1, ALU.logical_shift_right))
            link(dve.tensor_copy(ntile[:, :], cnt[:, :]))
            link(dve.tensor_copy(cum[0][:, :], ntile[:, :]))
            for k, s in enumerate((1, 2, 4, 8)):
                a, b = cum[k % 2], cum[1 - k % 2]
                link(dve.tensor_copy(b[:, :], a[:, :]))
                link(dve.tensor_tensor(b[:, s:], a[:, s:], a[:, :E - s], ALU.add))
            link(dve.tensor_scalar(skip[:, :], ntile[:, :], -float(PT), float(CAP), ALU.mult, ALU.add))
            link(dve.tensor_tensor(past[:, :, :], tile_no[:, :].unsqueeze(2).broadcast_to([1, MTILES, E]),
                                   cum[0][:, :].unsqueeze(1).broadcast_to([1, MTILES, E]), ALU.is_ge))
            link(dve.tensor_reduce(tab[:, :], past[:, :, :], AX.X, ALU.add))
            link(dve.tensor_scalar(table[0:1, 1, :], tab[:, :], float(E - 1), None, ALU.min))
            link(dve.tensor_tensor(past[:, :, :], past[:, :, :], skip[:, :].unsqueeze(1).broadcast_to([1, MTILES, E]),
                                   ALU.mult))
            link(dve.tensor_reduce(tab[:, :], past[:, :, :], AX.X, ALU.add))
            link(dve.scalar_tensor_tensor(out=tab[:, :], in0=tile_no[:, :], scalar=float(PT), in1=tab[:, :],
                                          op0=ALU.mult, op1=ALU.add))
            link(dve.tensor_scalar(table[0:1, 0, :], tab[:, :], float(E * CAP), None, ALU.min))


def expert_phase(nc, weights, ident, table, xd, yd):
    w1s, w2s = weights
    ctx = ExitStack()
    with ctx:
        sb, ps, sem = sb_of(nc, ctx, "e"), ps_of(nc, ctx, "e"), sem_of(nc, ctx, "e")
        R = 8
        YR = 4
        w1c = [sb(f"w1c{u}", [128, F]) for u in range(2)]
        xin = [sb(f"xin{u}", [PT, ROW]) for u in range(R)]
        xts = [sb(f"xts{u}", [128, PT]) for u in range(2)]
        act1 = [sb(f"act{u}", [128, 2, PT]) for u in range(2)]
        ys = [sb(f"ys{u}", [PT, D]) for u in range(YR)]
        tp = [ps(f"tp{u}", [128, 512]) for u in range(2)]
        hp = [ps(f"hp{u}", [128, 512]) for u in range(2)]
        yp = [ps(f"yp{u}", [128, 512]) for u in range(2)]
        s_go = sem("go")
        go = sb("go", [128, 1])
        s_in = [sem(f"in{u}") for u in range(R)]
        s_wc = sem("wc")
        s_tp = sem("tp")
        s_xt = sem("xt")
        s_hp = sem("hp")
        s_act = sem("act")
        s_yp = sem("yp")
        s_ys = sem("ys")
        s_out = [sem(f"out{u}") for u in range(R)]
        block = ctx.enter_context(nc.Block())

        def tiles(eng, body):
            for t in range(R):
                body(t, 0, t)
            with eng.Fori(1, MTILES // R - 1) as i:
                for u in range(R):
                    body(i * R + u, i, u)
            for t in range(MTILES - R, MTILES):
                body(t, t // R, t % R)

        def ahead(t, i, u, n):
            if isinstance(t, int) and t + n >= MTILES:
                return None
            return t + n, i + (u + n) // R, (u + n) % R

        @block.sync
        def _(sp):
            def load(t, i, u):
                row = sp.value_load(table[0:1, 0, ds(t, 1)], min_val=0, max_val=E * CAP)
                if not (isinstance(t, int) and t < R):
                    sp.wait_ge(s_out[u], i * 16)
                sp.dma_start(xin[u][:, :], xd[ds(row, PT), :]).then_inc(s_in[u], 16)

            tiles(sp, load)

        @block.tensor
        def _(pe):
            def flip(t, i, u):
                pe.wait_ge(s_in[u], i * 16 + 16)
                wait_count(pe, s_xt, 1, t, -1)
                pe.transpose(tp[u % 2][:, 0:PT], xin[u][:, 0:D], ident[0][:, :]).then_inc(s_tp, 1)

            def up(t, i, u):
                v = u % 2
                wait_count(pe, s_wc, 1, t, 1)
                wait_count(pe, s_xt, 1, t, 1)
                wait_count(pe, s_act, 1, t, -1)
                for f in range(2):
                    ins = pe.matmul(hp[v][:, f * PT:(f + 1) * PT], w1c[v][:, f * 128:(f + 1) * 128], xts[v][:, :],
                                    start=True, stop=True)
                ins.then_inc(s_hp, 1)

            def down(t, i, u):
                v = u % 2
                e = pe.value_load(table[0:1, 1, ds(t, 1)], min_val=0, max_val=E - 1)
                wait_count(pe, s_act, 1, t, 1)
                wait_count(pe, s_ys, 1, t, -1)
                for f in range(2):
                    ins = pe.matmul(yp[v][:, 0:D], act1[v][:, f, :],
                                    w2s[:, ds(e, 1), f, :].rearrange("p o d -> p (o d)"), start=f == 0, stop=f == 1)
                ins.then_inc(s_yp, 1)

            def body(t, i, u):
                if nxt := ahead(t, i, u, 2):
                    flip(*nxt)
                if nxt := ahead(t, i, u, 1):
                    up(*nxt)
                down(t, i, u)

            flip(0, 0, 0)
            flip(1, 0, 1)
            up(0, 0, 0)
            tiles(pe, body)

        @block.scalar
        def _(act):
            def evict(t, i, u):
                wait_count(act, s_tp, 1, t, 1)
                wait_count(act, s_hp, 1, t, -1)
                act.activation(xts[u % 2][:, :], tp[u % 2][:, 0:PT], ACT.Copy).then_inc(s_xt, 1)

            def gelu(t, i, u):
                wait_count(act, s_hp, 1, t, 1)
                wait_count(act, s_yp, 1, t, -1)
                act.activation(act1[u % 2][:, :, :].rearrange("p f n -> p (f n)"), hp[u % 2][:, 0:2 * PT], ACT.Gelu)\
                    .then_inc(s_act, 1)

            def body(t, i, u):
                if nxt := ahead(t, i, u, 2):
                    evict(*nxt)
                if nxt := ahead(t, i, u, 1):
                    gelu(*nxt)

            evict(0, 0, 0)
            evict(1, 0, 1)
            gelu(0, 0, 0)
            tiles(act, body)

        @block.vector
        def _(dve):
            def stage(t, i, u):
                e = dve.value_load(table[0:1, 1, ds(t, 1)], min_val=0, max_val=E - 1)
                wait_count(dve, s_hp, 1, t, -1)
                dve.tensor_copy(w1c[u % 2][:, :], w1s[:, ds(e, 1), :].rearrange("p o f -> p (o f)")).then_inc(s_wc, 1)

            def body(t, i, u):
                if nxt := ahead(t, i, u, 2):
                    stage(*nxt)
                wait_count(dve, s_yp, 1, t, 1)
                if not (isinstance(t, int) and t < YR):
                    dve.wait_ge(s_out[(u + YR) % R], (i + (u >= YR)) * 16)
                dve.tensor_copy(ys[u % YR][:, :], yp[u % 2][:, 0:D]).then_inc(s_ys, 1)

            stage(0, 0, 0)
            stage(1, 0, 1)
            tiles(dve, body)

        @block.gpsimd
        def _(pool):
            pool.memset(go[:, :], 0.0).then_inc(s_go, 1)

            def send(t, i, u):
                pool.wait_ge(s_in[u], i * 16 + 16)
                wait_count(pool, s_ys, 1, t, 1, met=s_go)
                pool.indirect_dma_start(yd[:, :], bass.IndirectOffsetOnAxis(ap=xin[u][:, D:ROW].bitcast(U32), axis=0),
                                        ys[u % YR][:, :], None, bounds_check=K * TOKENS - 1, oob_is_err=False)\
                    .then_inc(s_out[u], 16)

            tiles(pool, send)
            for u in range(R):
                pool.wait_ge(s_out[u], 16 * MTILES // R)


def combine_phase(nc, hid, gates, yd, out):
    ctx = ExitStack()
    with ctx:
        sb, sem = sb_of(nc, ctx, "c"), sem_of(nc, ctx, "c")
        N = 4
        yin = [sb(f"yin{u}", [TT, N, K * D]) for u in range(2)]
        res = [sb(f"res{u}", [TT, N, D]) for u in range(2)]
        s_in = [sem("in0"), sem("in1")]
        s_one = sem("one")
        s_two = sem("two")
        s_out = [sem("out0"), sem("out1")]
        yv = yd.rearrange("(t p k) d -> p t (k d)", p=TT, k=K)
        ov = out.rearrange("b n d -> (b n) d").rearrange("(t p) d -> p t d", p=TT)
        block = ctx.enter_context(nc.Block())
        ROUNDS = NTILES // N

        @block.sync
        def _(sp):
            def load(r, i, u):
                wait_count(sp, s_two, N, r - 2, N)
                sp.dma_start(yin[u][:, :, :], yv[:, ds(r * N, N), :]).then_inc(s_in[u], 16)

            rounds(sp, ROUNDS, 2, 0, load)

        @block.vector
        def _(dve):
            def body(r, i, u):
                dve.wait_ge(s_in[u], i * 16 + 16)
                if isinstance(r, int):
                    if i > 0:
                        dve.wait_ge(s_out[u], 16 * i)
                else:
                    dve.wait_ge(s_out[u], i * 16)
                for k, s in ((0, s_one), (1, s_two)):
                    for t in range(N):
                        row = hid[:, ds(r * N + t, 1), :] if k == 0 else res[u][:, t:t + 1, :]
                        if k:
                            wait_count(dve, s_one, N, r, t + 1)
                        dve.scalar_tensor_tensor(
                            out=res[u][:, t, :], in0=yin[u][:, t, k * D:(k + 1) * D],
                            scalar=gates[:, ds(r * N + t, 1), k], in1=row.rearrange("p o d -> p (o d)"),
                            op0=ALU.mult, op1=ALU.add).then_inc(s, 1)

            rounds(dve, ROUNDS, 2, 0, body)

        @block.scalar
        def _(act):
            def store(r, i, u):
                wait_count(act, s_two, N, r, N)
                act.dma_start(ov[:, ds(r * N, N), :], res[u][:, :, :]).then_inc(s_out[u], 16)

            rounds(act, ROUNDS, 2, 0, store)
            for u in range(2):
                act.wait_ge(s_out[u], 16 * ROUNDS // 2)


def vit_tower_kernel(nc, x, gamma, beta, tok_w, tok_b, edge_masks, ident_in, proj_w, k_bias, head_mask, lam, gn, group_mean, out_w, out_b, gate_w, iota_e, region, dest, tile_no, prefix,
                     w1, w2, out):
    xd = nc.dram_tensor("routed_rows", [XROWS, ROW], F32, kind="Internal").ap()
    yd = nc.dram_tensor("expert_rows", [K * TOKENS, D], F32, kind="Internal").ap()
    ctx = ExitStack()
    with ctx:
        sb = sb_of(nc, ctx, "k")
        hid = sb("hid", [TT, NTILES, D])
        ident = (sb("ident", [128, 128]), ident_in)
        gates = sb("gates", [TT, NTILES, K])
        table = sb("table", [1, 2, MTILES], I32)
        xt = sb("xt", [128, TOKENS])
        token_phase(nc, x, gamma, beta, tok_w, tok_b, edge_masks, ident, hid, xt)
        attention_phase(nc, proj_w, k_bias, head_mask, lam, ident, xt)
        weights = (sb("w1s", [128, E, F]), sb("w2s", [128, E, 2, D]))
        routing_phase(nc, gn, group_mean, out_w, out_b, gate_w, (iota_e, region, dest, tile_no), prefix,
                      w1, w2, ident, hid, xt, gates, table, weights, xd)
        expert_phase(nc, weights, ident, table, xd, yd)
        combine_phase(nc, hid, gates, yd, out)


def kernel(**inputs):
    import ml_dtypes as _ml
    import numpy as _np
    import concourse.bacc as _bacc
    from concourse import mybir as _mybir
    from concourse.bass_utils import run_bass_kernel_spmd as _run

    a = {n: _np.asarray(v) for n, v in inputs.items()}

    def pixels(m):
        return m.reshape(V, C, NP, PATCH, NP, PATCH).transpose(1, 3, 5, 0, 2, 4).reshape(128, V, NT)

    part = _np.arange(128)
    heads = (part[:, None] // HD == _np.arange(H)[None]).astype(_np.float32)
    head = _np.zeros((128, SLOTS), int)
    head[:, :H] = _np.arange(H)
    for i, hs in enumerate(TAILS):
        for j, h in enumerate(hs):
            head[KB * j:KB * (j + 1), H + i] = h
    tok = _np.arange(TT)
    laid = {
        "x": a["x"],
        "gamma": pixels(a["L0_tok_gamma"]),
        "beta": pixels(a["L0_tok_beta"]),
        "tok_w": a["L0_tok_W"].reshape(D, V, 128).transpose(2, 1, 0),
        "tok_b": _np.broadcast_to(a["L0_tok_b"], (TT, D)),
        "edge_masks": _np.stack([part % PATCH >= HALF, part % PATCH < HALF], 1).astype(_np.float32),
        "ident_in": _np.eye(128, dtype=_np.float32),
        "proj_w": _np.stack([a[f"L0_attn_{n}_w"].T for n in ("Q1", "Q2", "K1", "K2", "V")], 1),
        "k_bias": _np.stack([a["L0_attn_K1_b"], a["L0_attn_K2_b"]], 1),
        "head_mask": heads,
        "lam": _np.stack([a[f"L0_attn_lambda_{n}"][:, 0][head] for n in ("q1", "q2", "k1", "k2")], 1),
        "gn": _np.stack([a["L0_attn_gn_w"], a["L0_attn_gn_b"]], 1),
        "group_mean": ((part[:, None] // 32 == part[None] // 32) / 32).astype(_np.float32),
        "out_w": a["L0_attn_out_w"].T,
        "out_b": _np.broadcast_to(a["L0_attn_out_b"], (TT, D)),
        "gate_w": a["L0_ffn_W_gate"],
        "iota_e": _np.broadcast_to(_np.arange(E, dtype=_np.float32), (TT, E)),
        "region": _np.broadcast_to(_np.arange(E, dtype=_np.float32) * CAP, (TT, E)),
        "dest": (K * (_np.arange(TPG)[None, :, None] * TT + tok[:, None, None]) + _np.arange(K)).astype(_np.float32),
        "tile_no": _np.arange(MTILES, dtype=_np.float32)[None],
        "prefix": _np.stack([tok[:, None] < tok[None], _np.ones((TT, TT), bool)], 1).astype(_ml.bfloat16),
        "w1": a["L0_ffn_W1"].transpose(1, 0, 2),
        "w2": a["L0_ffn_W2"].reshape(E, 2, 128, D).transpose(2, 0, 1, 3),
    }
    nc = _bacc.Bacc("TRN2", target_bir_lowering=False, num_devices=1)
    arrays, args = {}, {}
    for name, v in laid.items():
        v = _np.ascontiguousarray(v)
        arrays[f"in_{name}_dram"] = v
        args[name] = nc.dram_tensor(f"in_{name}_dram", v.shape, _mybir.dt.from_np(v.dtype), kind="ExternalInput").ap()
    args["out"] = nc.dram_tensor("out_0_dram", (B, NT, D), _mybir.dt.float32, kind="ExternalOutput").ap()
    vit_tower_kernel(nc, **args)
    r = _run(nc, [arrays], core_ids=[0])
    return r.results[0]["out_0_dram"]
```

```python
import concourse.bass as bass
from concourse import mybir
from concourse.bass import ds
from contextlib import ExitStack

F32 = mybir.dt.float32
BF16 = mybir.dt.bfloat16
U32 = mybir.dt.uint32
I32 = mybir.dt.int32
ALU = mybir.AluOpType
ACT = mybir.ActivationFunctionType
AX = mybir.AxisListType

B, C, S = 64, 2, 104
PATCH, HALF = 8, 4
NP = S // PATCH
NT = NP * NP
ND = NP + 1
V = 5
D = 128
GB = 8
NG = B // GB
GT = GB * NT
TT = 104
TPG = GT // TT
NTILES = NG * TPG
TOKENS = B * NT
IMG = PATCH * S
DPAD = IMG + S + IMG + HALF


def wait_value(eng, sem, value, met):
    if met is not None and not isinstance(value, int):
        value = eng.snap(eng.to_reg(value))
        eng.wait_ge(met, 1)
    eng.wait_ge(sem, value)


def wait_count(eng, sem, per, b, n, met=None):
    value = per * b + n
    if isinstance(value, int) and value <= 0:
        return
    wait_value(eng, sem, value, met)


class Chain:

    def __init__(self, eng, sem, per, b):
        self.eng, self.sem, self.per, self.b, self.n = eng, sem, per, b, 0

    def link(self, ins, met=None):
        self.n += 1
        ins.then_inc(self.sem, 1)
        wait_value(self.eng, self.sem, self.per * self.b + self.n, met)

    def end(self):
        assert self.n == self.per, (self.n, self.per)


def rounds(eng, n, first, last, body):
    for b in range(first):
        body(b, b // 2, b % 2)
    with eng.Fori(first // 2, (n - last) // 2) as i:
        body(2 * i, i, 0)
        body(2 * i + 1, i, 1)
    for b in range(n - last, n):
        body(b, b // 2, b % 2)


def sb_of(nc, ctx, prefix):
    return lambda name, shape, dt=F32: ctx.enter_context(nc.sbuf_tensor(f"{prefix}_{name}", shape, dt))


def ps_of(nc, ctx, prefix):
    return lambda name, shape, dt=F32: ctx.enter_context(nc.psum_tensor(f"{prefix}_{name}", shape, dt))


def sem_of(nc, ctx, prefix):
    return lambda name: ctx.enter_context(nc.semaphore(f"{prefix}_{name}"))


def token_phase(nc, x, gamma, beta, tok_w, tok_b, edge_masks, ident, hid, xt):
    ctx = ExitStack()
    with ctx:
        sb, ps, sem = sb_of(nc, ctx, "t"), ps_of(nc, ctx, "t"), sem_of(nc, ctx, "t")
        raw_p = [sb(f"raw_p{u}", [GB * NP, C, IMG]) for u in range(2)]
        raw_d = [sb(f"raw_d{u}", [GB * ND, DPAD + S]) for u in range(2)]
        cols_p = sb("cols_p", [GB * NP, NP, C, PATCH, PATCH])
        cols_d = sb("cols_d", [GB * ND, ND, C, PATCH, PATCH])
        pat = [sb(f"pat{u}", [128, GB, NP, NP]) for u in range(2)]
        dia = [sb(f"dia{u}", [128, GB, ND, ND]) for u in range(2)]
        norm = sb("norm", [128, V, GB, NT])
        gam = sb("gam", [128, V, NT])
        bet = xt[:, 0:V * NT].rearrange("p (v n) -> p v n", v=V)
        w = sb("w", [128, V, D])
        bias = sb("bias", [TT, D])
        bias13 = sb("bias13", [TT, TPG, D])
        masks = sb("masks", [128, 2])
        ones = sb("ones", [128, 128])
        half = sb("half", [128, TPG])
        st = sb("st", [128, GB, V, 6])
        mv = sb("mv", [128, GB, 2])
        mm = sb("mm", [128, GB])
        ms = sb("ms", [128, GB, 2])
        var = sb("var", [128, GB])
        rstd = sb("rstd", [128, GB])
        shift = sb("shift", [128, GB])
        tst = sb("tst", [TT, TPG, 6])
        tmv = sb("tmv", [TT, TPG, 2])
        tvar = sb("tvar", [TT, TPG])
        trstd = sb("trstd", [TT, TPG])
        tshift = sb("tshift", [TT, TPG])
        xl = [sb(f"xl{u}", [TT, 4, D]) for u in range(2)]
        tp = [ps(f"tp{i}", [128, 4, 128]) for i in range(4)]
        stp = ps("stp", [128, 512])
        yp = [ps(f"yp{i}", [128, 512]) for i in range(2)]
        xp = ps("xp", [128, 4, TT])

        s_const = sem("const")
        s_in = [sem("in0"), sem("in1")]
        s_init = sem("init")
        s_cols = sem("cols")
        s_tp = sem("tp")
        s_tpe = sem("tpe")
        s_stat = sem("stat")
        s_statp = sem("statp")
        s_var = sem("var")
        s_rstd = sem("rstd")
        s_shift = sem("shift")
        s_norm = sem("norm")
        s_gam = sem("gam")
        s_gamp = sem("gamp")
        s_bet = sem("bet")
        s_rep = sem("rep")
        s_bt = sem("bt")
        s_bias = sem("bias")
        s_yp = sem("yp")
        s_y = sem("y")
        s_tvar = sem("tvar")
        s_trstd = sem("trstd")
        s_tshift = sem("tshift")
        s_xl = sem("xl")
        s_xp = sem("xp")
        s_xpe = sem("xpe")
        s_ts = sem("ts")
        s_tmv = sem("tmv")
        s_pix = sem("pix")
        FILLS = 8
        XFILLS = 4
        PIX_LINKS = 6
        GD = 7
        GP = GB - GD

        def gamma_of(eng, u, b):
            out = norm[:, :, b, :].rearrange("p v (a q) -> p v a q", q=NP)
            gm = gam[:, :, :].rearrange("p v (a q) -> p v a q", q=NP)
            eng.tensor_tensor(out[:, 0], pat[u][:, b, :, :], gm[:, 0], ALU.mult)
            for v, (r, c) in enumerate(((1, 0), (1, 1), (0, 0), (0, 1))):
                ins = eng.tensor_tensor(out[:, v + 1], dia[u][:, b, r:r + NP, c:c + NP], gm[:, v + 1], ALU.mult)
            return ins

        block = ctx.enter_context(nc.Block())

        @block.sync
        def _(sp):
            sp.dma_start(gam[:, :, :], gamma).then_inc(s_const, 16)
            sp.dma_start(bet[:, :, :], beta).then_inc(s_const, 16)
            sp.dma_start(w[:, :, :], tok_w).then_inc(s_const, 16)
            sp.dma_start(bias[:, :], tok_b).then_inc(s_const, 16)
            sp.dma_start(masks[:, :], edge_masks).then_inc(s_const, 16)
            sp.dma_start(ident[0][:, :], ident[1]).then_inc(s_const, 16)

            def load(g, i, u):
                if isinstance(g, int) and g < 2:
                    sp.wait_ge(s_init, 1)
                wait_count(sp, s_cols, 2, g - 2, 2)
                img = x[ds(g * GB, GB)] if not isinstance(g, int) else x[g * GB:(g + 1) * GB]
                for c in range(C):
                    sp.dma_start(raw_p[u][:, c, :], img[:, c].rearrange("b (p i) w -> b p (i w)", i=PATCH))\
                        .then_inc(s_in[u], 16)
                    o = HALF + c * IMG
                    sp.dma_start(raw_d[u][GB:GB * NP, o:o + IMG],
                                 img[:, c, HALF:S - HALF].rearrange("b (p i) w -> p b (i w)", i=PATCH))\
                        .then_inc(s_in[u], 16)
                    o = HALF + c * IMG
                    h = HALF * S
                    sp.dma_start(raw_d[u][0:GB, o + h:o + 2 * h],
                                 img[:, c, 0:HALF].rearrange("b i w -> b (i w)")).then_inc(s_in[u], 16)
                    sp.dma_start(raw_d[u][GB * NP:GB * ND, o:o + h],
                                 img[:, c, S - HALF:S].rearrange("b i w -> b (i w)")).then_inc(s_in[u], 16)

            rounds(sp, NG, 2, 0, load)

        LOADS = 16 * C * 4

        @block.gpsimd
        def _(pool):
            pool.memset(ones[:, :], 1.0 / 128.0)
            pool.memset(half[:, :], -0.5)
            pool.memset(raw_d[0][:, :], 0.0)
            pool.memset(raw_d[1][:, :], 0.0).then_inc(s_init, 1)
            pool.wait_ge(s_const, 96)

            def order(g, i, u):
                wait_value(pool, s_in[u], LOADS * (i + 1), s_const)
                wait_count(pool, s_tp, FILLS, g - 1, 4, met=s_const)
                for c in range(C):
                    ins = pool.tensor_copy(cols_p[:, :, c, :, :],
                                           raw_p[u][:, c, :].rearrange("p (i q j) -> p q i j", i=PATCH, j=PATCH))
                ins.then_inc(s_cols, 1)
                wait_count(pool, s_tp, FILLS, g - 1, FILLS, met=s_const)
                for c in range(C):
                    o = c * IMG
                    pool.tensor_copy(cols_d[:, 0:NP, c, :, :],
                                     raw_d[u][:, o:o + IMG].rearrange("p (i q j) -> p q i j", i=PATCH, j=PATCH))
                    o += S
                    ins = pool.tensor_copy(cols_d[:, NP, c, :, :],
                                           raw_d[u][:, o:o + IMG].rearrange("p (i w) -> p i w", w=S)[:, :, 0:PATCH])
                ins.then_inc(s_cols, 1)

            def image_power(g):
                wait_count(pool, s_var, 1, g, 1)
                wait_count(pool, s_norm, GB, g - 1, GB)
                pool.tensor_tensor(rstd[:, :], var[:, :], half[:, 0:GB], ALU.pow).then_inc(s_rstd, 1)

            def token_power(g):
                wait_count(pool, s_tvar, 1, g, 1)
                wait_count(pool, s_xl, XFILLS, g - 1, XFILLS)
                pool.tensor_tensor(trstd[:, :], tvar[:, :], half[0:TT, :], ALU.pow).then_inc(s_trstd, 1)

            def times_gamma(g, u):
                wait_count(pool, s_yp, XFILLS, g - 1, XFILLS)
                wait_count(pool, s_norm, GB, g, GB)
                for b in range(GD, GB):
                    gamma_of(pool, u, b).then_inc(s_gamp, 1)

            def body(g, i, u):
                left = NG if not isinstance(g, int) else NG - g
                times_gamma(g, u)
                if left > 2:
                    order(g + 2, i + 1, u)
                if left > 1:
                    image_power(g + 1)
                token_power(g)

            order(0, 0, 0)
            order(1, 0, 1)
            image_power(0)
            rounds(pool, NG, 2, 2, body)

        def fills():
            for k in range(4):
                yield "p", 4 * k, min(4, NP - 4 * k)
            for k in range(4):
                yield "d", 4 * k, min(4, ND - 4 * k)

        @block.tensor
        def _(pe):
            pe.wait_ge(s_const, 96)
            pe.wait_ge(s_init, 1)

            def turn(g):
                for f, (kind, q0, n) in enumerate(fills()):
                    if f in (0, 4):
                        wait_count(pe, s_cols, 2, g, 1 + f // 4)
                    wait_count(pe, s_tpe, FILLS, g, f - 3)
                    cols, rows = (cols_p, GB * NP) if kind == "p" else (cols_d, GB * ND)
                    for q in range(n):
                        ins = pe.transpose(tp[f % 4][:, q, 0:rows],
                                           cols[:, q0 + q, :, :, :].rearrange("p c i j -> p (c i j)"),
                                           ident[0][0:rows, 0:rows])
                    ins.then_inc(s_tp, 1)

            def stats(g):
                wait_count(pe, s_stat, 1, g, 1)
                pe.matmul(stp[:, 0:2 * GB], ones[:, :], mv[:, :, :].rearrange("p b k -> p (b k)"),
                          start=True, stop=True).then_inc(s_statp, 1)

            def embed(g, k):
                wait_count(pe, s_y, XFILLS, g, k - 1)
                for t in range(4 * k, min(4 * k + 4, TPG)):
                    images = -(-TT * (t + 1) // NT)
                    wait_count(pe, s_gam, GD, g, min(images, GD))
                    if images > GD:
                        wait_count(pe, s_gamp, GP, g, images - GD)
                    for v in range(V):
                        ins = pe.matmul(yp[k % 2][0:TT, (t - 4 * k) * D:(t - 4 * k + 1) * D],
                                        norm[:, v, :, :].rearrange("p b n -> p (b n)")[:, t * TT:(t + 1) * TT],
                                        w[:, v, :], start=v == 0, stop=v == V - 1)
                ins.then_inc(s_yp, 1)

            def turn_normed(g, k):
                wait_count(pe, s_xl, XFILLS, g, k + 1)
                wait_count(pe, s_xpe, XFILLS, g, k)
                for t in range(4 * k, min(4 * k + 4, TPG)):
                    ins = pe.transpose(xp[:, t - 4 * k, :], xl[k % 2][:, t - 4 * k, :], ident[0][0:TT, 0:TT])
                ins.then_inc(s_xp, 1)

            def body(g, i, u):
                left = NG if not isinstance(g, int) else NG - g
                past = not (isinstance(g, int) and g == 0)
                for k in range(XFILLS - 1):
                    embed(g, k)
                    if past:
                        turn_normed(g - 1, k)
                if past:
                    turn_normed(g - 1, XFILLS - 1)
                if left > 2:
                    turn(g + 2)
                embed(g, XFILLS - 1)
                if left > 1:
                    stats(g + 1)

            for v in range(V):
                ins = pe.matmul(yp[0][:, 0:NT], w[:, v, :], bet[:, v, :], start=v == 0, stop=v == V - 1)
            ins.then_inc(s_bet, 1)
            pe.wait_ge(s_rep, 1)
            for t in range(TPG):
                ins = pe.transpose(tp[t // 4][0:TT, t % 4, :],
                                   norm[:, 0, :, :].rearrange("p b n -> p (b n)")[:, t * TT:(t + 1) * TT],
                                   ident[0][:, :])
            ins.then_inc(s_bt, 1)
            pe.wait_ge(s_bias, 1)
            turn(0)
            turn(1)
            stats(0)
            rounds(pe, NG, 2, 2, body)
            for k in range(XFILLS):
                turn_normed(NG - 1, k)

        @block.scalar
        def _(act):
            act.wait_ge(s_const, 96)

            def evict(g, u):
                wait_count(act, s_gam, GD, g - 2, GD)
                wait_count(act, s_gamp, GP, g - 2, GP)
                for f, (kind, q0, n) in enumerate(fills()):
                    wait_count(act, s_tp, FILLS, g, f + 1)
                    src = tp[f % 4]
                    if kind == "p":
                        ins = act.activation(pat[u][:, :, :, q0:q0 + n].rearrange("p b a q -> p q (b a)"),
                                             src[:, 0:n, 0:GB * NP], ACT.Copy)
                    else:
                        out = dia[u][:, :, :, :].rearrange("p b a q -> p q a b")
                        src = src[:, :, 0:GB * ND].rearrange("p q (a b) -> p q a b", b=GB)
                        lo, hi = q0, q0 + n
                        if lo == 0:
                            act.activation(out[:, 0], src[:, 0], ACT.Copy, scale=masks[:, 0:1])
                            lo = 1
                        if hi == ND:
                            act.activation(out[:, NP], src[:, NP - q0], ACT.Copy, scale=masks[:, 1:2])
                            hi = NP
                        ins = act.activation(out[:, lo:hi], src[:, lo - q0:hi - q0], ACT.Copy)
                    ins.then_inc(s_tpe, 1)

            def normalise(g, u):
                wait_count(act, s_shift, 1, g, 1)
                for b in range(GB):
                    for buf in (pat[u], dia[u]):
                        ins = act.activation(buf[:, b, :, :], buf[:, b, :, :], ACT.Identity,
                                             bias=shift[:, b:b + 1], scale=rstd[:, b:b + 1])
                    ins.then_inc(s_norm, 1)

            def normalise_tokens(g):
                wait_count(act, s_tshift, 1, g, 1)
                for k in range(XFILLS + 1):
                    if k < XFILLS:
                        for t in range(4 * k, min(4 * k + 4, TPG)):
                            ins = act.activation(xl[k % 2][:, t - 4 * k, :],
                                                 hid[:, ds(g * TPG + t, 1), :].rearrange("p o d -> p (o d)"),
                                                 ACT.Identity, bias=tshift[:, t:t + 1], scale=trstd[:, t:t + 1])
                        ins.then_inc(s_xl, 1)
                    if k > 0:
                        wait_count(act, s_xp, XFILLS, g, k)
                        t0, n = 4 * (k - 1), min(4, TPG - 4 * (k - 1))
                        act.activation(xt[:, ds(g * GT + t0 * TT, n * TT)].rearrange("p (t n) -> p t n", n=TT),
                                       xp[:, 0:n, :], ACT.Copy).then_inc(s_xpe, 1)

            def body(g, i, u):
                left = NG if not isinstance(g, int) else NG - g
                if not (isinstance(g, int) and g == 0):
                    normalise_tokens(g - 1)
                if left > 2:
                    evict(g + 2, u)
                if left > 1:
                    normalise(g + 1, 1 - u)

            evict(0, 0)
            evict(1, 1)
            normalise(0, 0)
            rounds(act, NG, 2, 2, body)
            normalise_tokens(NG - 1)

        @block.vector
        def _(dve):
            dve.wait_ge(s_const, 96)

            def pixel_stats(g, u, images):
                wait_count(dve, s_tpe, FILLS, g, FILLS, met=s_const)
                for b in images:
                    dve.bn_stats(st[:, b, 0, :], pat[u][:, b, :, :].rearrange("p a q -> p (a q)"))
                    for v, (r, c) in enumerate(((1, 0), (1, 1), (0, 0), (0, 1))):
                        ins = dve.bn_stats(st[:, b, v + 1, :], dia[u][:, b, r:r + NP, c:c + NP])
                return ins

            def pixel_sums(ins, link):
                link(ins, met=s_const)
                for b in range(GB):
                    ins = dve.bn_aggr(mv[:, b, :], st[:, b, :, :].rearrange("p v k -> p (v k)"))
                link(ins)
                link(dve.tensor_tensor(mm[:, :], mv[:, :, 0], mv[:, :, 0], ALU.mult))
                dve.tensor_tensor(mv[:, :, 1], mv[:, :, 1], mm[:, :], ALU.add).then_inc(s_stat, 1)

            def pixel_var(g, link):
                wait_count(dve, s_statp, 1, g, 1)
                link(dve.tensor_copy(ms[:, :, :].rearrange("p b k -> p (b k)"), stp[:, 0:2 * GB]))
                link(dve.tensor_tensor(mm[:, :], ms[:, :, 0], ms[:, :, 0], ALU.mult))
                link(dve.tensor_tensor(mm[:, :], ms[:, :, 1], mm[:, :], ALU.subtract))
                dve.tensor_scalar(var[:, :], mm[:, :], 0.0, 1e-7, ALU.max, ALU.add).then_inc(s_var, 1)

            def pixel_shift(g):
                wait_count(dve, s_rstd, 1, g, 1)
                dve.scalar_tensor_tensor(out=shift[:, :], in0=ms[:, :, 0], scalar=-1.0, in1=rstd[:, :],
                                         op0=ALU.mult, op1=ALU.mult).then_inc(s_shift, 1)

            def times_gamma(g, u, images):
                wait_count(dve, s_yp, XFILLS, g - 1, XFILLS)
                for b in images:
                    wait_count(dve, s_norm, GB, g, b + 1)
                    gamma_of(dve, u, b).then_inc(s_gam, 1)

            def put(g, k):
                if k < XFILLS:
                    n = min(4, TPG - 4 * k)
                    wait_count(dve, s_yp, XFILLS, g, k + 1)
                    dve.tensor_tensor(hid[:, ds(g * TPG + 4 * k, n), :],
                                      yp[k % 2][0:TT, 0:n * D].rearrange("p (t d) -> p t d", d=D),
                                      bias13[:, 4 * k:4 * k + n, :], ALU.add).then_inc(s_y, 1)
                if 0 < k <= XFILLS:
                    wait_count(dve, s_y, XFILLS, g, k, met=s_const)
                    for t in range(4 * (k - 1), min(4 * k, TPG)):
                        row = hid[:, ds(g * TPG + t, 1), :].rearrange("p o d -> p (o d)")
                        ins = dve.bn_stats(tst[:, t, :], row)
                    ins.then_inc(s_ts, 1)
                if 1 < k:
                    wait_count(dve, s_ts, XFILLS, g, k - 1, met=s_const)
                    for t in range(4 * (k - 2), min(4 * (k - 1), TPG)):
                        ins = dve.bn_aggr(tmv[:, t, :], tst[:, t, :])
                if k == XFILLS + 1:
                    ins.then_inc(s_tmv, 1)
                    wait_count(dve, s_tmv, 1, g, 1)
                    dve.tensor_scalar(tvar[:, :], tmv[:, :, 1], 1e-5, None, ALU.add).then_inc(s_tvar, 1)

            def token_shift(g):
                wait_count(dve, s_trstd, 1, g, 1)
                dve.scalar_tensor_tensor(out=tshift[:, :], in0=tmv[:, :, 0], scalar=-1.0, in1=trstd[:, :],
                                         op0=ALU.mult, op1=ALU.mult).then_inc(s_tshift, 1)

            def body(g, i, u):
                more = not (isinstance(g, int) and g + 1 >= NG)
                pix = Chain(dve, s_pix, PIX_LINKS, g + 1)
                times_gamma(g, u, range(2))
                if not (isinstance(g, int) and g == 0):
                    token_shift(g - 1)
                times_gamma(g, u, range(2, GD))
                put(g, 0)
                if more:
                    pixel_stats(g + 1, 1 - u, range(GB // 2))
                put(g, 1)
                if more:
                    pixel_sums(pixel_stats(g + 1, 1 - u, range(GB // 2, GB)), pix.link)
                put(g, 2)
                if more:
                    pixel_var(g + 1, pix.link)
                    pix.end()
                put(g, 3)
                put(g, 4)
                if more:
                    pixel_shift(g + 1)
                put(g, 5)

            dve.wait_ge(s_bet, 1)
            dve.tensor_copy(norm[:, 0, :, :], yp[0][:, 0:NT].unsqueeze(1).broadcast_to([128, GB, NT])).then_inc(s_rep, 1)
            dve.wait_ge(s_bt, 1)
            for k in range(XFILLS):
                n = min(4, TPG - 4 * k)
                ins = dve.tensor_tensor(bias13[:, 4 * k:4 * k + n, :], tp[k][0:TT, 0:n, :],
                                        bias[:, :].unsqueeze(1).broadcast_to([TT, n, D]), ALU.add)
            ins.then_inc(s_bias, 1)
            dve.wait_ge(s_bias, 1)
            pix = Chain(dve, s_pix, PIX_LINKS, 0)
            pixel_sums(pixel_stats(0, 0, range(GB)), pix.link)
            pixel_var(0, pix.link)
            pixel_shift(0)
            rounds(dve, NG, 2, 2, body)
            token_shift(NG - 1)


H = 8
HD = D // H
HP = H // 2
A = 2
KA, KB = 128, NT - 128
KBP = 64
ODD = KA + KBP
TAILS = ((0, 2, 4), (1, 3, 5), (6, 7))
SLOTS = H + len(TAILS)
UNIT = 3
STEPS = -(-SLOTS // UNIT)
FLIPS = -(-SLOTS // 2)
PVS = HP + 1


def slots_of(j):
    return range(UNIT * j, min(UNIT * j + UNIT, SLOTS))


def attention_phase(nc, proj_w, k_bias, head_mask, lam_in, ident, xt):
    ctx = ExitStack()
    with ctx:
        sb, ps, sem = sb_of(nc, ctx, "a"), ps_of(nc, ctx, "a"), sem_of(nc, ctx, "a")
        w = sb("w", [128, 5, D])
        kbias = sb("kbias", [128, A])
        hmask = sb("hmask", [128, H])
        lam4 = sb("lam4", [128, 4, SLOTS])
        lw = sb("lw", [128, 2, SLOTS])
        nlam = sb("nlam", [128, SLOTS])
        xc = [sb(f"xc{u}", [128, KA + KBP]) for u in range(2)]
        qf = [sb(f"qf{u}", [128, A, NT]) for u in range(2)]
        kf = [sb(f"kf{u}", [128, A, KB + NT]) for u in range(2)]
        qm = [sb(f"qm{u}", [128, A, SLOTS, 128]) for u in range(2)]
        nmax = sb("nmax", [128, A, SLOTS])
        rsum = sb("rsum", [128, A, SLOTS])
        rcp = sb("rcp", [128, A, SLOTS])
        prob = sb("prob", [128, STEPS, A, UNIT, NT])
        att = sb("att", [128, FLIPS, ODD + NT])
        flip = sb("flip", [128, FLIPS, 3, 128])
        va = [sb(f"va{u}", [128, HP, 2, 2 * HD]) for u in range(2)]
        vb = [sb(f"vb{u}", [128, HP, 2 * HD]) for u in range(2)]
        vc = [sb(f"vc{u}", [128, 96]) for u in range(2)]
        bx = ps("bx", [128, 512])
        bs = [ps(f"bs{i}", [128, 512]) for i in range(4)]
        bt = [ps(f"bt{i}", [128, 512]) for i in range(2)]
        bo = ps("bo", [128, 512])

        s_const = sem("const")
        s_zero = sem("zero")
        s_lam = sem("lam")
        s_xc = sem("xc")
        s_q, s_qe = sem("q"), sem("qe")
        s_k, s_ke = sem("k"), sem("ke")
        s_kt = sem("kt")
        s_v, s_ve = sem("v"), sem("ve")
        s_qm = sem("qm")
        s_s = sem("s")
        s_mx = sem("mx")
        s_p = sem("p")
        s_rcp = sem("rcp")
        s_fac = sem("fac")
        s_sc = sem("sc")
        s_comb = sem("comb")
        s_t, s_te = sem("t"), sem("te")
        s_pv = sem("pv")
        s_o = sem("o")
        UNITS = A * STEPS
        block = ctx.enter_context(nc.Block())

        @block.sync
        def _(sp):
            for dst, src in ((w[:, :, :], proj_w), (kbias[:, :], k_bias), (hmask[:, :], head_mask),
                             (lam4[:, :, :], lam_in)):
                sp.dma_start(dst, src).then_inc(s_const, 16)
        CONST = 16 * 4

        @block.gpsimd
        def _(pool):
            for u in range(2):
                for t in (xc[u][:, NT:], qm[u][:, :, H:, :], va[u][:, :, :, :], vb[u][:, :, :], vc[u][:, :]):
                    pool.memset(t, 0.0)
            ins = pool.memset(att[:, :, :], 0.0)
            ins.then_inc(s_zero, 1)
            pool.wait_ge(s_zero, 1)
            pool.wait_ge(s_const, CONST)

            def fetch(b, u):
                wait_count(pool, s_v, 1, b - 2, 1, met=s_const)
                pool.tensor_copy(xc[u][:, 0:NT], xt[:, ds(b * NT, NT)]).then_inc(s_xc, 1)

            def spread(b, u):
                wait_count(pool, s_qe, 1, b, 1)
                wait_count(pool, s_s, UNITS, b - 2, UNITS)
                for a in range(A):
                    pool.tensor_tensor(qm[u][:, a, 0:H, :], qf[u][:, a, 0:KA].unsqueeze(1).broadcast_to([128, H, KA]),
                                       hmask[:, :].unsqueeze(2).broadcast_to([128, H, KA]), ALU.mult)
                    for i, heads in enumerate(TAILS):
                        n, hs = len(heads), slice(heads[0], heads[-1] + 1, heads[1] - heads[0])
                        ins = pool.tensor_tensor(
                            qm[u][:, a, H + i, 0:n * KB].rearrange("p (h n) -> p h n", n=KB),
                            qf[u][:, a, KA:NT].unsqueeze(1).broadcast_to([128, n, KB]),
                            hmask[:, hs].unsqueeze(2).broadcast_to([128, n, KB]), ALU.mult)
                ins.then_inc(s_qm, 1)

            def wrap(b, u):
                wait_count(pool, s_ke, 1, b, 1, met=s_const)
                pool.tensor_copy(kf[u][:, :, 0:KB], kf[u][:, :, NT:]).then_inc(s_kt, 1)

            def body(b, i, u):
                if not (isinstance(b, int) and b + 2 >= B):
                    fetch(b + 2, u)
                    spread(b + 2, u)
                    wrap(b + 2, u)

            for b in range(2):
                fetch(b, b)
            for b in range(2):
                spread(b, b)
                wrap(b, b)
            rounds(pool, B, 2, 2, body)

        @block.tensor
        def _(pe):
            pe.wait_ge(s_const, CONST)
            pe.wait_ge(s_zero, 1)

            def queries(b, u):
                wait_count(pe, s_xc, 1, b, 1)
                wait_count(pe, s_ve, 1, b - 1, 1)
                for a in range(A):
                    ins = pe.matmul(bx[:, a * NT:(a + 1) * NT], w[:, a, :], xc[u][:, 0:NT], start=True, stop=True)
                ins.then_inc(s_q, 1)

            def keys(b, u):
                wait_count(pe, s_qe, 1, b, 1)
                for a in range(A):
                    ins = pe.matmul(bx[:, a * NT:(a + 1) * NT], w[:, 2 + a, :], xc[u][:, 0:NT], start=True, stop=True)
                ins.then_inc(s_k, 1)

            def values(b, u):
                wait_count(pe, s_ke, 1, b, 1)
                pe.matmul(bx[:, 0:D], xc[u][:, 0:KA], w[:, 4, :], start=True, stop=True)
                pe.matmul(bx[0:KBP, D:2 * D], xc[u][:, KA:], w[:, 4, :], start=True, stop=True)
                pe.matmul(bx[KBP:, D:2 * D], xc[u][:, KA:], w[:, 4, :], start=True, stop=True).then_inc(s_v, 1)

            def score(b, u, j):
                if j == 0:
                    wait_count(pe, s_qm, 1, b, 1)
                    wait_count(pe, s_kt, 1, b, 1)
                for a in range(A):
                    n = A * j + a
                    wait_count(pe, s_p, UNITS, b, n - 3)
                    for s, t in enumerate(slots_of(j)):
                        k0 = 0 if t % 2 else KB
                        ins = pe.matmul(bs[n % 4][:, s * NT:(s + 1) * NT], qm[u][:, a, t, :], kf[u][:, a, k0:k0 + NT],
                                        start=True, stop=True)
                    ins.then_inc(s_s, 1)

            def turn(b, j):
                done = min(SLOTS, UNIT * (j + 1))
                for k in range(FLIPS):
                    if not UNIT * j < min(2 * k + 2, SLOTS) <= done:
                        continue
                    wait_count(pe, s_comb, STEPS, b, j + 1)
                    wait_count(pe, s_te, FLIPS, b, k - 1)
                    for c, col in enumerate((0, KA, ODD + KB)[:3 if 2 * k + 1 < SLOTS else 2]):
                        ins = pe.transpose(bt[k % 2][:, c * 128:(c + 1) * 128], att[:, k, col:col + 128], ident[0][:, :])
                    ins.then_inc(s_t, 1)

            def weigh(b, u, g):
                wait_count(pe, s_te, FLIPS, b, g + 1 if g < HP else FLIPS)
                if g == 0:
                    wait_count(pe, s_ve, 1, b, 1)
                    wait_count(pe, s_o, 1, b - 1, 1)
                if g < HP:
                    out = bo[32 * g:32 * g + 32, 0:KA]
                    for o in range(2):
                        pe.matmul(out, va[u][:, g, o, :], flip[:, g, 2 * o, :], start=o == 0, stop=False)
                    ins = pe.matmul(out, vb[u][:, g, :], flip[:, g, 1, :], start=False, stop=True)
                else:
                    for g in range(HP):
                        out = bo[32 * g:32 * g + 32, KA:NT]
                        for o in range(2):
                            i = next(i for i, heads in enumerate(TAILS) if 2 * g + o in heads)
                            at = KB * TAILS[i].index(2 * g + o)
                            pe.matmul(out, va[u][:, g, o, :], flip[:, HP + i // 2, 2 * (i % 2), at:at + KB],
                                      start=o == 0, stop=False)
                        if g < HP - 1:
                            ins = pe.matmul(out, vb[u][:, g, :], flip[:, HP, 1, KB * g:KB * g + KB],
                                            start=False, stop=True)
                        else:
                            for o in range(2):
                                ins = pe.matmul(out, vc[u][:, 32 * o:32 * o + 32], flip[:, HP + 1, 1, KB * o:KB * o + KB],
                                                start=False, stop=o == 1)
                ins.then_inc(s_pv, 1)

            def body(b, i, u):
                left = B if not isinstance(b, int) else B - b
                past = not (isinstance(b, int) and b == 0)
                score(b, u, 2)
                if past:
                    turn(b - 1, 3)
                    weigh(b - 1, 1 - u, 3)
                if left > 1:
                    values(b + 1, 1 - u)
                score(b, u, 3)
                turn(b, 0)
                if past:
                    weigh(b - 1, 1 - u, HP)
                if left > 1:
                    score(b + 1, 1 - u, 0)
                if left > 2:
                    queries(b + 2, u)
                turn(b, 1)
                weigh(b, u, 0)
                if left > 1:
                    score(b + 1, 1 - u, 1)
                if left > 2:
                    keys(b + 2, u)
                turn(b, 2)
                weigh(b, u, 1)
                weigh(b, u, 2)

            queries(0, 0)
            keys(0, 0)
            values(0, 0)
            queries(1, 1)
            keys(1, 1)
            score(0, 0, 0)
            score(0, 0, 1)
            rounds(pe, B, 2, 2, body)
            turn(B - 1, 3)
            weigh(B - 1, 1, 3)
            weigh(B - 1, 1, HP)

        @block.scalar
        def _(act):
            act.wait_ge(s_const, CONST)
            act.wait_ge(s_zero, 1)

            def queries(b, u):
                wait_count(act, s_q, 1, b, 1)
                wait_count(act, s_qm, 1, b - 2, 1)
                act.activation(qf[u][:, :, :], bx[:, 0:A * NT].rearrange("p (a n) -> p a n", a=A), ACT.Copy,
                               scale=HD ** -0.5).then_inc(s_qe, 1)

            def keys(b, u):
                wait_count(act, s_k, 1, b, 1)
                wait_count(act, s_s, UNITS, b - 2, UNITS)
                for a in range(A):
                    ins = act.activation(kf[u][:, a, KB:], bx[:, a * NT:(a + 1) * NT], ACT.Identity,
                                         bias=kbias[:, a:a + 1])
                ins.then_inc(s_ke, 1)

            def values(b, u):
                wait_count(act, s_v, 1, b, 1)
                wait_count(act, s_pv, PVS, b - 2, PVS)
                v = bx[:, 0:2 * D].rearrange("p (t g o d) -> p t g o d", t=2, g=HP, o=2)
                act.activation(va[u][:, :, 0, 0:HD], v[:, 0, :, 0, :], ACT.Copy)
                act.activation(va[u][:, :, 1, HD:], v[:, 0, :, 1, :], ACT.Copy)
                act.activation(vb[u][0:KBP, :, 0:HD], v[0:KBP, 1, :, 0, :], ACT.Copy)
                act.activation(vc[u][0:KBP, :].rearrange("p (o c) -> p o c", o=2)[:, :, 0:HD], v[0:KBP, 1, HP - 1, :, :],
                               ACT.Copy)
                act.activation(vb[u][KBP:, :, HD:], v[KBP:, 1, :, 1, :], ACT.Copy).then_inc(s_ve, 1)

            def exps(b, j):
                wait_count(act, s_comb, STEPS, b - 1, j + 1)
                for a in range(A):
                    n = A * j + a
                    wait_count(act, s_mx, UNITS, b, n + 1)
                    for s, t in enumerate(slots_of(j)):
                        ins = act.activation(prob[:, j, a, s, :], bs[n % 4][:, s * NT:(s + 1) * NT], ACT.Exp,
                                             bias=nmax[:, a, t:t + 1], accum_out=rsum[:, a, t:t + 1])
                    ins.then_inc(s_p, 1)

            def evict(b, ks):
                for k in ks:
                    wait_count(act, s_t, FLIPS, b, k + 1)
                    wait_count(act, s_pv, PVS, b - 1, min(k, HP) + 1)
                    n = 3 * 128 if 2 * k + 1 < SLOTS else 2 * 128
                    act.activation(flip[:, k, :, :].rearrange("p c q -> p (c q)")[:, 0:n], bt[k % 2][:, 0:n], ACT.Copy)\
                        .then_inc(s_te, 1)

            def body(b, i, u):
                left = B if not isinstance(b, int) else B - b
                exps(b, 1)
                if not (isinstance(b, int) and b == 0):
                    evict(b - 1, (4, 5))
                exps(b, 2)
                evict(b, (0,))
                if left > 1:
                    values(b + 1, 1 - u)
                exps(b, 3)
                if left > 2:
                    queries(b + 2, u)
                evict(b, (1, 2))
                if left > 1:
                    exps(b + 1, 0)
                if left > 2:
                    keys(b + 2, u)
                evict(b, (3,))

            act.wait_ge(s_lam, 1)
            act.activation(lw[:, :, :], lw[:, :, :], ACT.Exp).then_inc(s_lam, 1)
            queries(0, 0)
            keys(0, 0)
            values(0, 0)
            queries(1, 1)
            keys(1, 1)
            exps(0, 0)
            rounds(act, B, 2, 2, body)
            evict(B - 1, (4, 5))

        @block.vector
        def _(dve):
            dve.wait_ge(s_zero, 1)
            dve.wait_ge(s_const, CONST)
            dve.tensor_tensor(lw[:, :, :], lam4[:, 0:2, :], lam4[:, 2:4, :], ALU.mult).then_inc(s_lam, 1)
            dve.wait_ge(s_lam, 2)
            dve.tensor_tensor(nlam[:, :], lw[:, 1, :], lw[:, 0, :], ALU.subtract).then_inc(s_lam, 1)
            dve.wait_ge(s_lam, 3)
            dve.tensor_scalar(nlam[:, :], nlam[:, :], -0.2, None, ALU.add).then_inc(s_lam, 1)
            dve.wait_ge(s_lam, 4)

            def reduce(b, j, a):
                m, n = len(slots_of(j)), A * j + a
                wait_count(dve, s_s, UNITS, b, n + 1)
                dve.tensor_reduce(nmax[:, a, UNIT * j:UNIT * j + m],
                                  bs[n % 4][:, 0:m * NT].rearrange("p (s n) -> p s n", n=NT),
                                  AX.X, ALU.max, negate=True).then_inc(s_mx, 1)

            def invert(b, j):
                wait_count(dve, s_p, UNITS, b, A * (j + 1))
                cols = slice(UNIT * j, UNIT * j + len(slots_of(j)))
                dve.reciprocal(rcp[:, :, cols], rsum[:, :, cols]).then_inc(s_rcp, 1)

            def times_lambda(b, j):
                cols = slice(UNIT * j, UNIT * j + len(slots_of(j)))
                wait_count(dve, s_rcp, STEPS, b, j + 1)
                dve.tensor_tensor(rcp[:, 1, cols], rcp[:, 1, cols], nlam[:, cols], ALU.mult).then_inc(s_fac, 1)

            def combine(b, j):
                wait_count(dve, s_fac, STEPS, b, j + 1)
                for s, t in enumerate(slots_of(j)):
                    dve.tensor_scalar(prob[:, j, 1, s, :], prob[:, j, 1, s, :], rcp[:, 1, t:t + 1], None, ALU.mult)\
                        .then_inc(s_sc, 1)
                wait_count(dve, s_t, FLIPS, b - 1, slots_of(j)[-1] // 2 + 1)
                for s, t in enumerate(slots_of(j)):
                    at = ODD * (t % 2)
                    wait_count(dve, s_sc, SLOTS, b, t + 1)
                    ins = dve.scalar_tensor_tensor(out=att[:, t // 2, at:at + NT], in0=prob[:, j, 0, s, :],
                                                   scalar=rcp[:, 0, t:t + 1], in1=prob[:, j, 1, s, :],
                                                   op0=ALU.mult, op1=ALU.add)
                ins.then_inc(s_comb, 1)

            def put(b):
                wait_count(dve, s_pv, PVS, b, PVS)
                dve.tensor_copy(xt[:, ds(b * NT, NT)], bo[:, 0:NT]).then_inc(s_o, 1)

            def step(b, j, n):
                b, j = b + (j + n) // STEPS, (j + n) % STEPS
                return (b, j) if not isinstance(b, int) or b < B else None

            def body(b, i, u):
                for j in range(STEPS):
                    combine(b, j)
                    two, one = step(b, j, 2), step(b, j, 1)
                    if two:
                        reduce(*two, 0)
                    if one:
                        invert(*one)
                    if two:
                        reduce(*two, 1)
                    if one:
                        times_lambda(*one)
                    if j == 1 and not (isinstance(b, int) and b == 0):
                        put(b - 1)

            for j in range(2):
                for a in range(A):
                    reduce(0, j, a)
            invert(0, 0)
            times_lambda(0, 0)
            rounds(dve, B, 2, 2, body)
            put(B - 1)


E = 16
K = 2
F = 256
ROW = D + 1
PT = 128
CAP = TOKENS + PT
MTILES = (K * TOKENS + E * (PT - 1)) // PT
XROWS = E * CAP + PT
NOWHERE = 1 << 20


def routing_phase(nc, gn, group_mean, out_w, out_b, gate_w, iotas, prefix, w12, ident, hid, xt, gates, table,
                  weights, xd):
    ctx = ExitStack()
    with ctx:
        sb, ps, sem = sb_of(nc, ctx, "r"), ps_of(nc, ctx, "r"), sem_of(nc, ctx, "r")
        gnw = sb("gnw", [128, 2])
        gmean = sb("gmean", [128, 128])
        ow = sb("ow", [128, D])
        ob = sb("ob", [TT, D])
        gw = sb("gw", [128, E])
        iota_e = sb("iota_e", [TT, E])
        region = sb("region", [TT, E])
        dest = sb("dest", [TT, TPG, K])
        tile_no = sb("tile_no", [1, MTILES])
        pre = sb("pre", [TT, 2, TT], BF16)
        half = sb("half", [128, TPG])
        pad = sb("pad", [PT, ROW])
        st = sb("st", [128, GB, 6])
        mv = sb("mv", [128, GB, 2])
        mm = sb("mm", [128, GB])
        ms = sb("ms", [128, GB, 2])
        var = sb("var", [128, GB])
        rstd = sb("rstd", [128, GB])
        scale = sb("scale", [128, GB])
        shift = sb("shift", [128, GB])
        xn = [sb(f"xn{u}", [128, GB, NT]) for u in range(2)]
        tst = sb("tst", [TT, TPG, 6])
        tmv = sb("tmv", [TT, TPG, 2])
        tvar = sb("tvar", [TT, TPG])
        trstd = sb("trstd", [TT, TPG])
        rows = [sb(f"rows{u}", [TT, TPG, K, ROW]) for u in range(2)]
        x2t = sb("x2t", [128, TPG, TT])
        logit = sb("logit", [TT, TPG, E])
        top = sb("top", [TT, TPG])
        prob = sb("prob", [TT, TPG, E])
        rsum = sb("rsum", [TT, TPG])
        best = sb("best", [TT, TPG, 8])
        which = sb("which", [TT, TPG, 8], U32)
        whichf = sb("whichf", [TT, TPG, K])
        hot = sb("hot", [TT, TPG, K, E])
        hot16 = sb("hot16", [TT, TPG, E], BF16)
        base = sb("base", [TT, TPG + 1, E])
        pos = sb("pos", [TT, TPG, E])
        picked = sb("picked", [TT, TPG, K, E])
        slotf = sb("slotf", [TT, TPG, K])
        slot = [sb(f"slot{u}", [TT, TPG, K], U32) for u in range(2)]
        cnt = sb("cnt", [1, E], I32)
        ntile = sb("ntile", [1, E])
        cum = [sb(f"cum{i}", [1, E]) for i in range(2)]
        skip = sb("skip", [1, E])
        past = sb("past", [1, MTILES, E])
        tab = sb("tab", [1, MTILES])
        padrow = sb("padrow", [1, E], I32)
        gp = ps("gp", [128, 512])
        cy = [ps(f"cy{i}", [128, 512]) for i in range(2)]
        xp = [ps(f"xp{i}", [128, 4, TT]) for i in range(2)]
        lg = ps("lg", [128, TPG, E])
        pf = ps("pf", [128, 2, TPG * E])

        s_const = sem("const")
        s_init = sem("init")
        s_stat = sem("stat")
        s_statp = sem("statp")
        s_var = sem("var")
        s_rstd = sem("rstd")
        s_shift = sem("shift")
        s_xn = sem("xn")
        s_hb = sem("hb")
        s_cy = sem("cy")
        s_h = sem("h")
        s_ts = sem("ts")
        s_tvar = sem("tvar")
        s_trstd = sem("trstd")
        s_x2 = sem("x2")
        s_x2b = sem("x2b")
        s_xp = sem("xp")
        s_xpe = sem("xpe")
        s_lg = sem("lg")
        s_sub = sem("sub")
        s_exp = sem("exp")
        s_hot = sem("hot")
        s_pf = sem("pf")
        s_slot = sem("slot")
        s_sc = [sem("sc0"), sem("sc1")]
        s_pad = sem("pad")
        s_padw = sem("padw")
        s_proj = sem("proj")
        s_gate = sem("gate")
        s_end = sem("end")
        s_w = sem("w")
        PROJ_LINKS, GATE_LINKS = 11, 13 + TPG
        XF = 4
        block = ctx.enter_context(nc.Block())

        @block.sync
        def _(sp):
            for dst, src in ((gnw[:, :], gn), (gmean[:, :], group_mean), (ow[:, :], out_w), (ob[:, :], out_b),
                             (gw[:, :], gate_w), (iota_e[:, :], iotas[0]), (region[:, :], iotas[1]),
                             (dest[:, :, :], iotas[2]), (tile_no[:, :], iotas[3]), (pre[:, :, :], prefix)):
                sp.dma_start(dst, src).then_inc(s_const, 16)
            sp.dma_start(weights[:, :, :], w12).then_inc(s_w, 16)
            sp.wait_ge(s_pad, 1)
            for e in range(E):
                row = sp.value_load(padrow[0:1, e:e + 1], min_val=e * CAP, max_val=e * CAP + TOKENS)
                sp.dma_start(xd[ds(row, PT), :], pad[:, :]).then_inc(s_padw, 16)
            sp.dma_start(xd[E * CAP:E * CAP + PT, :], pad[:, :]).then_inc(s_padw, 16)
            sp.wait_ge(s_padw, 16 * (E + 1))
            sp.wait_ge(s_w, 16)
        CONST = 160

        @block.gpsimd
        def _(pool):
            pool.memset(half[:, :], -0.5)
            pool.memset(pad[:, 0:D], 0.0)
            pool.memset(pad[:, D:ROW].bitcast(U32), NOWHERE)
            pool.memset(base[:, :, :], 0.0).then_inc(s_init, 1)
            pool.wait_ge(s_init, 1)
            pool.wait_ge(s_const, CONST)

            def image_power(g):
                wait_count(pool, s_var, 1, g, 1)
                pool.tensor_tensor(rstd[:, :], var[:, :], half[:, 0:GB], ALU.pow).then_inc(s_rstd, 1)

            def token_power(g):
                wait_count(pool, s_tvar, 1, g, 1)
                pool.tensor_tensor(trstd[:, :], tvar[:, :], half[0:TT, :], ALU.pow).then_inc(s_trstd, 1)

            def send(g, u, tiles):
                wait_count(pool, s_slot, 1, g, 1, met=s_const)
                wait_count(pool, s_x2b, XF, g, XF, met=s_const)
                for t in tiles:
                    for k in range(K):
                        pool.indirect_dma_start(xd[:, :], bass.IndirectOffsetOnAxis(ap=slot[u][:, t, k:k + 1], axis=0),
                                                rows[u][:, t, k, :], None).then_inc(s_sc[u], 16)

            def body(g, i, u):
                more = not (isinstance(g, int) and g + 1 >= NG)
                past = not (isinstance(g, int) and g == 0)
                if past:
                    send(g - 1, 1 - u, range(0, 3))
                token_power(g)
                if past:
                    send(g - 1, 1 - u, range(3, 8))
                if more:
                    image_power(g + 1)
                if past:
                    send(g - 1, 1 - u, range(8, TPG))

            image_power(0)
            rounds(pool, NG, 2, 2, body)
            send(NG - 1, 1, range(TPG))
            for u in range(2):
                pool.wait_ge(s_sc[u], 16 * K * TPG * NG // 2)

        @block.tensor
        def _(pe):
            pe.wait_ge(s_const, CONST)

            def stats(g):
                wait_count(pe, s_stat, 1, g, 1)
                pe.matmul(gp[:, 0:2 * GB], gmean[:, :], mv[:, :, :].rearrange("p b k -> p (b k)"),
                          start=True, stop=True).then_inc(s_statp, 1)

            def project(g, u, ks):
                for k in ks:
                    wait_count(pe, s_h, XF, g, k - 1)
                    for t in range(4 * k, min(4 * k + 4, TPG)):
                        wait_count(pe, s_xn, GB, g, -(-TT * (t + 1) // NT))
                        ins = pe.matmul(cy[k % 2][0:TT, (t - 4 * k) * D:(t - 4 * k + 1) * D],
                                        xn[u][:, :, :].rearrange("p b n -> p (b n)")[:, t * TT:(t + 1) * TT],
                                        ow[:, :], start=True, stop=True)
                    ins.then_inc(s_cy, 1)

            def turn(g, u):
                for k in range(XF):
                    wait_count(pe, s_x2, XF, g, k + 1)
                    wait_count(pe, s_xpe, XF, g, k - 1)
                    for t in range(4 * k, min(4 * k + 4, TPG)):
                        ins = pe.transpose(xp[k % 2][:, t - 4 * k, :], rows[u][:, t, 0, 0:D], ident[0][0:TT, 0:TT])
                    ins.then_inc(s_xp, 1)

            def logits(g):
                wait_count(pe, s_sub, 1, g - 1, 1)
                for t in range(TPG):
                    wait_count(pe, s_xpe, XF, g, t // 4 + 1)
                    ins = pe.matmul(lg[0:TT, t, :], x2t[:, t, :], gw[:, :], start=True, stop=True)
                ins.then_inc(s_lg, 1)

            def count(g):
                wait_count(pe, s_hot, 1, g, 1)
                wait_count(pe, s_slot, 1, g - 1, 1)
                for m in range(2):
                    ins = pe.matmul(pf[0:TT, m, :], pre[:, m, :], hot16[:, :, :].rearrange("p t e -> p (t e)"),
                                    start=True, stop=True)
                ins.then_inc(s_pf, 1)

            def body(g, i, u):
                more = not (isinstance(g, int) and g + 1 >= NG)
                turn(g, u)
                logits(g)
                if more:
                    stats(g + 1)
                count(g)
                if more:
                    project(g + 1, 1 - u, range(XF))

            stats(0)
            project(0, 0, range(XF))
            rounds(pe, NG, 2, 2, body)

        @block.scalar
        def _(act):
            act.wait_ge(s_const, CONST)

            def normalise(g, u):
                wait_count(act, s_shift, 1, g, 1)
                wait_count(act, s_cy, XF, g - 2, XF)
                for b in range(GB):
                    act.activation(xn[u][:, b, :], xt[:, ds((g * GB + b) * NT, NT)], ACT.Identity,
                                   bias=shift[:, b:b + 1], scale=scale[:, b:b + 1]).then_inc(s_xn, 1)

            def body(g, i, u):
                wait_count(act, s_lg, 1, g - 1, 1)
                for k in range(XF):
                    n = min(4, TPG - 4 * k)
                    wait_count(act, s_xp, XF, g, k + 1)
                    act.activation(x2t[:, 4 * k:4 * k + n, :], xp[k % 2][:, 0:n, :], ACT.Copy).then_inc(s_xpe, 1)
                wait_count(act, s_sub, 1, g, 1)
                act.activation(prob[:, :, :], logit[:, :, :], ACT.Exp).then_inc(s_exp, 1)
                if not (isinstance(g, int) and g + 1 >= NG):
                    normalise(g + 1, 1 - u)
                for k in range(XF):
                    n = min(4, TPG - 4 * k)
                    act.activation(rows[u][:, 4 * k:4 * k + n, 1, 0:D], rows[u][:, 4 * k:4 * k + n, 0, 0:D], ACT.Copy)\
                        .then_inc(s_x2b, 1)

            normalise(0, 0)
            rounds(act, NG, 2, 2, body)

        @block.vector
        def _(dve):
            dve.wait_ge(s_const, CONST)
            dve.wait_ge(s_init, 1)

            def image_stats(g, link):
                wait_count(dve, s_statp, 1, g - 1, 1, met=s_const)
                for b in range(GB):
                    ins = dve.bn_stats(st[:, b, :], xt[:, ds((g * GB + b) * NT, NT)])
                link(ins, met=s_const)
                for b in range(GB):
                    ins = dve.bn_aggr(mv[:, b, :], st[:, b, :])
                link(ins)
                link(dve.tensor_tensor(mm[:, :], mv[:, :, 0], mv[:, :, 0], ALU.mult))
                dve.tensor_tensor(mv[:, :, 1], mv[:, :, 1], mm[:, :], ALU.add).then_inc(s_stat, 1)

            def image_var(g, link):
                wait_count(dve, s_statp, 1, g, 1)
                link(dve.tensor_copy(ms[:, :, :].rearrange("p b k -> p (b k)"), gp[:, 0:2 * GB]))
                link(dve.tensor_tensor(mm[:, :], ms[:, :, 0], ms[:, :, 0], ALU.mult))
                link(dve.tensor_tensor(mm[:, :], ms[:, :, 1], mm[:, :], ALU.subtract))
                dve.tensor_scalar(var[:, :], mm[:, :], 0.0, 1e-5, ALU.max, ALU.add).then_inc(s_var, 1)

            def image_affine(g, link):
                wait_count(dve, s_rstd, 1, g, 1)
                wait_count(dve, s_xn, GB, g - 1, GB)
                link(dve.tensor_scalar(scale[:, :], rstd[:, :], gnw[:, 0:1], None, ALU.mult))
                link(dve.tensor_tensor(mm[:, :], ms[:, :, 0], scale[:, :], ALU.mult))
                dve.tensor_scalar(shift[:, :], mm[:, :], -1.0, gnw[:, 1:2], ALU.mult, ALU.add).then_inc(s_shift, 1)

            def residual(g, link):
                tiles = hid[:, ds(g * TPG, TPG), :]
                dve.tensor_tensor(tiles, tiles, ob[:, :].unsqueeze(1).broadcast_to([TT, TPG, D]), ALU.add)\
                    .then_inc(s_hb, 1)
                wait_count(dve, s_hb, 1, g, 1)
                for k in range(XF + 2):
                    if k < XF:
                        n = min(4, TPG - 4 * k)
                        wait_count(dve, s_cy, XF, g, k + 1)
                        tiles = hid[:, ds(g * TPG + 4 * k, n), :]
                        dve.tensor_tensor(tiles, cy[k % 2][0:TT, 0:n * D].rearrange("p (t d) -> p t d", d=D), tiles,
                                          ALU.add).then_inc(s_h, 1)
                    if 0 < k <= XF:
                        wait_count(dve, s_h, XF, g, k, met=s_const)
                        for t in range(4 * (k - 1), min(4 * k, TPG)):
                            row = hid[:, ds(g * TPG + t, 1), :].rearrange("p o d -> p (o d)")
                            ins = dve.bn_stats(tst[:, t, :], row)
                        ins.then_inc(s_ts, 1)
                    if 1 < k:
                        wait_count(dve, s_ts, XF, g, k - 1, met=s_const)
                        for t in range(4 * (k - 2), min(4 * (k - 1), TPG)):
                            ins = dve.bn_aggr(tmv[:, t, :], tst[:, t, :])
                link(ins)
                dve.tensor_scalar(tvar[:, :], tmv[:, :, 1], 1e-5, None, ALU.add).then_inc(s_tvar, 1)

            def normalise(g, i, u, link):
                wait_count(dve, s_trstd, 1, g, 1)
                if isinstance(g, int):
                    if g >= 2:
                        dve.wait_ge(s_sc[u], 16 * K * TPG * (g // 2))
                else:
                    dve.wait_ge(s_sc[u], i * (16 * K * TPG))
                for t in range(TPG):
                    row = hid[:, ds(g * TPG + t, 1), :].rearrange("p o d -> p (o d)")
                    ins = dve.tensor_scalar(rows[u][:, t, 0, 0:D], row, tmv[:, t, 0:1], trstd[:, t:t + 1],
                                            ALU.subtract, ALU.mult)
                    if t % 4 == 3 or t == TPG - 1:
                        ins.then_inc(s_x2, 1)
                link(dve.tensor_copy(rows[u][:, :, :, D].bitcast(U32), dest[:, :, :]))
                link(dve.tensor_scalar(dest[:, :, :], dest[:, :, :], float(K * GT), None, ALU.add), met=s_const)

            def less_top(g, link):
                wait_count(dve, s_lg, 1, g, 1)
                wait_count(dve, s_exp, 1, g - 1, 1)
                link(dve.tensor_reduce(top[:, :], lg[0:TT, :, :], AX.X, ALU.max))
                dve.tensor_tensor(logit[:, :, :], lg[0:TT, :, :], top[:, :].unsqueeze(2).broadcast_to([TT, TPG, E]),
                                  ALU.subtract).then_inc(s_sub, 1)

            def best_two(g, link):
                wait_count(dve, s_exp, 1, g, 1)
                link(dve.tensor_reduce(rsum[:, :], prob[:, :, :], AX.X, ALU.add))
                link(dve.reciprocal(rsum[:, :], rsum[:, :]))
                link(dve.tensor_tensor(prob[:, :, :], prob[:, :, :], rsum[:, :].unsqueeze(2).broadcast_to([TT, TPG, E]),
                                       ALU.mult), met=s_const)
                for t in range(TPG):
                    ins = dve.max(best[:, t, :], prob[:, t, :])
                link(ins, met=s_const)
                for t in range(TPG):
                    ins = dve.max_index(which[:, t, :], best[:, t, :], prob[:, t, :])
                link(ins)
                dve.tensor_copy(gates[:, ds(g * TPG, TPG), :], best[:, :, 0:K])
                link(dve.tensor_copy(whichf[:, :, :], which[:, :, 0:K]))
                link(dve.tensor_tensor(hot[:, :, :, :],
                                       iota_e[:, :].unsqueeze(1).unsqueeze(1).broadcast_to([TT, TPG, K, E]),
                                       whichf[:, :, :].unsqueeze(3).broadcast_to([TT, TPG, K, E]), ALU.is_equal))
                dve.tensor_tensor(hot16[:, :, :], hot[:, :, 0, :], hot[:, :, 1, :], ALU.add).then_inc(s_hot, 1)

            def places(g, u, link):
                link(dve.tensor_copy(base[:, 0, :], base[:, TPG, :]))
                wait_count(dve, s_pf, 1, g, 1)
                tot = pf[0:TT, 1, :].rearrange("p (t e) -> p t e", e=E)
                for t in range(TPG):
                    link(dve.tensor_tensor(base[:, t + 1, :], tot[:, t, :], base[:, t, :], ALU.add))
                link(dve.tensor_tensor(pos[:, :, :], pf[0:TT, 0, :].rearrange("p (t e) -> p t e", e=E),
                                       base[:, 0:TPG, :], ALU.add))
                link(dve.tensor_tensor(pos[:, :, :], pos[:, :, :], region[:, :].unsqueeze(1).broadcast_to([TT, TPG, E]),
                                       ALU.add))
                link(dve.tensor_tensor(picked[:, :, :, :], hot[:, :, :, :],
                                       pos[:, :, :].unsqueeze(2).broadcast_to([TT, TPG, K, E]), ALU.mult))
                link(dve.tensor_reduce(slotf[:, :, :], picked[:, :, :, :], AX.X, ALU.add))
                dve.tensor_copy(slot[u][:, :, :], slotf[:, :, :]).then_inc(s_slot, 1)

            def body(g, i, u):
                more = not (isinstance(g, int) and g + 1 >= NG)
                proj, gate = Chain(dve, s_proj, PROJ_LINKS, g + 1), Chain(dve, s_gate, GATE_LINKS, g)
                if more:
                    image_stats(g + 1, proj.link)
                less_top(g, gate.link)
                if more:
                    image_var(g + 1, proj.link)
                best_two(g, gate.link)
                if more:
                    image_affine(g + 1, proj.link)
                places(g, u, gate.link)
                gate.end()
                if more:
                    residual(g + 1, proj.link)
                    normalise(g + 1, i + u, 1 - u, proj.link)
                    proj.end()

            proj = Chain(dve, s_proj, PROJ_LINKS, 0)
            image_stats(0, proj.link)
            image_var(0, proj.link)
            image_affine(0, proj.link)
            residual(0, proj.link)
            normalise(0, 0, 0, proj.link)
            proj.end()
            rounds(dve, NG, 2, 2, body)

            n = [0]

            def link(ins):
                n[0] += 1
                ins.then_inc(s_end, 1)
                dve.wait_ge(s_end, n[0])

            count = base[0:1, TPG, :]
            link(dve.tensor_copy(cnt[:, :], count))
            dve.tensor_tensor(padrow[:, :], count, region[0:1, :], ALU.add).then_inc(s_pad, 1)
            link(dve.tensor_scalar(skip[:, :], count, float(PT - 1), None, ALU.add))
            link(dve.tensor_copy(cnt[:, :], skip[:, :]))
            link(dve.tensor_single_scalar(cnt[:, :], cnt[:, :], PT.bit_length() - 1, ALU.logical_shift_right))
            link(dve.tensor_copy(ntile[:, :], cnt[:, :]))
            link(dve.tensor_copy(cum[0][:, :], ntile[:, :]))
            for k, s in enumerate((1, 2, 4, 8)):
                a, b = cum[k % 2], cum[1 - k % 2]
                link(dve.tensor_copy(b[:, :], a[:, :]))
                link(dve.tensor_tensor(b[:, s:], a[:, s:], a[:, :E - s], ALU.add))
            link(dve.tensor_scalar(skip[:, :], ntile[:, :], -float(PT), float(CAP), ALU.mult, ALU.add))
            link(dve.tensor_tensor(past[:, :, :], tile_no[:, :].unsqueeze(2).broadcast_to([1, MTILES, E]),
                                   cum[0][:, :].unsqueeze(1).broadcast_to([1, MTILES, E]), ALU.is_ge))
            link(dve.tensor_reduce(tab[:, :], past[:, :, :], AX.X, ALU.add))
            link(dve.tensor_scalar(table[0:1, 1, :], tab[:, :], float(E - 1), None, ALU.min))
            link(dve.tensor_tensor(past[:, :, :], past[:, :, :], skip[:, :].unsqueeze(1).broadcast_to([1, MTILES, E]),
                                   ALU.mult))
            link(dve.tensor_reduce(tab[:, :], past[:, :, :], AX.X, ALU.add))
            link(dve.scalar_tensor_tensor(out=tab[:, :], in0=tile_no[:, :], scalar=float(PT), in1=tab[:, :],
                                          op0=ALU.mult, op1=ALU.add))
            link(dve.tensor_scalar(table[0:1, 0, :], tab[:, :], float(E * CAP), None, ALU.min))


def expert_phase(nc, weights, ident, table, xd, yd):
    ctx = ExitStack()
    with ctx:
        sb, ps, sem = sb_of(nc, ctx, "e"), ps_of(nc, ctx, "e"), sem_of(nc, ctx, "e")
        R = 8
        YR = 4
        HR = 4
        wc = [sb(f"wc{u}", [128, 2 * F]) for u in range(HR)]
        xin = [sb(f"xin{u}", [PT, ROW]) for u in range(R)]
        xts = [sb(f"xts{u}", [128, PT]) for u in range(2)]
        act1 = [sb(f"act{u}", [128, 2, PT]) for u in range(HR)]
        ys = [sb(f"ys{u}", [PT, D]) for u in range(YR)]
        tp = [ps(f"tp{u}", [128, 512]) for u in range(2)]
        hp = [ps(f"hp{u}", [128, 512]) for u in range(HR)]
        yp = [ps(f"yp{u}", [128, 512]) for u in range(2)]
        s_go = sem("go")
        go = sb("go", [128, 1])
        s_in = [sem(f"in{u}") for u in range(R)]
        s_wc = sem("wc")
        s_tp = sem("tp")
        s_xt = sem("xt")
        s_hp = sem("hp")
        s_act = sem("act")
        s_yp = sem("yp")
        s_ys = sem("ys")
        s_out = [sem(f"out{u}") for u in range(R)]
        block = ctx.enter_context(nc.Block())

        def tiles(eng, body):
            for t in range(R):
                body(t, 0, t)
            with eng.Fori(1, MTILES // R - 1) as i:
                for u in range(R):
                    body(i * R + u, i, u)
            for t in range(MTILES - R, MTILES):
                body(t, t // R, t % R)

        def ahead(t, i, u, n):
            if isinstance(t, int) and t + n >= MTILES:
                return None
            return t + n, i + (u + n) // R, (u + n) % R

        @block.sync
        def _(sp):
            def load(t, i, u):
                row = sp.value_load(table[0:1, 0, ds(t, 1)], min_val=0, max_val=E * CAP)
                if not (isinstance(t, int) and t < R):
                    sp.wait_ge(s_out[u], i * 16)
                sp.dma_start(xin[u][:, :], xd[ds(row, PT), :]).then_inc(s_in[u], 16)

            tiles(sp, load)

        @block.tensor
        def _(pe):
            def flip(t, i, u):
                pe.wait_ge(s_in[u], i * 16 + 16)
                pe.transpose(tp[u % 2][:, 0:PT], xin[u][:, 0:D], ident[0][:, :]).then_inc(s_tp, 1)

            def up(t, i, u):
                v = u % 2
                wait_count(pe, s_wc, 1, t, 1)
                wait_count(pe, s_xt, 1, t, 1)
                for f in range(2):
                    ins = pe.matmul(hp[u % HR][:, f * PT:(f + 1) * PT], wc[u % HR][:, f * 128:(f + 1) * 128],
                                    xts[v][:, :], start=True, stop=True)
                ins.then_inc(s_hp, 1)

            def down(t, i, u):
                v = u % 2
                wait_count(pe, s_act, 1, t, 1)
                wait_count(pe, s_ys, 1, t, -1)
                for f in range(2):
                    ins = pe.matmul(yp[v][:, 0:D], act1[u % HR][:, f, :],
                                    wc[u % HR][:, F + f * D:F + (f + 1) * D], start=f == 0, stop=f == 1)
                ins.then_inc(s_yp, 1)

            def body(t, i, u):
                if nxt := ahead(t, i, u, 2):
                    flip(*nxt)
                if nxt := ahead(t, i, u, 1):
                    up(*nxt)
                down(t, i, u)

            flip(0, 0, 0)
            flip(1, 0, 1)
            up(0, 0, 0)
            tiles(pe, body)

        @block.scalar
        def _(act):
            def evict(t, i, u):
                wait_count(act, s_tp, 1, t, 1)
                wait_count(act, s_hp, 1, t, -1)
                act.activation(xts[u % 2][:, :], tp[u % 2][:, 0:PT], ACT.Copy).then_inc(s_xt, 1)

            def gelu(t, i, u):
                wait_count(act, s_hp, 1, t, 1)
                wait_count(act, s_yp, 1, t, 1 - HR)
                act.activation(act1[u % HR][:, :, :].rearrange("p f n -> p (f n)"), hp[u % HR][:, 0:2 * PT], ACT.Gelu)\
                    .then_inc(s_act, 1)

            def body(t, i, u):
                if nxt := ahead(t, i, u, 2):
                    evict(*nxt)
                if nxt := ahead(t, i, u, 1):
                    gelu(*nxt)
                wait_count(act, s_yp, 1, t, 1)
                if not (isinstance(t, int) and t < YR):
                    act.wait_ge(s_out[(u + YR) % R], (i + (u >= YR)) * 16)
                act.activation(ys[u % YR][:, :], yp[u % 2][:, 0:D], ACT.Copy).then_inc(s_ys, 1)

            evict(0, 0, 0)
            evict(1, 0, 1)
            gelu(0, 0, 0)
            tiles(act, body)

        @block.vector
        def _(dve):
            def stage(t, i, u):
                wait_count(dve, s_yp, 1, t, 1 - HR)
                e = dve.value_load(table[0:1, 1, ds(t, 1)], min_val=0, max_val=E - 1)
                dve.tensor_copy(wc[u % HR][:, :], weights[:, ds(e, 1), :].rearrange("p o f -> p (o f)")).then_inc(s_wc, 1)

            def body(t, i, u):
                if nxt := ahead(t, i, u, 2):
                    stage(*nxt)

            stage(0, 0, 0)
            stage(1, 0, 1)
            tiles(dve, body)

        @block.gpsimd
        def _(pool):
            pool.memset(go[:, :], 0.0).then_inc(s_go, 1)

            def send(t, i, u):
                pool.wait_ge(s_in[u], i * 16 + 16)
                wait_count(pool, s_ys, 1, t, 1, met=s_go)
                pool.indirect_dma_start(yd[:, :], bass.IndirectOffsetOnAxis(ap=xin[u][:, D:ROW].bitcast(U32), axis=0),
                                        ys[u % YR][:, :], None, bounds_check=K * TOKENS - 1, oob_is_err=False)\
                    .then_inc(s_out[u], 16)

            tiles(pool, send)
            for u in range(R):
                pool.wait_ge(s_out[u], 16 * MTILES // R)


def combine_phase(nc, hid, gates, yd, out):
    ctx = ExitStack()
    with ctx:
        sb, sem = sb_of(nc, ctx, "c"), sem_of(nc, ctx, "c")
        N = TPG
        yin = [sb(f"yin{u}", [TT, N, K * D]) for u in range(2)]
        res = [sb(f"res{u}", [TT, N, D]) for u in range(2)]
        s_in = [sem("in0"), sem("in1")]
        s_one = sem("one")
        s_two = sem("two")
        s_pool = sem("pool")
        POOLED = 4
        NV = N - POOLED
        POOL_STEPS = 4
        s_out = [sem("out0"), sem("out1")]
        yv = yd.rearrange("(t p k) d -> p t (k d)", p=TT, k=K)
        ov = out.rearrange("b n d -> (b n) d").rearrange("(t p) d -> p t d", p=TT)
        block = ctx.enter_context(nc.Block())
        ROUNDS = NTILES // N

        @block.sync
        def _(sp):
            def load(r, i, u):
                wait_count(sp, s_two, NV, r - 2, NV)
                wait_count(sp, s_pool, POOL_STEPS, r - 2, POOL_STEPS)
                sp.dma_start(yin[u][:, :, :], yv[:, ds(r * N, N), :]).then_inc(s_in[u], 16)

            rounds(sp, ROUNDS, 2, 0, load)

        @block.vector
        def _(dve):
            def body(r, i, u):
                dve.wait_ge(s_in[u], i * 16 + 16)
                if isinstance(r, int):
                    if i > 0:
                        dve.wait_ge(s_out[u], 16 * i)
                else:
                    dve.wait_ge(s_out[u], i * 16)
                for k, s in ((0, s_one), (1, s_two)):
                    for t in range(NV):
                        row = hid[:, ds(r * N + t, 1), :] if k == 0 else res[u][:, t:t + 1, :]
                        if k:
                            wait_count(dve, s_one, NV, r, t + 1)
                        dve.scalar_tensor_tensor(
                            out=res[u][:, t, :], in0=yin[u][:, t, k * D:(k + 1) * D],
                            scalar=gates[:, ds(r * N + t, 1), k], in1=row.rearrange("p o d -> p (o d)"),
                            op0=ALU.mult, op1=ALU.add).then_inc(s, 1)

            rounds(dve, ROUNDS, 2, 0, body)

        @block.gpsimd
        def _(pool):
            def body(r, i, u):
                pool.wait_ge(s_in[u], i * 16 + 16)
                if isinstance(r, int):
                    if i > 0:
                        pool.wait_ge(s_out[u], 16 * i)
                else:
                    pool.wait_ge(s_out[u], i * 16)
                for k in range(K):
                    part = yin[u][:, NV:, k * D:(k + 1) * D]
                    factor = gates[:, ds(r * N + NV, POOLED), k:k + 1].broadcast_to([TT, POOLED, D])
                    pool.tensor_tensor(part, part, factor, ALU.mult).then_inc(s_pool, 1)
                wait_count(pool, s_pool, POOL_STEPS, r, 2)
                pool.tensor_tensor(res[u][:, NV:, :], yin[u][:, NV:, 0:D], yin[u][:, NV:, D:], ALU.add)\
                    .then_inc(s_pool, 1)
                wait_count(pool, s_pool, POOL_STEPS, r, 3)
                pool.tensor_tensor(res[u][:, NV:, :], res[u][:, NV:, :], hid[:, ds(r * N + NV, POOLED), :], ALU.add)\
                    .then_inc(s_pool, 1)

            rounds(pool, ROUNDS, 2, 0, body)

        @block.scalar
        def _(act):
            def store(r, i, u):
                wait_count(act, s_two, NV, r, NV)
                wait_count(act, s_pool, POOL_STEPS, r, POOL_STEPS)
                act.dma_start(ov[:, ds(r * N, N), :], res[u][:, :, :]).then_inc(s_out[u], 16)

            rounds(act, ROUNDS, 2, 0, store)
            for u in range(2):
                act.wait_ge(s_out[u], 16 * ROUNDS // 2)


def vit_tower_kernel(nc, x, gamma, beta, tok_w, tok_b, edge_masks, ident_in, proj_w, k_bias, head_mask, lam, gn,
                     group_mean, out_w, out_b, gate_w, iota_e, region, dest, tile_no, prefix, w12, out):
    xd = nc.dram_tensor("routed_rows", [XROWS, ROW], F32, kind="Internal").ap()
    yd = nc.dram_tensor("expert_rows", [K * TOKENS, D], F32, kind="Internal").ap()
    ctx = ExitStack()
    with ctx:
        sb = sb_of(nc, ctx, "k")
        hid = sb("hid", [TT, NTILES, D])
        ident = (sb("ident", [128, 128]), ident_in)
        gates = sb("gates", [TT, NTILES, K])
        table = sb("table", [1, 2, MTILES], I32)
        xt = sb("xt", [128, TOKENS])
        token_phase(nc, x, gamma, beta, tok_w, tok_b, edge_masks, ident, hid, xt)
        attention_phase(nc, proj_w, k_bias, head_mask, lam, ident, xt)
        weights = sb("weights", [128, E, 2 * F])
        routing_phase(nc, gn, group_mean, out_w, out_b, gate_w, (iota_e, region, dest, tile_no), prefix,
                      w12, ident, hid, xt, gates, table, weights, xd)
        expert_phase(nc, weights, ident, table, xd, yd)
        combine_phase(nc, hid, gates, yd, out)


def kernel(**inputs):
    import ml_dtypes as _ml
    import numpy as _np
    import concourse.bacc as _bacc
    from concourse import mybir as _mybir
    from concourse.bass_utils import run_bass_kernel_spmd as _run

    a = {n: _np.asarray(v) for n, v in inputs.items()}

    def pixels(m):
        return m.reshape(V, C, NP, PATCH, NP, PATCH).transpose(1, 3, 5, 0, 2, 4).reshape(128, V, NT)

    part = _np.arange(128)
    heads = (part[:, None] // HD == _np.arange(H)[None]).astype(_np.float32)
    head = _np.zeros((128, SLOTS), int)
    head[:, :H] = _np.arange(H)
    for i, hs in enumerate(TAILS):
        for j, h in enumerate(hs):
            head[KB * j:KB * (j + 1), H + i] = h
    tok = _np.arange(TT)
    laid = {
        "x": a["x"],
        "gamma": pixels(a["L0_tok_gamma"]),
        "beta": pixels(a["L0_tok_beta"]),
        "tok_w": a["L0_tok_W"].reshape(D, V, 128).transpose(2, 1, 0),
        "tok_b": _np.broadcast_to(a["L0_tok_b"], (TT, D)),
        "edge_masks": _np.stack([part % PATCH >= HALF, part % PATCH < HALF], 1).astype(_np.float32),
        "ident_in": _np.eye(128, dtype=_np.float32),
        "proj_w": _np.stack([a[f"L0_attn_{n}_w"].T for n in ("Q1", "Q2", "K1", "K2", "V")], 1),
        "k_bias": _np.stack([a["L0_attn_K1_b"], a["L0_attn_K2_b"]], 1),
        "head_mask": heads,
        "lam": _np.stack([a[f"L0_attn_lambda_{n}"][:, 0][head] for n in ("q1", "q2", "k1", "k2")], 1),
        "gn": _np.stack([a["L0_attn_gn_w"], a["L0_attn_gn_b"]], 1),
        "group_mean": ((part[:, None] // 32 == part[None] // 32) / 32).astype(_np.float32),
        "out_w": a["L0_attn_out_w"].T,
        "out_b": _np.broadcast_to(a["L0_attn_out_b"], (TT, D)),
        "gate_w": a["L0_ffn_W_gate"],
        "iota_e": _np.broadcast_to(_np.arange(E, dtype=_np.float32), (TT, E)),
        "region": _np.broadcast_to(_np.arange(E, dtype=_np.float32) * CAP, (TT, E)),
        "dest": (K * (_np.arange(TPG)[None, :, None] * TT + tok[:, None, None]) + _np.arange(K)).astype(_np.float32),
        "tile_no": _np.arange(MTILES, dtype=_np.float32)[None],
        "prefix": _np.stack([tok[:, None] < tok[None], _np.ones((TT, TT), bool)], 1).astype(_ml.bfloat16),
        "w12": _np.concatenate([a["L0_ffn_W1"].transpose(1, 0, 2),
                                a["L0_ffn_W2"].reshape(E, 2, 128, D).transpose(2, 0, 1, 3).reshape(128, E, 2 * D)], 2),
    }
    nc = _bacc.Bacc("TRN2", target_bir_lowering=False, num_devices=1)
    arrays, args = {}, {}
    for name, v in laid.items():
        v = _np.ascontiguousarray(v)
        arrays[f"in_{name}_dram"] = v
        args[name] = nc.dram_tensor(f"in_{name}_dram", v.shape, _mybir.dt.from_np(v.dtype), kind="ExternalInput").ap()
    args["out"] = nc.dram_tensor("out_0_dram", (B, NT, D), _mybir.dt.float32, kind="ExternalOutput").ap()
    vit_tower_kernel(nc, **args)
    r = _run(nc, [arrays], core_ids=[0])
    return r.results[0]["out_0_dram"]
```
